# Optimizing a Trainium2 kernel written in Bass

```python
import numpy as np
import jax
import jax.numpy as jnp

def _softmax(x, axis=-1):
    return jax.nn.softmax(x, axis=axis)

def _gelu(x):
    return jax.nn.gelu(x, approximate=True)

def _silu(x):
    return jax.nn.silu(x)

def _sigmoid(x):
    return jax.nn.sigmoid(x)

def _layernorm(x, axis=-1, eps=1e-05):
    m = jnp.mean(x, axis=axis, keepdims=True)
    v = jnp.var(x, axis=axis, keepdims=True)
    return (x - m) / jnp.sqrt(v + eps)

def _scatter_add(tgt, idx, src, axis=0):
    return tgt.at[idx].add(src)

def _segment_sum(src, seg, n):
    return jax.ops.segment_sum(src, seg, n)
kernel_name = 'mk_gnn_preln_d4_gnn_r8_7b6047'

def setup_inputs(seed: int=0):
    np.random.seed(seed)
    _w = jnp.asarray

    def _rec_inputs():
        import jax
        import jax.numpy as jnp
        _gk = jax.random.key(seed)
        x = -0.000202 + 1 * jax.random.normal(jax.random.fold_in(_gk, 1), (6250, 128), jnp.float32)
        src = jax.random.randint(jax.random.fold_in(_gk, 2), (200000,), 0, 6250, jnp.int32)
        dst = jnp.minimum((6250 * jax.random.uniform(jax.random.fold_in(_gk, 3), (200000,)) ** 2.0).astype(jnp.int32), 49999)
        _o = jnp.argsort(dst, stable=True)
        src = src[_o]
        dst = dst[_o]
        edge_attr_20 = jax.random.uniform(jax.random.fold_in(_gk, 12), (200000, 20), jnp.float32, 0.0, 1)
        edge_type_64 = jax.random.randint(jax.random.fold_in(_gk, 14), (200000,), 0, 64, jnp.int32)
        edge_weight1 = jax.random.uniform(jax.random.fold_in(_gk, 15), (200000, 1), jnp.float32, 0.0, 1)
        return (x, src, dst, edge_attr_20, edge_type_64, edge_weight1)
    x, src, dst, edge_attr_20, edge_type_64, edge_weight1 = _rec_inputs()

    def _L0_gnn_setup():
        import jax, jax.numpy as jnp
        import numpy as np
        N_NODES = 6250
        N_EDGES = 75000
        D_IN = 128
        D_OUT = 128
        EPS = 0.0
        key = jax.random.key(seed)
        kx, ke, k1, k2, k3, k4 = jax.random.split(key, 6)
        x = jax.random.normal(kx, (N_NODES, D_IN), dtype=jnp.float32)
        edge_index = jax.random.randint(ke, (2, N_EDGES), 0, N_NODES, dtype=jnp.int64)
        s1 = 1.0 / np.sqrt(D_IN)
        s2 = 1.0 / np.sqrt(D_OUT)
        W1 = jax.random.uniform(k1, (D_IN, D_OUT), jnp.float32, -s1, s1)
        b1 = jax.random.uniform(k2, (D_OUT,), jnp.float32, -s1, s1)
        W2 = jax.random.uniform(k3, (D_OUT, D_OUT), jnp.float32, -s2, s2)
        b2 = jax.random.uniform(k4, (D_OUT,), jnp.float32, -s2, s2)
        return {'x': x, 'edge_index': edge_index, 'W1': W1, 'b1': b1, 'W2': W2, 'b2': b2}
    _L0_gnn_all = _L0_gnn_setup()
    _L0_gnn_in = {k: v for k, v in _L0_gnn_all.items() if k in ('W1', 'b1', 'W2', 'b2')}
    del _L0_gnn_all

    def _L1_gnn_setup():
        import jax, jax.numpy as jnp
        import numpy as np
        N_ATOMS = 6250
        N_PAIRS = 200000
        F = 128
        NF = 128
        RBF = 20
        LOG2 = float(np.log(2.0))

        def shifted_softplus(x):
            return jax.nn.softplus(x) - LOG2
        key = jax.random.key(seed)
        ks = jax.random.split(key, 12)
        inv = lambda n: 1.0 / np.sqrt(n)
        return {'atomic_embedding': jax.random.normal(ks[0], (N_ATOMS, F), jnp.float32), 'pair_indices': jax.random.randint(ks[1], (2, N_PAIRS), 0, N_ATOMS, jnp.int32), 'f_ij': jax.random.uniform(ks[2], (N_PAIRS, RBF), jnp.float32), 'f_ij_cutoff': jax.random.uniform(ks[3], (N_PAIRS, 1), jnp.float32), 'W_in': jax.random.normal(ks[4], (F, NF), jnp.float32) * inv(F), 'W_f1': jax.random.normal(ks[5], (RBF, NF), jnp.float32) * inv(RBF), 'b_f1': jnp.zeros((NF,), jnp.float32), 'W_f2': jax.random.normal(ks[6], (NF, NF), jnp.float32) * inv(NF), 'b_f2': jnp.zeros((NF,), jnp.float32), 'W_o1': jax.random.normal(ks[7], (NF, F), jnp.float32) * inv(NF), 'b_o1': jnp.zeros((F,), jnp.float32), 'W_o2': jax.random.normal(ks[8], (F, F), jnp.float32) * inv(F), 'b_o2': jnp.zeros((F,), jnp.float32)}
    _L1_gnn_all = _L1_gnn_setup()
    _L1_gnn_in = {k: v for k, v in _L1_gnn_all.items() if k in ('W_in', 'W_f1', 'b_f1', 'W_f2', 'b_f2', 'W_o1', 'b_o1', 'W_o2', 'b_o2')}
    del _L1_gnn_all

    def _L2_gnn_setup():
        import jax, jax.numpy as jnp
        import numpy as np
        N_NODES = 6250
        N_EDGES = 80000
        D = 128
        BN_EPS = 1e-05
        NEG_SLOPE = 0.2

        def _gatv2(x, edge_index, edge_attr, Wl, bl, Wr, br, We, att, bias_out):
            src, dst = (edge_index[0], edge_index[1])
            xl = x @ Wl + bl
            xr = x @ Wr + br
            e = edge_attr @ We
            m = xl[src] + xr[dst] + e
            m = jax.nn.leaky_relu(m, NEG_SLOPE)
            logits = m @ att
            n = x.shape[0]
            mx = jax.ops.segment_max(logits, dst, num_segments=n)
            ex = jnp.exp(logits - mx[dst])
            den = jax.ops.segment_sum(ex, dst, num_segments=n)
            alpha = ex / (den[dst] + 1e-16)
            out = jax.ops.segment_sum(xl[src] * alpha[:, None], dst, num_segments=n)
            return out + bias_out
        key = jax.random.key(seed)
        ks = jax.random.split(key, 8)
        s = 1.0 / np.sqrt(D)
        x = jax.random.normal(ks[0], (N_NODES, D), dtype=jnp.float32)
        edge_index = jax.random.randint(ks[1], (2, N_EDGES), 0, N_NODES, dtype=jnp.int32)
        edge_attr = jax.random.uniform(ks[2], (N_EDGES, 1), dtype=jnp.float32)
        Wl = jax.random.normal(ks[3], (D, D), dtype=jnp.float32) * s
        Wr = jax.random.normal(ks[4], (D, D), dtype=jnp.float32) * s
        We = jax.random.normal(ks[5], (1, D), dtype=jnp.float32) * s
        att = jax.random.normal(ks[6], (D,), dtype=jnp.float32) * s
        return {'x': x, 'edge_index': edge_index, 'edge_attr': edge_attr, 'Wl': Wl, 'bl': jnp.zeros((D,), jnp.float32), 'Wr': Wr, 'br': jnp.zeros((D,), jnp.float32), 'We': We, 'att': att, 'bias_out': jnp.zeros((D,), jnp.float32), 'bn_gamma': jnp.ones((D,), jnp.float32), 'bn_beta': jnp.zeros((D,), jnp.float32)}
    _L2_gnn_all = _L2_gnn_setup()
    _L2_gnn_in = {k: v for k, v in _L2_gnn_all.items() if k in ('Wl', 'bl', 'Wr', 'br', 'We', 'att', 'bias_out', 'bn_gamma', 'bn_beta')}
    del _L2_gnn_all

    def _L3_gnn_setup():
        import jax, jax.numpy as jnp
        import numpy as np
        from jax import lax
        EMBED_DIM = 128
        N_RELATIONS = 64
        N_ENTITIES = 12500
        N_EDGES = 75000
        key = jax.random.key(seed)
        k1, k2, k3, k4, k5, k6 = jax.random.split(key, 6)
        entity_emb = jax.random.normal(k1, (N_ENTITIES, EMBED_DIM), dtype=jnp.float32)
        heads = jax.random.randint(k2, (N_EDGES,), 0, N_ENTITIES)
        rels = jax.random.randint(k3, (N_EDGES,), 0, N_RELATIONS)
        tails = jax.random.randint(k4, (N_EDGES,), 0, N_ENTITIES)
        rel_embed_weight = 0.01 * jax.random.normal(k5, (N_RELATIONS, EMBED_DIM), dtype=jnp.float32)
        xavier = float(np.sqrt(6.0 / (EMBED_DIM + EMBED_DIM)))
        W = jax.random.uniform(k6, (EMBED_DIM, EMBED_DIM), dtype=jnp.float32, minval=-xavier, maxval=xavier)
        return {'entity_emb': entity_emb, 'rel_embed_weight': rel_embed_weight, 'W': W, 'heads': heads, 'rels': rels, 'tails': tails}
    _L3_gnn_all = _L3_gnn_setup()
    _L3_gnn_in = {k: v for k, v in _L3_gnn_all.items() if k in ('rel_embed_weight', 'W')}
    del _L3_gnn_all
    return {'x': x, 'src': src, 'dst': dst, 'edge_attr_20': edge_attr_20, 'edge_type_64': edge_type_64, 'edge_weight1': edge_weight1, 'L0_gnn_W1': _L0_gnn_in['W1'], 'L0_gnn_b1': _L0_gnn_in['b1'], 'L0_gnn_W2': _L0_gnn_in['W2'], 'L0_gnn_b2': _L0_gnn_in['b2'], 'L1_gnn_W_in': _L1_gnn_in['W_in'], 'L1_gnn_W_f1': _L1_gnn_in['W_f1'], 'L1_gnn_b_f1': _L1_gnn_in['b_f1'], 'L1_gnn_W_f2': _L1_gnn_in['W_f2'], 'L1_gnn_b_f2': _L1_gnn_in['b_f2'], 'L1_gnn_W_o1': _L1_gnn_in['W_o1'], 'L1_gnn_b_o1': _L1_gnn_in['b_o1'], 'L1_gnn_W_o2': _L1_gnn_in['W_o2'], 'L1_gnn_b_o2': _L1_gnn_in['b_o2'], 'L2_gnn_Wl': _L2_gnn_in['Wl'], 'L2_gnn_bl': _L2_gnn_in['bl'], 'L2_gnn_Wr': _L2_gnn_in['Wr'], 'L2_gnn_br': _L2_gnn_in['br'], 'L2_gnn_We': _L2_gnn_in['We'], 'L2_gnn_att': _L2_gnn_in['att'], 'L2_gnn_bias_out': _L2_gnn_in['bias_out'], 'L2_gnn_bn_gamma': _L2_gnn_in['bn_gamma'], 'L2_gnn_bn_beta': _L2_gnn_in['bn_beta'], 'L3_gnn_rel_embed_weight': _L3_gnn_in['rel_embed_weight'], 'L3_gnn_W': _L3_gnn_in['W']}

def reference(x, src, dst, edge_attr_20, edge_type_64, edge_weight1, L0_gnn_W1, L0_gnn_b1, L0_gnn_W2, L0_gnn_b2, L1_gnn_W_in, L1_gnn_W_f1, L1_gnn_b_f1, L1_gnn_W_f2, L1_gnn_b_f2, L1_gnn_W_o1, L1_gnn_b_o1, L1_gnn_W_o2, L1_gnn_b_o2, L2_gnn_Wl, L2_gnn_bl, L2_gnn_Wr, L2_gnn_br, L2_gnn_We, L2_gnn_att, L2_gnn_bias_out, L2_gnn_bn_gamma, L2_gnn_bn_beta, L3_gnn_rel_embed_weight, L3_gnn_W):
    import jax
    import jax.numpy as jnp

    def _L0_gnn_ref(x, edge_index, W1, b1, W2, b2):
        import jax, jax.numpy as jnp
        import numpy as np
        N_NODES = 6250
        N_EDGES = 75000
        D_IN = 128
        D_OUT = 128
        EPS = 0.0
        src = edge_index[0]
        dst = edge_index[1]
        agg = jax.ops.segment_sum(x[src], dst, num_segments=N_NODES)
        h = (1.0 + EPS) * x + agg
        h = jax.nn.relu(h @ W1 + b1)
        return h @ W2 + b2

    def _L1_gnn_ref(atomic_embedding, pair_indices, f_ij, f_ij_cutoff, W_in, W_f1, b_f1, W_f2, b_f2, W_o1, b_o1, W_o2, b_o2):
        import jax, jax.numpy as jnp
        import numpy as np
        N_ATOMS = 6250
        N_PAIRS = 200000
        F = 128
        NF = 128
        RBF = 20
        LOG2 = float(np.log(2.0))

        def shifted_softplus(x):
            return jax.nn.softplus(x) - LOG2
        idx_i = pair_indices[0]
        idx_j = pair_indices[1]
        x = atomic_embedding @ W_in
        W_ij = shifted_softplus(f_ij @ W_f1 + b_f1) @ W_f2 + b_f2
        W_ij = W_ij * f_ij_cutoff
        x_ij = x[idx_j] * W_ij
        out = jax.ops.segment_sum(x_ij, idx_i, num_segments=N_ATOMS)
        return shifted_softplus(out @ W_o1 + b_o1) @ W_o2 + b_o2

    def _L2_gnn_ref(x, edge_index, edge_attr, Wl, bl, Wr, br, We, att, bias_out, bn_gamma, bn_beta):
        import jax, jax.numpy as jnp
        import numpy as np
        N_NODES = 6250
        N_EDGES = 80000
        D = 128
        BN_EPS = 1e-05
        NEG_SLOPE = 0.2

        def _gatv2(x, edge_index, edge_attr, Wl, bl, Wr, br, We, att, bias_out):
            src, dst = (edge_index[0], edge_index[1])
            xl = x @ Wl + bl
            xr = x @ Wr + br
            e = edge_attr @ We
            m = xl[src] + xr[dst] + e
            m = jax.nn.leaky_relu(m, NEG_SLOPE)
            logits = m @ att
            n = x.shape[0]
            mx = jax.ops.segment_max(logits, dst, num_segments=n)
            ex = jnp.exp(logits - mx[dst])
            den = jax.ops.segment_sum(ex, dst, num_segments=n)
            alpha = ex / (den[dst] + 1e-16)
            out = jax.ops.segment_sum(xl[src] * alpha[:, None], dst, num_segments=n)
            return out + bias_out
        h = x + _gatv2(x, edge_index, edge_attr, Wl, bl, Wr, br, We, att, bias_out)
        h = jax.nn.gelu(h, approximate=False)
        mean = jnp.mean(h, axis=0)
        var = jnp.mean((h - mean) ** 2, axis=0)
        h = (h - mean) * jax.lax.rsqrt(var + BN_EPS) * bn_gamma + bn_beta
        return h

    def _L3_gnn_ref(entity_emb, rel_embed_weight, W, heads, rels, tails):
        import jax, jax.numpy as jnp
        import numpy as np
        from jax import lax
        EMBED_DIM = 128
        N_RELATIONS = 64
        N_ENTITIES = 12500
        N_EDGES = 75000
        n_entities = entity_emb.shape[0]
        e_h = entity_emb[heads]
        e_t = entity_emb[tails]
        e_r = rel_embed_weight[rels]
        score = jnp.sum(e_t * jnp.tanh(e_h + e_r), axis=-1)
        score_exp = jnp.exp(score - lax.stop_gradient(jnp.max(score)))
        score_sum = jax.ops.segment_sum(score_exp, heads, num_segments=n_entities)
        attn = score_exp / (score_sum[heads] + 1e-10)
        agg = jax.ops.segment_sum(attn[:, None] * e_t, heads, num_segments=n_entities)
        out = (entity_emb + agg) @ W.T
        return jax.nn.leaky_relu(out, negative_slope=0.2)
    edge_index = jnp.stack([src, dst])
    h = jnp.maximum(_layernorm(x, axis=-1), 0.0)
    x = x + _L0_gnn_ref(h, edge_index, L0_gnn_W1, L0_gnn_b1, L0_gnn_W2, L0_gnn_b2)
    h = jnp.maximum(_layernorm(x, axis=-1), 0.0)
    x = x + _L1_gnn_ref(h, edge_index, edge_attr_20, edge_weight1, L1_gnn_W_in, L1_gnn_W_f1, L1_gnn_b_f1, L1_gnn_W_f2, L1_gnn_b_f2, L1_gnn_W_o1, L1_gnn_b_o1, L1_gnn_W_o2, L1_gnn_b_o2)
    h = jnp.maximum(_layernorm(x, axis=-1), 0.0)
    x = x + _L2_gnn_ref(h, edge_index, edge_weight1, L2_gnn_Wl, L2_gnn_bl, L2_gnn_Wr, L2_gnn_br, L2_gnn_We, L2_gnn_att, L2_gnn_bias_out, L2_gnn_bn_gamma, L2_gnn_bn_beta)
    h = jnp.maximum(_layernorm(x, axis=-1), 0.0)
    x = x + _L3_gnn_ref(h, L3_gnn_rel_embed_weight, L3_gnn_W, src, edge_type_64, dst)
    return x

_drawn_inputs = setup_inputs


def setup_inputs(seed=0):
    import zlib

    import numpy as np

    out = dict(_drawn_inputs(seed))
    spreads = {'L1_gnn_b_f1': (0.0, 0.1),
     'L1_gnn_b_f2': (0.0, 0.1),
     'L1_gnn_b_o1': (0.0, 0.652),
     'L1_gnn_b_o2': (0.0, 0.441),
     'L2_gnn_bl': (0.0, 0.344),
     'L2_gnn_br': (0.0, 2.0),
     'L2_gnn_bias_out': (0.0, 0.323),
     'L2_gnn_bn_gamma': (1.0, 0.2),
     'L2_gnn_bn_beta': (0.0, 0.469)}
    factors = {'L0_gnn_b1': 8.0,
     'L0_gnn_b2': 4.681,
     'L2_gnn_Wr': 8.0,
     'L2_gnn_We': 29.925,
     'L2_gnn_att': 2.751,
     'L3_gnn_rel_embed_weight': 193.827}
    for name, (base, spread) in spreads.items():
        noise = np.random.default_rng([zlib.crc32(name.encode()), seed]).standard_normal(out[name].shape)
        drawn = base * np.exp(spread * noise) if base else spread * noise
        out[name] = jnp.asarray(drawn.astype(out[name].dtype))
    for name, factor in factors.items():
        out[name] = (out[name] * factor).astype(out[name].dtype)
    return out
```

```python
from contextlib import ExitStack

import concourse.bass as bass
from concourse import mybir

F32 = mybir.dt.float32
BF16 = mybir.dt.bfloat16
I32 = mybir.dt.int32
ALU = mybir.AluOpType
ACT = mybir.ActivationFunctionType
AX = mybir.AxisListType.X

P = 128
NODES = 6250
D = 128
EDGES = 200000
RBF = 20
NTYPE = 64
LOG2 = 0.6931471805599453

WIN = (NODES + P - 1) // P
WP = WIN + 1
LAST = NODES - (WIN - 1) * P
KG = 4
GE = KG * P
U = 4
NG = (EDGES // GE + 1 + WIN + U - 1) // U * U
T = 10
NCH = (EDGES + GE + P * T - 1) // (P * T)
J = NCH * T
EP = P * J
JC = J // 5
FULL = EDGES // J
REST = EDGES - FULL * J
RW = 24
C_WT, C_SRC, C_DST, C_TYPE = 20, 21, 22, 23
MW = 132
M_SRC, M_DST, M_TYPE = 128, 129, 130
NOWHERE = WP * P
BIG = 2.0 ** 100
LOW = -(2.0 ** 90)
FAR = float(1 << 22)
NL = NG + 2 * U
GP = NL // KG


class Since:

    def __init__(self):
        self.counts = {}

    def __call__(self, sem):
        return self.counts.get(sem.name, 0)

    def passed(self, n, *sems):
        for sem in sems:
            self.counts[sem.name] = self(sem) + n


def flat(ap):
    return ap.rearrange("p a b -> p (a b)")


def program(nc, x, src, dst, attr, etype, weight, W1, b1, W2, b2, W_in, W_f1, b_f1, W_f2, b_f2,
            W_o1, b_o1, W_o2, b_o2, Wl, bl, Wr, br, We, att, bias_out, bn_g, bn_b, rel, WT3, out):
    since = Since()
    top = ExitStack()

    def sb(stack, name, shape, dt=F32):
        return stack.enter_context(nc.sbuf_tensor(name, shape, dt))

    def pb(stack, name, shape, dt=F32):
        return stack.enter_context(nc.psum_tensor(name, shape, dt))

    def sem(name, stack=top):
        return stack.enter_context(nc.semaphore(name))

    def dram(name, shape, dt=F32):
        return nc.dram_tensor(name, shape, dt, kind="Internal").ap()

    with top:
        erec = dram("edge_records", [EP, RW])
        epos = dram("edge_positions", [EP, 1], I32)
        mrec = dram("message_records", [EP, MW])
        table3 = dram("split_table", [WP * P, 3 * D], BF16)
        table = dram("node_table", [WP * P, D])
        lists = dram("group_lists", [2, 2, NL], I32)
        bases = dram("group_bases", [2, NL])

        iota_b = sb(top, "iota_b", [P, P], BF16)
        iota_w = sb(top, "iota_w", [P, WP], BF16)
        iota_i = sb(top, "iota_i", [P, P], I32)
        ident = sb(top, "ident", [P, P])
        ident_b = sb(top, "ident_b", [P, P], BF16)
        apart_b = sb(top, "apart_b", [P, P], BF16)
        before_b = sb(top, "before_b", [P, P], BF16)
        ones = sb(top, "ones", [P, P])
        ones_b = sb(top, "ones_b", [P, P], BF16)
        glist = [sb(top, f"glist{o}", [1, 2, NL], I32) for o in range(2)]
        gbase = [sb(top, f"gbase{o}", [P, NL]) for o in range(2)]
        weights = {}
        for name, w in dict(W1=W1, W2=W2, W_in=W_in, W_f2=W_f2, W_o1=W_o1, W_o2=W_o2, Wl=Wl, Wr=Wr,
                            WT3=WT3).items():
            weights[name] = sb(top, "w_" + name, [P, D]), w
        w_f1 = sb(top, "w_f1", [RBF, D])
        rows = {}
        for name, b in dict(b1=b1, b2=b2, b_o1=b_o1, b_o2=b_o2, bl=bl, br=br).items():
            rows[name] = sb(top, "row_" + name, [1, D]), b
        wide = {}
        for name, b in dict(b_f2=b_f2, We=We, att=att, bias_out=bias_out, bn_g=bn_g, bn_b=bn_b).items():
            wide[name] = sb(top, "wide_" + name, [P, D]), b
        bf1 = sb(top, "bf1", [P, 1])
        rel_f = sb(top, "rel_f", [NTYPE, D])
        rel3 = sb(top, "rel3", [NTYPE, 3 * D], BF16)
        relr = sb(top, "relr", [NTYPE, D])

        loaded, made, cast, chain, stored = (sem(n) for n in ("loaded", "made", "cast", "chain", "stored"))
        linked = [0]

        def link(eng, ins):
            linked[0] += 1
            ins.then_inc(chain, 1)
            eng.wait_ge(chain, linked[0])

        n_loads = len(weights) + len(rows) + len(wide) + 3
        with nc.Block() as block:
            @block.sync
            def _(sp):
                for t, w in weights.values():
                    sp.dma_start(t[:, :], w).then_inc(loaded, 16)
                for t, b in rows.values():
                    sp.dma_start(t[:, :], b.rearrange("(a n) -> a n", a=1)).then_inc(loaded, 16)
                for t, b in wide.values():
                    b = b if len(b.shape) == 2 else b.rearrange("(a n) -> a n", a=1)
                    sp.dma_start(t[:, :], b.broadcast_to([P, D])).then_inc(loaded, 16)
                sp.dma_start(w_f1[:, :], W_f1).then_inc(loaded, 16)
                sp.dma_start(bf1[:, :], b_f1.rearrange("(n a) -> n a", a=1)).then_inc(loaded, 16)
                sp.dma_start(rel_f[:, :], rel).then_inc(loaded, 16)
                sp.wait_ge(loaded, 16 * n_loads)

            @block.gpsimd
            def _(pool):
                pool.iota(iota_i[:, :], pattern=[[1, P]], base=0, channel_multiplier=0).then_inc(made, 1)
                pool.memset(ident[:, :], 0.0).then_inc(made, 1)
                pool.memset(before_b[:, :], 1.0).then_inc(made, 1)
                pool.wait_ge(made, 3)
                pool.affine_select(out=ident[:, :], in_=ident[:, :], compare_op=ALU.not_equal, fill=1.0,
                                   base=0, pattern=[[-1, P]], channel_multiplier=1).then_inc(made, 1)
                pool.affine_select(out=before_b[:, :], in_=before_b[:, :], compare_op=ALU.is_ge, fill=0.0,
                                   base=-1, pattern=[[1, P]], channel_multiplier=-1).then_inc(made, 1)

            @block.vector
            def _(dve):
                dve.wait_ge(made, 5)
                nc.vector.tensor_copy(iota_b[:, :], iota_i[:, :]).then_inc(cast, 1)
                nc.vector.tensor_copy(iota_w[:, :], iota_i[:, 0:WP]).then_inc(cast, 1)
                nc.vector.tensor_copy(ident_b[:, :], ident[:, :]).then_inc(cast, 1)
                nc.vector.tensor_scalar(apart_b[:, :], ident[:, :], BIG, -BIG, ALU.mult, ALU.add).then_inc(cast, 1)
                nc.vector.memset(ones[:, :], 1.0).then_inc(cast, 1)
                nc.vector.memset(ones_b[:, :], 1.0).then_inc(cast, 1)
                dve.wait_ge(loaded, 16 * n_loads)
                split3(nc, lambda ins: link(dve, ins), rel3[:, 0:D], rel3[:, D:2 * D], rel3[:, 2 * D:3 * D],
                       rel_f[:, :], relr[:, :])

        k = Kit()
        k.nc, k.since, k.link, k.chain, k.linked, k.sem, k.sb, k.pb = nc, since, link, chain, linked, sem, sb, pb
        k.x, k.out = x, out
        k.src, k.dst, k.attr, k.etype, k.weight = src, dst, attr, etype, weight
        k.erec, k.epos, k.mrec, k.table3, k.table, k.lists, k.bases = erec, epos, mrec, table3, table, lists, bases
        k.iota_b, k.iota_w, k.ident, k.ident_b, k.apart_b = iota_b, iota_w, ident, ident_b, apart_b
        k.before_b, k.ones, k.ones_b, k.glist, k.gbase = before_b, ones, ones_b, glist, gbase
        k.weights, k.rows, k.wide, k.w_f1, k.bf1, k.rel3 = weights, rows, wide, w_f1, bf1, rel3
        k.banks = pb(top, "banks", [P, 8, 512])
        k.psum = [k.banks[:, i, :] for i in range(8)]
        pack_edges(k)
        k.xs = sb(top, "xs", [P, WIN, D])
        k.hs = sb(top, "hs", [P, WIN, D])
        k.acc = sb(top, "acc", [P, WP, MW])
        k.near = sb(top, "near", [P, WP, 3 * D], BF16)
        k.staging, k.staging_t = sb(top, "staging", [P, TILES * D]), sb(top, "staging_t", [P, TILES * D])
        k.top_score = sb(top, "top_score", [P, WP])
        k.stat = [sb(top, f"stat{i}", [P, WIN]) for i in range(2)]
        k.top, k.stored, k.begun = top, stored, sem("begun")
        k.stage = {n: sem(n) for n in (
            "staged", "turned", "turned_sb", "multiplied", "epilogued", "bulk_act", "bulk_pe",
            "rel_ready", "onehot_ready", "onehot_turned", "onehotT_ready", "summed", "added", "row_used",
            "attr_turned", "attrT_ready", "hidden_ready", "soft1", "soft2", "soft3", "soft4", "soft_ready",
            "filter_ready", "far_ready", "biased", "message_ready", "index_ready", "meta_ready",
            "edge_term", "near_ready", "in1", "in2", "in3", "product", "summed_up", "scores", "spread", "group_max",
            "new_max", "exp_in", "max_kept", "weighed", "shrink", "prob_turned", "prob_ready")}
        k.rows_in = [sem(f"rows_in{u}") for u in range(U)]
        k.pool_done = [sem(f"pool_done{u}") for u in range(U)]

        load_nodes(k)
        layernorm_relu(k)
        publish(k, k.hs, True)
        segment_sums(k, 0)
        node_product(k, "W1", "b1", k.hs, k.hs, "relu", add=k.acc)
        node_product(k, "W2", "b2", k.hs, k.xs, "add")

        layernorm_relu(k)
        node_product(k, "W_in", None, k.hs, k.hs, "copy")
        split_near(k, k.hs)
        filter_messages(k)
        segment_sums(k, 1)
        node_product(k, "W_o1", "b_o1", k.acc, k.hs, "copy")
        shifted_softplus(k)
        node_product(k, "W_o2", "b_o2", k.hs, k.xs, "add")

        layernorm_relu(k)
        with nc.sbuf_tensor("right", [P, WIN, D], F32) as right:
            node_product(k, "Wl", "bl", k.hs, right, "copy")
            publish(k, right, False)
            node_product(k, "Wr", "br", k.hs, right, "copy")
            split_near(k, right)
        attention(k, 0)
        gat_output(k)

        layernorm_relu(k)
        publish(k, k.hs, False)
        split_near(k, k.hs)
        attention(k, 1)
        relation_output(k)
        node_product(k, "WT3", None, k.hs, k.xs, "leaky")
        store_nodes(k)


class Kit:
    pass


def split3(nc, link, hi, mid, lo, source, rest):
    link(nc.vector.tensor_copy(hi, source))
    link(nc.vector.tensor_tensor(rest, source, hi, ALU.subtract))
    link(nc.vector.tensor_copy(mid, rest))
    link(nc.vector.tensor_tensor(rest, rest, mid, ALU.subtract))
    link(nc.vector.tensor_copy(lo, rest))


def pack_edges(k):
    nc, link, sem, sb = k.nc, k.link, k.sem, k.sb
    with ExitStack() as own:
        ends = [sb(own, n, [P, J], I32) for n in ("e_src", "e_dst", "e_type")]
        e_wt = sb(own, "e_wt", [P, J])
        win_i = sb(own, "win_i", [P, J], I32)
        win = [sb(own, f"win{o}", [P, J + 2 * T], BF16) for o in range(2)]
        at = sb(own, "at", [P, 2, JC * RBF])
        rec = sb(own, "rec", [P, 2, JC * RW])
        cleared, ends_in, packed = sem("cleared"), sem("ends_in"), sem("packed")
        attr_in = [sem(f"attr_in{s}") for s in range(2)]
        rec_out = [sem(f"rec_out{s}") for s in range(2)]
        pads = (WIN * P, NOWHERE, 0)
        nchunk = J // JC

        def split_pad(t, view, width, c0, n):
            pairs = [(t[0:FULL, 0:n * width], view[0:FULL * J * width]
                      .rearrange("(p j) -> p j", p=FULL)[:, c0 * width:(c0 + n) * width])]
            m = max(0, min(n, REST - c0))
            if m:
                lo = (FULL * J + c0) * width
                pairs.append((t[FULL:FULL + 1, 0:m * width],
                              view[lo:lo + m * width].rearrange("(a j) -> a j", a=1)))
            return pairs

        flats = [k.src, k.dst, k.etype]
        attr_flat = k.attr.rearrange("e r -> (e r)")
        n_ends = len(split_pad(e_wt, k.weight.rearrange("e a -> (e a)"), 1, 0, J)) * 4

        with nc.Block() as block:
            @block.sync
            def _(sp):
                sp.wait_ge(cleared, 6)
                for t, v in zip(ends + [e_wt], flats + [k.weight.rearrange("e a -> (e a)")]):
                    for to, of in split_pad(t, v, 1, 0, J):
                        sp.dma_start(to, of).then_inc(ends_in, 16)
                out_view = k.erec.rearrange("(p j) c -> p (j c)", p=P)
                count = [0, 0]
                for c in range(nchunk):
                    if c >= 2:
                        sp.wait_ge(packed, c - 1)
                    for to, of in split_pad(at[:, c % 2, :], attr_flat, RBF, c * JC, JC):
                        sp.dma_start(to, of).then_inc(attr_in[c % 2], 16)
                    if c >= 1:
                        sp.wait_ge(packed, c)
                        sp.dma_start(out_view[:, (c - 1) * JC * RW:c * JC * RW],
                                     rec[:, (c - 1) % 2, :]).then_inc(rec_out[(c - 1) % 2], 16)
                sp.wait_ge(packed, nchunk)
                sp.dma_start(out_view[:, (nchunk - 1) * JC * RW:], rec[:, (nchunk - 1) % 2, :])\
                    .then_inc(rec_out[(nchunk - 1) % 2], 16)
                for s in range(2):
                    sp.wait_ge(rec_out[s], 16 * len(range(s, nchunk, 2)))

            @block.vector
            def _(dve):
                for t, pad in zip(ends, pads):
                    nc.vector.memset(t[:, :], pad).then_inc(cleared, 1)
                nc.vector.memset(e_wt[:, :], 0.0).then_inc(cleared, 1)
                nc.vector.memset(at[:, :, :], 0.0).then_inc(cleared, 1)
                nc.vector.memset(rec[:, :, :], 0.0).then_inc(cleared, 1)
                dve.wait_ge(ends_in, 16 * n_ends)
                for o, t in ((0, ends[1]), (1, ends[0])):
                    link(dve, nc.vector.tensor_scalar(win_i[:, :], t[:, :], 7, None, ALU.logical_shift_right))
                    link(dve, nc.vector.tensor_copy(win[o][:, 0:J], win_i[:, :]))
                    link(dve, nc.vector.memset(win[o][:, J:], float(WIN)))
                arrived = [0, 0]
                for c in range(nchunk):
                    s = c % 2
                    arrived[s] += 16 * len(split_pad(at[:, s, :], attr_flat, RBF, c * JC, JC))
                    dve.wait_ge(attr_in[s], arrived[s])
                    if c >= 2:
                        dve.wait_ge(rec_out[s], 16 * (c // 2))
                    r = rec[:, s, :].rearrange("p (j c) -> p j c", c=RW)
                    ri = r.bitcast(I32)
                    cols = slice(c * JC, (c + 1) * JC)
                    link(dve, nc.vector.tensor_copy(r[:, :, 0:RBF], at[:, s, :].rearrange("p (j c) -> p j c", c=RBF)))
                    link(dve, nc.vector.tensor_copy(r[:, :, C_WT], e_wt[:, cols]))
                    link(dve, nc.vector.tensor_copy(ri[:, :, C_SRC], ends[0][:, cols]))
                    link(dve, nc.vector.tensor_copy(ri[:, :, C_DST], ends[1][:, cols]))
                    nc.vector.tensor_copy(ri[:, :, C_TYPE], ends[2][:, cols]).then_inc(packed, 1)
                    dve.wait_ge(packed, c + 1)

        hot = sb(own, "hot", [P, 2, T, WP], BF16)
        count = [sb(own, f"count{o}", [P, WP]) for o in range(2)]
        hot_ready, hot_used, counted = sem("hot_ready"), sem("hot_used"), sem("counted")
        first = [sb(own, f"first{o}", [P, WP]) for o in range(2)]

        def one_hot(o, col, s):
            return nc.vector.tensor_tensor(
                hot[:, s, :, :], win[o][:, col].unsqueeze(2).to_broadcast([P, T, WP]),
                k.iota_w[:, :].unsqueeze(1).to_broadcast([P, T, WP]), ALU.is_equal)

        cols = lambda ch: bass.ds(ch * T, T)
        for o in range(2):
            with nc.Block() as block:
                @block.vector
                def _(dve):
                    h0 = k.since(hot_used)
                    for s in range(2):
                        one_hot(o, cols(s), s).then_inc(hot_ready, 1)
                    with dve.Fori(2, NCH - 1, 2) as c:
                        for s in range(2):
                            dve.wait_ge(hot_used, h0 + c + (s - 1))
                            one_hot(o, cols(c + s), s).then_inc(hot_ready, 1)
                    dve.wait_ge(hot_used, h0 + NCH - 2)
                    one_hot(o, cols(NCH - 1), 0).then_inc(hot_ready, 1)
                    dve.wait_ge(hot_used, h0 + NCH)
                    nc.vector.tensor_reduce(count[o][:, :], k.psum[0][:, 0:T * WP].rearrange("p (t w) -> p w t", w=WP),
                                            AX, ALU.add).then_inc(counted, 1)
                    dve.wait_ge(counted, o + 1)

                @block.tensor
                def _(pe):
                    h0 = k.since(hot_ready)

                    def add(s, **f):
                        return nc.tensor.matmul(k.psum[0][:, 0:T * WP], k.ones_b[:, :],
                                                hot[:, s, :, :].rearrange("p t w -> p (t w)"), **f)
                    pe.wait_ge(hot_ready, h0 + 1)
                    add(0, start=True, stop=False).then_inc(hot_used, 1)
                    pe.wait_ge(hot_ready, h0 + 2)
                    add(1, start=False, stop=False).then_inc(hot_used, 1)
                    with pe.Fori(2, NCH - 1, 2) as c:
                        for s in range(2):
                            pe.wait_ge(hot_ready, h0 + c + (s + 1))
                            add(s, start=False, stop=False).then_inc(hot_used, 1)
                    pe.wait_ge(hot_ready, h0 + NCH)
                    add(0, start=False, stop=True).then_inc(hot_used, 1)
            k.since.passed(NCH, hot_ready, hot_used)

        a = [sb(own, f"scan{i}", [P, WP]) for i in range(2)]
        groups, groups_i = sb(own, "groups", [P, WP]), sb(own, "groups_i", [P, WP], I32)
        gi_i, gi = sb(own, "gi_i", [GP, KG], I32), sb(own, "gi", [GP, KG])
        past = sb(own, "past", [GP, KG, WIN])
        took = sb(own, "took", [GP, KG, WIN])
        gw, gs = [sb(own, f"gw{o}", [GP, KG]) for o in range(2)], [sb(own, f"gs{o}", [GP, KG]) for o in range(2)]
        gw_i, gs_i = [sb(own, f"gwi{o}", [GP, KG], I32) for o in range(2)], [sb(own, f"gsi{o}", [GP, KG], I32) for o in range(2)]
        gb = [sb(own, f"gb{o}", [GP, KG]) for o in range(2)]
        run = sb(own, "run", [P, WP])
        numbered, listed, list_out, list_in = sem("numbered"), sem("listed"), sem("list_out"), sem("list_in")

        def scan(dve, source, n):
            cur, other = source, 0
            step = 1
            while step < n:
                nxt = a[other]
                link(dve, nc.vector.tensor_copy(nxt[:, 0:step], cur[:, 0:step]))
                link(dve, nc.vector.tensor_tensor(nxt[:, step:n], cur[:, step:n], cur[:, 0:n - step], ALU.add))
                cur, other, step = nxt, 1 - other, 2 * step
            return cur

        with nc.Block() as block:
            @block.gpsimd
            def _(pool):
                pool.iota(gi_i[:, :], pattern=[[1, KG]], base=0, channel_multiplier=KG).then_inc(numbered, 1)

            @block.vector
            def _(dve):
                dve.wait_ge(numbered, 1)
                link(dve, nc.vector.tensor_copy(gi[:, :], gi_i[:, :]))
                for o in range(2):
                    ends_at = scan(dve, count[o], WP)
                    link(dve, nc.vector.tensor_tensor(first[o][:, :], ends_at[:, 0:WP], count[o][:, :], ALU.subtract))
                    link(dve, nc.vector.tensor_scalar(groups_i[:, :], count[o][:, :], float(GE - 1), None, ALU.add))
                    link(dve, nc.vector.tensor_scalar(groups_i[:, :], groups_i[:, :], GE.bit_length() - 1, None,
                                                      ALU.logical_shift_right))
                    link(dve, nc.vector.tensor_copy(groups[:, :], groups_i[:, :]))
                    upto = scan(dve, groups, WIN)
                    link(dve, nc.vector.tensor_tensor(past[:, :, :], gi[:, :].unsqueeze(2).to_broadcast([GP, KG, WIN]),
                                                      upto[0:GP, 0:WIN].unsqueeze(1).to_broadcast([GP, KG, WIN]), ALU.is_ge))
                    link(dve, nc.vector.tensor_reduce(gw[o][:, :], past[:, :, :], AX, ALU.add))
                    link(dve, nc.vector.scalar_tensor_tensor(groups[:, 0:WIN], groups[:, 0:WIN], -float(GE),
                                                             count[o][:, 0:WIN], ALU.mult, ALU.add))
                    link(dve, nc.vector.tensor_tensor(took[:, :, :], past[:, :, :],
                                                      groups[0:GP, 0:WIN].unsqueeze(1).to_broadcast([GP, KG, WIN]), ALU.mult))
                    link(dve, nc.vector.tensor_reduce(gs[o][:, :], took[:, :, :], AX, ALU.add))
                    link(dve, nc.vector.scalar_tensor_tensor(gs[o][:, :], gi[:, :], float(GE), gs[o][:, :], ALU.mult, ALU.add))
                    link(dve, nc.vector.tensor_scalar(gs[o][:, :], gs[o][:, :], float(EDGES), None, ALU.min))
                    link(dve, nc.vector.tensor_copy(gs_i[o][:, :], gs[o][:, :]))
                    link(dve, nc.vector.tensor_copy(gw_i[o][:, :], gw[o][:, :]))
                    link(dve, nc.vector.tensor_scalar(gb[o][:, :], gw[o][:, :], float(P), None, ALU.mult))
                nc.vector.tensor_copy(run[:, :], first[1][:, :]).then_inc(listed, 1)

            @block.sync
            def _(sp):
                sp.wait_ge(listed, 1)
                for o in range(2):
                    for i, t in enumerate((gw_i[o], gs_i[o])):
                        sp.dma_start(k.lists[o, i, :].rearrange("(p q) -> p q", p=GP), t[:, :]).then_inc(list_out, 16)
                    sp.dma_start(k.bases[o, :].rearrange("(p q) -> p q", p=GP), gb[o][:, :]).then_inc(list_out, 16)
                sp.wait_ge(list_out, 96)
                for o in range(2):
                    sp.dma_start(k.glist[o][:, :, :], k.lists[o, :, :].rearrange("(a i) g -> a i g", a=1)).then_inc(list_in, 16)
                    sp.dma_start(k.gbase[o][:, :], k.bases[o:o + 1, :].broadcast_to([P, NL])).then_inc(list_in, 16)
                sp.wait_ge(list_in, 64)

        pos = sb(own, "pos", [P, J])
        pos_i = sb(own, "pos_i", [P, J], I32)
        place = sb(own, "place", [P, 2, T, WP])
        ranked, placed, based, own_place = (sem(n) for n in ("ranked", "placed", "based", "own_place"))
        reduced = sem("reduced")
        pos_ready, pos_out = sem("pos_ready"), sem("pos_out")
        with nc.Block() as block:
            @block.vector
            def _(dve):
                h0 = k.since(hot_ready)
                for s in range(2):
                    one_hot(1, cols(s), s).then_inc(hot_ready, 1)
                dve.sem_inc(based, 2)

                def rank(c, s):
                    dve.wait_ge(ranked, c + (s + 1))
                    dve.wait_ge(based, c + (s + 2))
                    nc.vector.tensor_tensor(place[:, s, :, :], k.psum[2 * s][:, 0:T * WP].rearrange("p (t w) -> p t w", w=WP),
                                            run[:, :].unsqueeze(1).to_broadcast([P, T, WP]), ALU.add).then_inc(placed, 1)
                    dve.wait_ge(placed, c + (s + 1))
                    nc.vector.tensor_tensor(run[:, :], run[:, :], k.psum[2 * s + 1][:, 0:WP], ALU.add).then_inc(based, 1)
                    dve.wait_ge(hot_ready, h0 + c + (s + 1))
                    nc.vector.tensor_tensor(place[:, s, :, :], place[:, s, :, :], hot[:, s, :, :], ALU.mult).then_inc(own_place, 1)
                    dve.wait_ge(own_place, c + (s + 1))
                    nc.vector.tensor_reduce(pos[:, cols(c + s)], place[:, s, :, :], AX, ALU.add).then_inc(reduced, 1)
                with dve.Fori(0, NCH - 1, 2) as c:
                    for s in range(2):
                        rank(c, s)
                        one_hot(1, cols(c + (s + 2)), s).then_inc(hot_ready, 1)
                rank(NCH - 1, 0)
                dve.wait_ge(reduced, NCH)
                nc.vector.tensor_copy(pos_i[:, :], pos[:, :]).then_inc(pos_ready, 1)

            @block.tensor
            def _(pe):
                h0 = k.since(hot_ready)

                def rank(c, s):
                    pe.wait_ge(hot_ready, h0 + c + (s + 1))
                    pe.wait_ge(based, c + (s + 1))
                    f = hot[:, s, :, :].rearrange("p t w -> p (t w)")
                    nc.tensor.matmul(k.psum[2 * s][:, 0:T * WP], k.before_b[:, :], f, start=True, stop=False)
                    for t in range(T - 1):
                        n = T - 1 - t
                        nc.tensor.matmul(k.psum[2 * s][:, (t + 1) * WP:T * WP].rearrange("p (t w) -> p t w", w=WP),
                                         k.ones_b[:, :], hot[:, s, t:t + 1, :].to_broadcast([P, n, WP]),
                                         start=False, stop=t == T - 2)
                    for t in range(T):
                        last = nc.tensor.matmul(k.psum[2 * s + 1][:, 0:WP], k.ones_b[:, :], hot[:, s, t, :],
                                                start=t == 0, stop=t == T - 1)
                    last.then_inc(ranked, 1)
                with pe.Fori(0, NCH - 1, 2) as c:
                    for s in range(2):
                        rank(c, s)
                rank(NCH - 1, 0)

            @block.sync
            def _(sp):
                sp.wait_ge(pos_ready, 1)
                sp.dma_start(k.epos.rearrange("(p j) a -> p (j a)", p=P), pos_i[:, :]).then_inc(pos_out, 16)
                sp.wait_ge(pos_out, 16)
        k.since.passed(NCH + 1, hot_ready)



def load_nodes(k):
    nc, link, xs = k.nc, k.link, k.xs
    zeroed, x_in = k.sem("zeroed"), k.sem("x_in")
    k.valid = k.sb(k.top, "valid", [P, 1])
    valid_i = k.sb(k.top, "valid_i", [P, 1], I32)
    with nc.Block() as block:
        @block.vector
        def _(dve):
            nc.vector.memset(xs[:, WIN - 1, :], 0.0).then_inc(zeroed, 1)
            dve.wait_ge(x_in, 1)
            link(dve, nc.vector.tensor_copy(k.valid[:, :], valid_i[:, :]))
            link(dve, nc.vector.tensor_scalar(k.valid[:, :], k.valid[:, :], float(LAST), None, ALU.is_lt))
            link(dve, nc.vector.memset(k.near[:, WIN, :], 0.0))

        @block.gpsimd
        def _(pool):
            pool.iota(valid_i[:, :], pattern=[[0, 1]], base=0, channel_multiplier=1).then_inc(x_in, 1)

        @block.sync
        def _(sp):
            sp.wait_ge(zeroed, 1)
            sp.wait_ge(x_in, 1)
            sp.dma_start(xs[:, 0:WIN - 1, :], k.x[0:(WIN - 1) * P, :].rearrange("(w p) d -> p w d", p=P)).then_inc(x_in, 16)
            sp.dma_start(xs[0:LAST, WIN - 1, :], k.x[(WIN - 1) * P:NODES, :]).then_inc(x_in, 16)
            sp.wait_ge(x_in, 33)


def layernorm_relu(k):
    nc, link, xs, hs = k.nc, k.link, k.xs, k.hs
    sq = k.acc[:, 0:WIN, 0:D]
    stat = k.stat
    by_act = k.stage["bulk_act"]
    b = k.since(by_act)
    with nc.Block() as block:
        @block.vector
        def _(dve):
            link(dve, nc.vector.tensor_reduce(stat[0][:, :], xs[:, :, :], AX, ALU.add))
            link(dve, nc.vector.tensor_scalar(stat[0][:, :], stat[0][:, :], 1.0 / D, None, ALU.mult))
            link(dve, nc.vector.tensor_tensor(hs[:, :, :], xs[:, :, :], stat[0][:, :].unsqueeze(2).to_broadcast([P, WIN, D]),
                                              ALU.subtract))
            link(dve, nc.vector.tensor_tensor(sq, hs[:, :, :], hs[:, :, :], ALU.mult))
            link(dve, nc.vector.tensor_reduce(stat[1][:, :], sq, AX, ALU.add))
            nc.vector.tensor_scalar(stat[1][:, :], stat[1][:, :], 1.0 / D, 1e-5, ALU.mult, ALU.add).then_inc(by_act, 1)
            dve.wait_ge(by_act, b + 2)
            link(dve, nc.vector.reciprocal(stat[1][:, :], stat[1][:, :]))
            link(dve, nc.vector.scalar_tensor_tensor(hs[:, :, :], hs[:, :, :], 0.0,
                                                     stat[1][:, :].unsqueeze(2).to_broadcast([P, WIN, D]), ALU.max, ALU.mult))

        @block.scalar
        def _(act):
            act.wait_ge(by_act, b + 1)
            nc.scalar.activation(stat[1][:, :], stat[1][:, :], ACT.Sqrt).then_inc(by_act, 1)
    k.since.passed(2, by_act)


def split_near(k, t):
    nc = k.nc
    with nc.Block() as block:
        @block.vector
        def _(dve):
            parts = [k.near[:, 0:WIN, i * D:(i + 1) * D] for i in range(3)]
            split3(nc, lambda ins: k.link(dve, ins), *parts, t[:, :, :], k.acc[:, 0:WIN, 0:D])


def publish(k, t, split):
    nc = k.nc
    if split:
        split_near(k, t)
    out = k.stored
    b = k.since(out)
    with nc.Block() as block:
        @block.sync
        def _(sp):
            if split:
                sp.dma_start(k.table3.rearrange("(w p) c -> p w c", p=P), k.near[:, :, :]).then_inc(out, 16)
                sp.wait_ge(out, b + 16)
            else:
                sp.dma_start(k.table[0:WIN * P, :].rearrange("(w p) c -> p w c", p=P), t[:, :, :]).then_inc(out, 16)
                sp.dma_start(k.table[WIN * P:WP * P, :], k.ones[:, :]).then_inc(out, 16)
                sp.wait_ge(out, b + 32)
    k.since.passed(16 if split else 32, out)


TILES = 7


def node_product(k, W, bias, src, dst, how, add=None):
    assert WIN % TILES == 0
    nc, n = k.nc, TILES * D
    staged, turned, turned_sb, multiplied, epilogued = (k.stage[x] for x in ("staged", "turned", "turned_sb", "multiplied", "epilogued"))
    s, t, ts, m, e = (k.since(x) for x in (staged, turned, turned_sb, multiplied, epilogued))
    all_banks = k.banks[:, :, :].rearrange("p b c -> p (b c)")
    w_sb = k.weights[W][0]
    row = k.rows[bias][0] if bias else None
    turns = WIN // TILES
    with nc.Block() as block:
        @block.vector
        def _(dve):
            dve.sem_inc(epilogued, 1)
            with dve.Fori(0, turns) as i:
                win = bass.ds(i * TILES, TILES)
                st = k.staging[:, :].rearrange("p (w d) -> p w d", d=D)
                dve.wait_ge(epilogued, e + 1 + i * 2)
                if add is None:
                    nc.vector.tensor_scalar(st, src[:, win, 0:D], 1.0, None, ALU.mult).then_inc(staged, 1)
                else:
                    nc.vector.tensor_tensor(st, src[:, win, 0:D], add[:, win, 0:D], ALU.add).then_inc(staged, 1)
                ps = all_banks[:, 1024:1024 + n].rearrange("p (w d) -> p w d", d=D)
                dve.wait_ge(multiplied, m + i + 1)
                if how == "relu":
                    nc.vector.tensor_scalar(dst[:, win, :], ps, 0.0, None, ALU.max).then_inc(epilogued, 2)
                elif how == "copy":
                    nc.vector.tensor_scalar(dst[:, win, :], ps, 1.0, None, ALU.mult).then_inc(epilogued, 2)
                elif how == "add":
                    nc.vector.tensor_tensor(dst[:, win, :], ps, dst[:, win, :], ALU.add).then_inc(epilogued, 2)
                else:
                    nc.vector.tensor_scalar(st, ps, 0.2, None, ALU.mult).then_inc(epilogued, 1)
                    dve.wait_ge(epilogued, e + i * 2 + 2)
                    nc.vector.tensor_tensor(st, st, ps, ALU.max).then_inc(k.stage["bulk_pe"], 1)
                    dve.wait_ge(k.stage["bulk_pe"], k.since(k.stage["bulk_pe"]) + i + 1)
                    nc.vector.tensor_tensor(dst[:, win, :], st, dst[:, win, :], ALU.add).then_inc(epilogued, 1)
            dve.wait_ge(epilogued, e + 1 + 2 * turns)

        @block.tensor
        def _(pe):
            with pe.Fori(0, turns) as i:
                pe.wait_ge(staged, s + i + 1)
                for w in range(TILES):
                    last = nc.tensor.transpose(all_banks[:, w * D:(w + 1) * D], k.staging[:, w * D:(w + 1) * D], k.ident[:, :])
                last.then_inc(turned, 1)
                pe.wait_ge(turned_sb, ts + i + 1)
                for w in range(TILES):
                    o = all_banks[:, 1024 + w * D:1024 + (w + 1) * D]
                    last = nc.tensor.matmul(o, k.staging_t[:, w * D:(w + 1) * D], w_sb[:, :], start=True, stop=row is None)
                    if row is not None:
                        last = nc.tensor.matmul(o, k.ones[0:1, :], row[:, :], start=False, stop=True)
                last.then_inc(multiplied, 1)

        @block.scalar
        def _(act):
            with act.Fori(0, turns) as i:
                act.wait_ge(turned, t + i + 1)
                nc.scalar.activation(k.staging_t[:, :], all_banks[:, 0:n], ACT.Copy).then_inc(turned_sb, 1)
    k.since.passed(turns, staged, turned, turned_sb, multiplied)
    k.since.passed(2 * turns + 1, epilogued)
    if how == "leaky":
        k.since.passed(turns, k.stage["bulk_pe"])


def shifted_softplus(k):
    nc, link, hs = k.nc, k.link, k.hs
    soft = k.acc[:, 0:WIN, 0:D]
    by_act = k.stage["bulk_act"]
    b = k.since(by_act)
    with nc.Block() as block:
        @block.scalar
        def _(act):
            nc.scalar.activation(soft, hs[:, :, :], ACT.Abs).then_inc(by_act, 1)
            act.wait_ge(by_act, b + 1)
            nc.scalar.activation(soft, soft, ACT.Exp, scale=-1.0).then_inc(by_act, 1)
            act.wait_ge(by_act, b + 2)
            nc.scalar.activation(soft, soft, ACT.Ln, bias=1.0).then_inc(by_act, 1)

        @block.vector
        def _(dve):
            dve.wait_ge(by_act, b + 3)
            link(dve, nc.vector.tensor_scalar(hs[:, :, :], hs[:, :, :], 0.0, -LOG2, ALU.max, ALU.add))
            link(dve, nc.vector.tensor_tensor(hs[:, :, :], hs[:, :, :], soft, ALU.add))
    k.since.passed(3, by_act)



def skewed(eng, *stages):
    most = max(lead for lead, _ in stages)
    for n in range(-most, 0):
        for lead, stage in stages:
            if n + lead >= 0:
                stage(0, n + lead)
    with eng.Fori(0, NG, U) as g:
        for u in range(U):
            for lead, stage in stages:
                stage(g, u + lead)


def landed(g, ahead, each=16):
    return g * (each // U) + (ahead // U + 1) * each


def per_slot(since, sems, each, lead):
    for u, sem in enumerate(sems):
        since.passed(each * (NG // U + (u < lead)), sem)


def window(eng, k, o, g):
    return bass.ds(eng.value_load(k.glist[o][0:1, 0, bass.ds(g, 1)], min_val=0, max_val=WIN), 1)


def first_edge(eng, k, o, g):
    return eng.value_load(k.glist[o][0:1, 1, bass.ds(g, 1)], min_val=0, max_val=EDGES)


def segment_sums(k, o):
    nc, st = k.nc, k.stage
    rel_ready, onehot_ready, summed, added = (st[x] for x in ("rel_ready", "onehot_ready", "summed", "added"))
    width, key = (RW, C_DST) if o == 0 else (MW, M_SRC)
    records = k.erec if o == 0 else k.mrec
    s_rel, s_hot, s_sum, s_add = (k.since(x) for x in (rel_ready, onehot_ready, summed, added))
    s_row, s_pool = [k.since(x) for x in k.rows_in], [k.since(x) for x in k.pool_done]
    lead = 1
    with ExitStack() as own:
        rows = k.sb(own, f"sum_rows{o}", [P, U, KG, width])
        rel = k.sb(own, f"sum_rel{o}", [P, U, KG])
        hot = k.sb(own, f"sum_hot{o}", [P, U, KG, P], BF16 if o == 0 else F32)
        far = k.sb(own, "sum_far", [P, U, KG, 3 * D], BF16) if o == 0 else None
        with nc.Block() as block:
            @block.sync
            def _(sp):
                def load(g, a):
                    sp.wait_ge(summed, s_sum + g + a + 1)
                    e0 = first_edge(sp, k, o, g + a)
                    sp.dma_start(rows[:, a % U, :, :].rearrange("p q c -> p (q c)"),
                                 records[bass.ds(e0, GE), :].rearrange("(p q) c -> p (q c)", q=KG))\
                        .then_inc(k.rows_in[a % U], 16)
                skewed(sp, (lead, load))

            if o == 0:
                @block.gpsimd
                def _(pool):
                    def gather(g, a):
                        pool.wait_ge(k.rows_in[a], s_row[a] + landed(g, a))
                        pool.wait_ge(summed, s_sum + g + a + 1)
                        pool.sem_inc(k.begun, 1)
                        for q in range(KG):
                            pool.indirect_dma_start(
                                far[:, a, q, :], None, k.table3[:, :],
                                bass.IndirectOffsetOnAxis(ap=rows[:, a, q, C_SRC:C_SRC + 1].bitcast(I32), axis=0))\
                                .then_inc(k.pool_done[a], 16)
                    skewed(pool, (0, gather))

            @block.vector
            def _(dve):
                nc.vector.memset(k.acc[:, :, :], 0.0).then_inc(added, 2)

                def one_hot(g, a):
                    u = a % U
                    dve.wait_ge(k.rows_in[u], s_row[u] + landed(g, a))
                    dve.wait_ge(summed, s_sum + g + a + 1)
                    nc.vector.tensor_scalar(rel[:, u, :], rows[:, u, :, key].bitcast(I32), k.gbase[o][:, bass.ds(g + a, 1)],
                                            None, ALU.subtract).then_inc(rel_ready, 1)
                    dve.wait_ge(rel_ready, s_rel + g + a + 1)
                    for q in range(KG):
                        last = nc.vector.tensor_scalar(hot[:, u, q, :], k.iota_b[:, :], rel[:, u, q:q + 1], None, ALU.is_equal)
                    last.then_inc(onehot_ready, 1)

                def add(g, a):
                    w = window(dve, k, o, g + a)
                    dve.wait_ge(summed, s_sum + U + g + a + 1)
                    dve.wait_ge(added, s_add + 2 + g + a)
                    nc.vector.tensor_tensor(k.acc[:, w, 0:D], k.psum[a % 2][:, 0:D].unsqueeze(1), k.acc[:, w, 0:D],
                                            ALU.add).then_inc(added, 1)
                skewed(dve, (lead, one_hot), (0, add))

            @block.tensor
            def _(pe):
                pe.sem_inc(summed, U)

                def total(g, a):
                    pe.wait_ge(onehot_ready, s_hot + g + a + 1)
                    pe.wait_ge(added, s_add + g + a + 1)
                    if o == 0:
                        pe.wait_ge(k.pool_done[a], s_pool[a] + landed(g, a, 16 * KG))
                    for q in range(KG):
                        for part in range(3 if o == 0 else 1):
                            rhs = far[:, a, q, part * D:(part + 1) * D] if o == 0 else rows[:, a, q, 0:D]
                            last = nc.tensor.matmul(k.psum[a % 2][:, 0:D], hot[:, a, q, :], rhs,
                                                    start=q == 0 and part == 0, stop=q == KG - 1 and part == (2 if o == 0 else 0))
                    last.then_inc(summed, 1)
                skewed(pe, (0, total))
    k.since.passed(NG + lead, rel_ready, onehot_ready)
    k.since.passed(NG + U, summed)
    k.since.passed(NG + 2, added)
    per_slot(k.since, k.rows_in, 16, lead)
    if o == 0:
        per_slot(k.since, k.pool_done, 16 * KG, 0)


def filter_messages(k):
    nc, st = k.nc, k.stage
    names = ("rel_ready", "onehot_ready", "onehot_turned", "onehotT_ready", "attr_turned", "attrT_ready", "hidden_ready",
             "soft1", "soft2", "soft3", "soft4", "soft_ready", "filter_ready", "far_ready", "biased", "index_ready",
             "message_ready")
    (rel_ready, onehot_ready, onehot_turned, onehotT_ready, attr_turned, attrT_ready, hidden_ready, soft1, soft2, soft3,
     soft4, soft_ready, filter_ready, far_ready, biased, index_ready, message_ready) = (st[x] for x in names)
    at = {st[x].name: k.since(st[x]) for x in names}
    s_row, s_pool = [k.since(x) for x in k.rows_in], [k.since(x) for x in k.pool_done]
    w_f2, b_f2 = k.weights["W_f2"][0], k.wide["b_f2"][0]
    pads = EP - EDGES
    with ExitStack() as own:
        sb = lambda name, shape, dt=F32: k.sb(own, name, shape, dt)
        rows, pos = sb("f_rows", [P, U, KG, RW]), sb("f_pos", [P, U, KG], I32)
        rel, hot = sb("f_rel", [P, U, KG]), sb("f_hot", [P, U, KG, P], BF16)
        hot_t, attr_t = sb("f_hot_t", [P, U, GE], BF16), sb("f_attr_t", [RBF, 2, GE])
        soft, sp_t = sb("f_soft", [P, 2, GE]), sb("f_sp", [P, 2, GE])
        tmp, index, off = sb("f_tmp", [P, KG, D]), sb("f_index", [P, U, KG], I32), sb("f_off", [P, KG])
        msg = sb("f_msg", [P, U, KG, MW])
        pad = sb("f_pad", [pads // 8, 8, MW])
        pad_i = pad[:, :, :].bitcast(I32)
        hot_ps = k.psum[0].bitcast(BF16)[:, 0:GE]
        attr_ps = k.psum[1][0:RBF, :]
        hidden_ps, far_ps, filter_ps = k.psum[2:4], k.psum[4:6], k.psum[6:8]
        padded = k.sem("padded")

        with nc.Block() as block:
            @block.sync
            def _(sp):
                sp.wait_ge(padded, 2)
                sp.dma_start(k.mrec[EDGES:EP, :].rearrange("(p j) c -> p j c", j=8), pad[:, :, :]).then_inc(padded, 16)

                def load(g, a):
                    u = a % U
                    sp.wait_ge(message_ready, at[message_ready.name] + g + a + 1)
                    e0 = first_edge(sp, k, 0, g + a)
                    sp.dma_start(rows[:, u, :, :].rearrange("p q c -> p (q c)"),
                                 k.erec[bass.ds(e0, GE), :].rearrange("(p q) c -> p (q c)", q=KG)).then_inc(k.rows_in[u], 16)
                    sp.dma_start(pos[:, u, :], k.epos[bass.ds(e0, GE), :].rearrange("(p q) c -> p (q c)", q=KG))\
                        .then_inc(k.rows_in[u], 16)
                skewed(sp, (3, load))
                sp.wait_ge(padded, 18)

            @block.gpsimd
            def _(pool):
                def scatter(g, a):
                    pool.wait_ge(message_ready, at[message_ready.name] + U + g + a + 1)
                    pool.sem_inc(k.begun, 1)
                    for q in range(KG):
                        pool.indirect_dma_start(
                            k.mrec[:, :], bass.IndirectOffsetOnAxis(ap=index[:, a, q:q + 1], axis=0), msg[:, a, q, :], None,
                            bounds_check=EDGES - 1, oob_is_err=False).then_inc(k.pool_done[a], 16)
                skewed(pool, (0, scatter))
                for u in range(U):
                    pool.wait_ge(k.pool_done[u], s_pool[u] + 16 * KG * NG // U)

            @block.vector
            def _(dve):
                nc.vector.memset(pad[:, :, :], 0.0).then_inc(padded, 1)
                dve.wait_ge(padded, 1)
                nc.vector.memset(pad_i[:, :, M_SRC:M_SRC + 1], NOWHERE).then_inc(padded, 1)
                nc.vector.memset(msg[:, :, :, :], 0.0).then_inc(message_ready, U)
                dve.wait_ge(message_ready, at[message_ready.name] + U)
                dve.sem_inc(soft_ready, 2)
                dve.sem_inc(index_ready, 1)

                def one_hot(g, a):
                    u = a % U
                    dve.wait_ge(k.rows_in[u], s_row[u] + landed(g, a, 32))
                    nc.vector.tensor_scalar(rel[:, u, :], rows[:, u, :, C_DST].bitcast(I32), k.gbase[0][:, bass.ds(g + a, 1)],
                                            None, ALU.subtract).then_inc(rel_ready, 1)
                    dve.wait_ge(rel_ready, at[rel_ready.name] + g + a + 1)
                    for q in range(KG):
                        last = nc.vector.tensor_scalar(hot[:, u, q, :], k.iota_b[:, :], rel[:, u, q:q + 1], None, ALU.is_equal)
                    last.then_inc(onehot_ready, 1)

                def softplus(g, a):
                    b = a % 2
                    dve.wait_ge(soft1, at[soft1.name] + g + a + 1)
                    nc.vector.tensor_scalar(sp_t[:, b, :], hidden_ps[b], k.bf1[:, :], 0.0, ALU.add, ALU.max).then_inc(soft4, 1)
                    dve.wait_ge(soft4, at[soft4.name] + g + a + 1)
                    dve.wait_ge(soft3, at[soft3.name] + g + a + 1)
                    nc.vector.scalar_tensor_tensor(sp_t[:, b, :], sp_t[:, b, :], -LOG2, soft[:, b, :], ALU.add, ALU.add)\
                        .then_inc(soft_ready, 1)

                def message(g, a):
                    u, b = a % U, a % 2
                    dve.wait_ge(index_ready, at[index_ready.name] + 1 + 2 * (g + a))
                    nc.vector.tensor_scalar(off[:, :], rel[:, u, :], float(P), FAR, ALU.is_ge, ALU.mult).then_inc(index_ready, 1)
                    dve.wait_ge(index_ready, at[index_ready.name] + 2 * (g + a) + 2)
                    dve.wait_ge(k.pool_done[u], s_pool[u] + landed(g, a, 16 * KG) - 16 * KG)
                    nc.vector.tensor_tensor(index[:, u, :], off[:, :], pos[:, u, :], ALU.add).then_inc(index_ready, 1)
                    nc.vector.tensor_copy(msg[:, u, :, M_SRC:M_SRC + 3].bitcast(I32), rows[:, u, :, C_SRC:C_SRC + 3].bitcast(I32))
                    dve.wait_ge(filter_ready, at[filter_ready.name] + g + a + 1)
                    dve.wait_ge(message_ready, at[message_ready.name] + U + g + a)
                    nc.vector.tensor_tensor(tmp[:, :, :], filter_ps[b].rearrange("p (q d) -> p q d", d=D),
                                            b_f2[:, :].unsqueeze(1).to_broadcast([P, KG, D]), ALU.add).then_inc(biased, 1)
                    dve.wait_ge(biased, at[biased.name] + g + a + 1)
                    dve.wait_ge(far_ready, at[far_ready.name] + g + a + 1)
                    for q in range(KG):
                        last = nc.vector.scalar_tensor_tensor(msg[:, u, q, 0:D], tmp[:, q, :], rows[:, u, q, C_WT:C_WT + 1],
                                                              far_ps[b][:, q * D:(q + 1) * D], ALU.mult, ALU.mult)
                    last.then_inc(message_ready, 1)
                skewed(dve, (1, softplus), (3, one_hot), (0, message))

            @block.scalar
            def _(act):
                act.sem_inc(onehotT_ready, 1)
                act.sem_inc(attrT_ready, 1)

                def turn(g, a):
                    u, b = a % U, a % 2
                    act.wait_ge(onehot_turned, at[onehot_turned.name] + g + a + 1)
                    nc.scalar.activation(hot_t[:, u, :], hot_ps, ACT.Copy).then_inc(onehotT_ready, 1)
                    act.wait_ge(attr_turned, at[attr_turned.name] + g + a + 1)
                    nc.scalar.activation(attr_t[:, b, :], attr_ps, ACT.Copy).then_inc(attrT_ready, 1)

                def soften(g, a):
                    b = a % 2
                    act.wait_ge(hidden_ready, at[hidden_ready.name] + g + a + 1)
                    nc.scalar.activation(soft[:, b, :], hidden_ps[b], ACT.Abs, bias=k.bf1[:, :]).then_inc(soft1, 1)
                    act.wait_ge(soft1, at[soft1.name] + g + a + 1)
                    nc.scalar.activation(soft[:, b, :], soft[:, b, :], ACT.Exp, scale=-1.0).then_inc(soft2, 1)
                    act.wait_ge(soft2, at[soft2.name] + g + a + 1)
                    nc.scalar.activation(soft[:, b, :], soft[:, b, :], ACT.Ln, bias=1.0).then_inc(soft3, 1)
                skewed(act, (3, turn), (2, soften))

            @block.tensor
            def _(pe):
                def turn(g, a):
                    u = a % U
                    pe.wait_ge(onehot_ready, at[onehot_ready.name] + g + a + 1)
                    pe.wait_ge(onehotT_ready, at[onehotT_ready.name] + g + a + 1)
                    for q in range(KG):
                        last = nc.tensor.transpose(hot_ps[:, q * P:(q + 1) * P], hot[:, u, q, :], k.ident_b[:, :])
                    last.then_inc(onehot_turned, 1)
                    pe.wait_ge(attrT_ready, at[attrT_ready.name] + g + a + 1)
                    for q in range(KG):
                        last = nc.tensor.transpose(attr_ps[:, q * P:(q + 1) * P], rows[:, u, q, 0:RBF], k.ident[:, :])
                    last.then_inc(attr_turned, 1)

                def filters(g, a):
                    b = a % 2
                    pe.wait_ge(message_ready, at[message_ready.name] + U - 1 + g + a)
                    near_rows(pe, k, 0, g + a, far_ps[b], hot_t[:, a % U, :], onehotT_ready, at[onehotT_ready.name] + 1 + g + a + 1)\
                        .then_inc(far_ready, 1)
                    pe.wait_ge(soft_ready, at[soft_ready.name] + 2 + g + a + 1)
                    for q in range(KG):
                        last = nc.tensor.matmul(filter_ps[b][:, q * D:(q + 1) * D], sp_t[:, b, q * P:(q + 1) * P], w_f2[:, :],
                                                start=True, stop=True)
                    last.then_inc(filter_ready, 1)

                def hidden(g, a):
                    b = a % 2
                    pe.wait_ge(attrT_ready, at[attrT_ready.name] + 1 + g + a + 1)
                    pe.wait_ge(soft_ready, at[soft_ready.name] + g + a + 1)
                    nc.tensor.matmul(hidden_ps[b], k.w_f1[:, :], attr_t[:, b, :], start=True, stop=True).then_inc(hidden_ready, 1)
                skewed(pe, (2, hidden), (3, turn), (1, filters))
    since = k.since
    since.passed(NG + 2, hidden_ready, soft1, soft2, soft3)
    since.passed(NG + 3, rel_ready, onehot_ready, onehot_turned, attr_turned, soft_ready)
    since.passed(NG + 4, onehotT_ready, attrT_ready)
    since.passed(NG + 1, soft4, filter_ready, far_ready)
    since.passed(NG, biased)
    since.passed(2 * NG + 1, index_ready)
    since.passed(NG + U, message_ready)
    per_slot(since, k.rows_in, 32, 3)
    per_slot(since, k.pool_done, 16 * KG, 0)


def near_rows(pe, k, o, g, ps, hot_t, ready, value, stop=True):
    nc = k.nc
    w = window(pe, k, o, g)
    pe.wait_ge(ready, value)
    for q in range(KG):
        for part in range(3):
            last = nc.tensor.matmul(ps[:, q * D:(q + 1) * D], hot_t[:, q * P:(q + 1) * P], k.near[:, w, part * D:(part + 1) * D]
                                    .rearrange("p a d -> p (a d)"), start=part == 0, stop=stop and part == 2)
    return last


def attention(k, layer):
    nc, st, o = k.nc, k.stage, layer
    names = ("rel_ready", "onehot_ready", "onehot_turned", "onehotT_ready", "edge_term", "near_ready", "in1", "in2", "in3",
             "product", "summed_up", "scores", "spread", "group_max", "new_max", "exp_in", "max_kept", "weighed", "shrink",
             "prob_turned", "prob_ready", "summed", "added")
    (rel_ready, onehot_ready, onehot_turned, onehotT_ready, edge_term, near_ready, in1, in2, in3, product, summed_up, scores,
     spread, group_max, new_max, exp_in, max_kept, weighed, shrink, prob_turned, prob_ready, summed, added) = \
        (st[x] for x in names)
    base = {st[x].name: k.since(st[x]) for x in names}
    s_row, s_pool = [k.since(x) for x in k.rows_in], [k.since(x) for x in k.pool_done]
    at = lambda sem, n: base[sem.name] + n
    width, key, other = (RW, C_DST, C_SRC) if o == 0 else (MW, M_SRC, M_DST)
    records = k.erec if o == 0 else k.mrec
    HW = P if o == 0 else P + NTYPE
    We, att = k.wide["We"][0], k.wide["att"][0]
    XW = D + 4
    with ExitStack() as own:
        sb = lambda name, shape, dt=F32: k.sb(own, f"{name}{o}", shape, dt)
        rows, rel, hide = sb("a_rows", [P, U, KG, width]), sb("a_rel", [P, U, KG]), sb("a_hide", [P, U, KG])
        kind = sb("a_kind", [P, U, KG])
        hot, hot_t = sb("a_hot", [P, 2, KG, HW], BF16), sb("a_hot_t", [P, U, GE], BF16)
        kind_t = sb("a_kind_t", [NTYPE, 2, GE], BF16) if o else None
        far = sb("a_far", [P, U, KG, XW])
        term = sb("a_term", [P, 2, KG, D])
        work = sb("a_work", [P, KG, D])
        raw, score = sb("a_raw", [P, KG]), sb("a_score", [P, U, KG])
        gmax, nmax = sb("a_gmax", [P, 1]), sb("a_nmax", [P, 1])
        minus, fall, factor = sb("a_minus", [P, 2]), sb("a_fall", [P, 2]), sb("a_factor", [P, 2])
        prob_t, prob = sb("a_prob_t", [P, 2, GE]), sb("a_prob", [P, 2, GE])
        hot_ps = k.psum[0].bitcast(BF16)
        near_ps, spread_ps, prob_ps, sum_ps = k.psum[1:3], k.psum[3:5], k.psum[5], k.psum[6:8]

        with nc.Block() as block:
            @block.sync
            def _(sp):
                def load(g, a):
                    sp.wait_ge(summed, at(summed, g + a + 1))
                    e0 = first_edge(sp, k, o, g + a)
                    sp.dma_start(rows[:, a % U, :, :].rearrange("p q c -> p (q c)"),
                                 records[bass.ds(e0, GE), :].rearrange("(p q) c -> p (q c)", q=KG)).then_inc(k.rows_in[a % U], 16)
                skewed(sp, (3, load))

            @block.gpsimd
            def _(pool):
                def gather(g, a):
                    u = a % U
                    pool.wait_ge(k.rows_in[u], s_row[u] + landed(g, a))
                    pool.wait_ge(summed, at(summed, g + a + 1))
                    pool.sem_inc(k.begun, 1)
                    for q in range(KG):
                        pool.indirect_dma_start(
                            far[:, u, q, 0:D], None, k.table[:, :],
                            bass.IndirectOffsetOnAxis(ap=rows[:, u, q, other:other + 1].bitcast(I32), axis=0))\
                            .then_inc(k.pool_done[u], 16)
                skewed(pool, (3, gather))

            @block.vector
            def _(dve):
                nc.vector.memset(k.acc[:, :, :], 0.0)
                nc.vector.memset(far[:, :, :, :], 1.0)
                nc.vector.memset(k.top_score[:, :], LOW).then_inc(added, 2)
                dve.wait_ge(added, at(added, 2))
                dve.sem_inc(summed, U)
                dve.sem_inc(max_kept, 1)
                dve.sem_inc(scores, 2)

                def one_hot(g, a):
                    u, b, n = a % U, a % 2, g + a
                    dve.wait_ge(k.rows_in[u], s_row[u] + landed(g, a))
                    nc.vector.tensor_scalar(rel[:, u, :], rows[:, u, :, key].bitcast(I32), k.gbase[o][:, bass.ds(n, 1)],
                                            None, ALU.subtract).then_inc(rel_ready, 1)
                    if o:
                        nc.vector.tensor_copy(kind[:, u, :], rows[:, u, :, M_TYPE].bitcast(I32)).then_inc(rel_ready, 1)
                    dve.wait_ge(rel_ready, at(rel_ready, (1 + o) * (n + 1)))
                    dve.wait_ge(onehot_turned, at(onehot_turned, n + 1))
                    for q in range(KG):
                        last = nc.vector.tensor_scalar(hot[:, b, q, 0:P], k.iota_b[:, :], rel[:, u, q:q + 1], None, ALU.is_equal)
                        if o:
                            last = nc.vector.tensor_scalar(hot[:, b, q, P:HW], k.iota_b[:, 0:NTYPE], kind[:, u, q:q + 1], None,
                                                           ALU.is_equal)
                    nc.vector.tensor_scalar(hide[:, u, :], rel[:, u, :], float(P), -BIG, ALU.is_ge, ALU.mult).then_inc(onehot_ready, 1)

                def score_edges(g, a):
                    u, b, n = a % U, a % 2, g + a
                    dve.wait_ge(k.pool_done[u], s_pool[u] + landed(g, a, 16 * KG))
                    dve.wait_ge(scores, at(scores, 2 + n))
                    if o == 0:
                        dve.wait_ge(near_ready, at(near_ready, n + 1))
                        nc.vector.tensor_tensor(work[:, :, :], near_ps[b].rearrange("p (q d) -> p q d", d=D), far[:, u, :, 0:D],
                                                ALU.add).then_inc(in1, 1)
                        dve.wait_ge(in1, at(in1, n + 1))
                        dve.wait_ge(edge_term, at(edge_term, n + 1))
                        nc.vector.tensor_tensor(work[:, :, :], work[:, :, :], term[:, b, :, :], ALU.add).then_inc(in2, 1)
                        dve.wait_ge(in2, at(in2, n + 1))
                        nc.vector.scalar_tensor_tensor(work[:, :, :], work[:, :, :], 0.2, work[:, :, :], ALU.mult, ALU.max)\
                            .then_inc(in3, 1)
                        dve.wait_ge(in3, at(in3, n + 1))
                        nc.vector.tensor_tensor(work[:, :, :], work[:, :, :], att[:, :].unsqueeze(1).to_broadcast([P, KG, D]),
                                                ALU.mult).then_inc(product, 1)
                    else:
                        dve.wait_ge(edge_term, at(edge_term, n + 1))
                        nc.vector.tensor_tensor(work[:, :, :], term[:, b, :, :], far[:, u, :, 0:D], ALU.mult).then_inc(product, 1)
                    dve.wait_ge(product, at(product, n + 1))
                    nc.vector.tensor_reduce(raw[:, :], work[:, :, :], AX, ALU.add).then_inc(summed_up, 1)
                    dve.wait_ge(summed_up, at(summed_up, n + 1))
                    nc.vector.tensor_tensor(score[:, u, :], raw[:, :], hide[:, u, :], ALU.add).then_inc(scores, 1)

                def node_max(g, a):
                    b, n = a % 2, g + a
                    w = window(dve, k, o, n)
                    dve.wait_ge(spread, at(spread, n + 1))
                    dve.wait_ge(max_kept, at(max_kept, 1 + n))
                    nc.vector.tensor_reduce(gmax[:, :], spread_ps[b], AX, ALU.max).then_inc(group_max, 1)
                    dve.wait_ge(group_max, at(group_max, n + 1))
                    nc.vector.tensor_tensor(nmax[:, :], gmax[:, :], k.top_score[:, w], ALU.max).then_inc(new_max, 1)
                    dve.wait_ge(new_max, at(new_max, n + 1))
                    nc.vector.tensor_scalar(minus[:, b:b + 1], nmax[:, :], -1.0, None, ALU.mult)
                    nc.vector.tensor_tensor(fall[:, b:b + 1], k.top_score[:, w], nmax[:, :], ALU.subtract).then_inc(exp_in, 1)
                    dve.wait_ge(exp_in, at(exp_in, n + 1))
                    nc.vector.tensor_scalar(k.top_score[:, w], nmax[:, :], 1.0, None, ALU.mult).then_inc(max_kept, 1)

                def add(g, a):
                    b, n = a % 2, g + a
                    w = window(dve, k, o, n)
                    dve.wait_ge(summed, at(summed, U + n + 1))
                    dve.wait_ge(shrink, at(shrink, n + 1))
                    dve.wait_ge(added, at(added, 2 + n))
                    nc.vector.scalar_tensor_tensor(k.acc[:, w, 0:D + 1], k.acc[:, w, 0:D + 1], factor[:, b:b + 1],
                                                   sum_ps[b][:, 0:D + 1].unsqueeze(1), ALU.mult, ALU.add).then_inc(added, 1)
                skewed(dve, (3, one_hot), (1, node_max), (2, score_edges), (0, add))

            @block.scalar
            def _(act):
                act.sem_inc(onehotT_ready, 1)

                def take_prob(g, a):
                    b, n = a % 2, g + a
                    act.wait_ge(prob_turned, at(prob_turned, n + 1))
                    act.wait_ge(summed, at(summed, U - 1 + n))
                    nc.scalar.activation(prob[:, b, :], prob_ps, ACT.Copy).then_inc(prob_ready, 1)

                def turn(g, a):
                    u, b, n = a % U, a % 2, g + a
                    act.wait_ge(onehot_turned, at(onehot_turned, 2 + n + 1))
                    if o:
                        nc.scalar.activation(kind_t[:, b, :], hot_ps[0:NTYPE, GE:2 * GE], ACT.Copy)
                    nc.scalar.activation(hot_t[:, u, :], hot_ps[:, 0:GE], ACT.Copy).then_inc(onehotT_ready, 1)

                def weigh(g, a):
                    b, n = a % 2, g + a
                    act.wait_ge(exp_in, at(exp_in, n + 1))
                    nc.scalar.activation(prob_t[:, b, :], spread_ps[b], ACT.Exp, bias=minus[:, b:b + 1]).then_inc(weighed, 1)
                    act.wait_ge(added, at(added, n + 1))
                    nc.scalar.activation(factor[:, b:b + 1], fall[:, b:b + 1], ACT.Exp).then_inc(shrink, 1)

                def terms(g, a):
                    u, b, n = a % U, a % 2, g + a
                    act.wait_ge(scores, at(scores, n + 1))
                    if o == 0:
                        for q in range(KG):
                            last = nc.scalar.activation(term[:, b, q, :], We[:, :], ACT.Copy, scale=rows[:, u, q, C_WT:C_WT + 1])
                        last.then_inc(edge_term, 1)
                    else:
                        act.wait_ge(near_ready, at(near_ready, n + 1))
                        nc.scalar.activation(term[:, b, :, :], near_ps[b].rearrange("p (q d) -> p q d", d=D), ACT.Tanh)\
                            .then_inc(edge_term, 1)
                skewed(act, (0, take_prob), (3, turn), (1, weigh), (3, terms))

            @block.tensor
            def _(pe):
                pe.sem_inc(onehot_turned, 2)

                def spreads(g, a):
                    u, b, n = a % U, a % 2, g + a
                    pe.wait_ge(scores, at(scores, 2 + n + 1))
                    nc.tensor.matmul(spread_ps[b], k.apart_b[:, :], hot_t[:, u, :], start=True, stop=False, skip_group_check=True)
                    for q in range(KG):
                        last = nc.tensor.matmul(spread_ps[b][:, q * P:(q + 1) * P], score[:, u, q:q + 1].to_broadcast([P, P]),
                                                k.ident[:, :], start=False, stop=q == KG - 1, skip_group_check=True)
                    last.then_inc(spread, 1)

                def turn(g, a):
                    b, n = a % 2, g + a
                    pe.wait_ge(onehot_ready, at(onehot_ready, n + 1))
                    pe.wait_ge(onehotT_ready, at(onehotT_ready, n + 1))
                    for q in range(KG):
                        last = nc.tensor.transpose(hot_ps[:, q * P:(q + 1) * P], hot[:, b, q, 0:P], k.ident_b[:, :])
                        if o:
                            last = nc.tensor.transpose(hot_ps[0:NTYPE, GE + q * P:GE + (q + 1) * P], hot[:, b, q, P:HW],
                                                       k.ident_b[:, :])
                    last.then_inc(onehot_turned, 1)

                def sums(g, a):
                    u, b, n = a % U, a % 2, g + a
                    pe.wait_ge(prob_ready, at(prob_ready, n + 1))
                    pe.wait_ge(added, at(added, n + 1))
                    for q in range(KG):
                        last = nc.tensor.matmul(sum_ps[b][:, 0:D + 1], prob[:, b, q * P:(q + 1) * P], far[:, u, q, 0:D + 1],
                                                start=q == 0, stop=q == KG - 1)
                    last.then_inc(summed, 1)

                def rows_near(g, a):
                    u, b, n = a % U, a % 2, g + a
                    pe.wait_ge(scores, at(scores, n + 1))
                    if o == 0:
                        near_rows(pe, k, o, n, near_ps[b], hot_t[:, u, :], onehotT_ready, at(onehotT_ready, 1 + n + 1))\
                            .then_inc(near_ready, 1)
                        return
                    w = window(pe, k, o, n)
                    pe.wait_ge(onehotT_ready, at(onehotT_ready, 1 + n + 1))
                    for q in range(KG):
                        cols = slice(q * P, (q + 1) * P)
                        for part in range(3):
                            nc.tensor.matmul(near_ps[b][:, cols], hot_t[:, u, cols], k.near[:, w, part * D:(part + 1) * D]
                                             .rearrange("p a d -> p (a d)"), start=part == 0, stop=False)
                        for part in range(3):
                            last = nc.tensor.matmul(near_ps[b][:, cols], kind_t[:, b, cols], k.rel3[:, part * D:(part + 1) * D],
                                                    start=False, stop=part == 2)
                    last.then_inc(near_ready, 1)

                def turn_prob(g, a):
                    b, n = a % 2, g + a
                    pe.wait_ge(weighed, at(weighed, n + 1))
                    for q in range(KG):
                        last = nc.tensor.transpose(prob_ps[:, q * P:(q + 1) * P], prob_t[:, b, q * P:(q + 1) * P], k.ident[:, :])
                    last.then_inc(prob_turned, 1)
                skewed(pe, (1, spreads), (3, turn), (0, sums), (3, rows_near), (1, turn_prob))
    since = k.since
    since.passed((NG + 3) * (1 + o), rel_ready)
    since.passed(NG + 3, onehot_ready, near_ready, edge_term)
    since.passed(NG + 5, onehot_turned)
    since.passed(NG + 4, onehotT_ready, scores)
    if o == 0:
        since.passed(NG + 2, in1, in2, in3)
    since.passed(NG + 2, product, summed_up, added, max_kept)
    since.passed(NG + 1, spread, group_max, new_max, exp_in, weighed, shrink, prob_turned)
    since.passed(NG, prob_ready)
    since.passed(NG + U, summed)
    per_slot(since, k.rows_in, 16, 3)
    per_slot(since, k.pool_done, 16 * KG, 3)


def gat_output(k):
    nc, link, hs, acc, stat = k.nc, k.link, k.hs, k.acc, k.stat
    by_act, by_pe = k.stage["bulk_act"], k.stage["bulk_pe"]
    b, p = k.since(by_act), k.since(by_pe)
    full = [P, WIN, D]
    spread = lambda t: t.unsqueeze(1).to_broadcast(full)
    with ExitStack() as own:
        part, mean = k.sb(own, "bn_part", [P, D]), k.sb(own, "bn_mean", [P, D])
        scale = k.sb(own, "bn_scale", [P, D])
        with nc.Block() as block:
            @block.vector
            def _(dve):
                link(dve, nc.vector.tensor_scalar(stat[0][:, :], acc[:, 0:WIN, D], 1e-16, None, ALU.add))
                link(dve, nc.vector.reciprocal(stat[0][:, :], stat[0][:, :]))
                link(dve, nc.vector.tensor_tensor(acc[:, 0:WIN, 0:D], acc[:, 0:WIN, 0:D], stat[0][:, :].unsqueeze(2).to_broadcast(full), ALU.mult))
                link(dve, nc.vector.tensor_tensor(hs[:, :, :], hs[:, :, :], acc[:, 0:WIN, 0:D], ALU.add))
                nc.vector.tensor_tensor(hs[:, :, :], hs[:, :, :], spread(k.wide["bias_out"][0][:, :]), ALU.add).then_inc(by_act, 1)
                dve.wait_ge(by_act, b + 2)
                for i, t in enumerate((hs[:, :, :], acc[:, 0:WIN, 0:D])):
                    if i:
                        link(dve, nc.vector.tensor_tensor(t, hs[:, :, :], hs[:, :, :], ALU.mult))
                    link(dve, nc.vector.tensor_scalar(t[:, WIN - 1, :], t[:, WIN - 1, :], k.valid[:, :], None, ALU.mult))
                    nc.vector.tensor_reduce(part[:, :], t.rearrange("p w d -> p d w"), AX, ALU.add).then_inc(by_pe, 1)
                    dve.wait_ge(by_pe, p + 2 * i + 2)
                    if i == 0:
                        link(dve, nc.vector.tensor_scalar(mean[:, :], k.psum[0][:, 0:D], 1.0 / NODES, None, ALU.mult))
                        link(dve, nc.vector.tensor_tensor(hs[:, :, :], hs[:, :, :], spread(mean[:, :]), ALU.subtract))
                    else:
                        nc.vector.tensor_scalar(scale[:, :], k.psum[0][:, 0:D], 1.0 / NODES, 1e-5, ALU.mult, ALU.add).then_inc(by_act, 1)
                dve.wait_ge(by_act, b + 4)
                link(dve, nc.vector.reciprocal(scale[:, :], scale[:, :]))
                link(dve, nc.vector.tensor_tensor(scale[:, :], scale[:, :], k.wide["bn_g"][0][:, :], ALU.mult))
                link(dve, nc.vector.tensor_tensor(hs[:, :, :], hs[:, :, :], spread(scale[:, :]), ALU.mult))
                link(dve, nc.vector.tensor_tensor(hs[:, :, :], hs[:, :, :], spread(k.wide["bn_b"][0][:, :]), ALU.add))
                link(dve, nc.vector.tensor_tensor(k.xs[:, :, :], k.xs[:, :, :], hs[:, :, :], ALU.add))

            @block.scalar
            def _(act):
                act.wait_ge(by_act, b + 1)
                nc.scalar.activation(hs[:, :, :], hs[:, :, :], ACT.Gelu).then_inc(by_act, 1)
                act.wait_ge(by_act, b + 3)
                nc.scalar.activation(scale[:, :], scale[:, :], ACT.Sqrt).then_inc(by_act, 1)

            @block.tensor
            def _(pe):
                for i in range(2):
                    pe.wait_ge(by_pe, p + 2 * i + 1)
                    nc.tensor.matmul(k.psum[0][:, 0:D], k.ones[:, :], part[:, :], start=True, stop=True).then_inc(by_pe, 1)
    k.since.passed(4, by_act, by_pe)


def relation_output(k):
    nc, link, acc, stat = k.nc, k.link, k.acc, k.stat
    by_act, by_pe = k.stage["bulk_act"], k.stage["bulk_pe"]
    b, p = k.since(by_act), k.since(by_pe)
    full = [P, WIN, D]
    with ExitStack() as own:
        col, row, top = k.sb(own, "top_col", [P, 1]), k.sb(own, "top_row", [1, 1]), k.sb(own, "top_all", [P, 1])
        with nc.Block() as block:
            @block.vector
            def _(dve):
                nc.vector.tensor_reduce(col[:, :], k.top_score[:, 0:WIN], AX, ALU.max).then_inc(by_pe, 1)
                dve.wait_ge(by_pe, p + 2)
                nc.vector.tensor_reduce(row[:, :], k.psum[0][0:1, 0:P], AX, ALU.max).then_inc(by_pe, 1)
                dve.wait_ge(by_pe, p + 4)
                link(dve, nc.vector.tensor_scalar(top[:, :], k.psum[1][:, 0:1], -1.0, None, ALU.mult))
                nc.vector.tensor_scalar(stat[0][:, :], k.top_score[:, 0:WIN], top[:, :], 0.0, ALU.add, ALU.min).then_inc(by_act, 1)
                dve.wait_ge(by_act, b + 2)
                link(dve, nc.vector.tensor_tensor(stat[1][:, :], acc[:, 0:WIN, D], stat[0][:, :], ALU.mult))
                link(dve, nc.vector.tensor_scalar(stat[1][:, :], stat[1][:, :], 1e-10, None, ALU.add))
                link(dve, nc.vector.reciprocal(stat[1][:, :], stat[1][:, :]))
                link(dve, nc.vector.tensor_tensor(stat[1][:, :], stat[1][:, :], stat[0][:, :], ALU.mult))
                link(dve, nc.vector.tensor_tensor(acc[:, 0:WIN, 0:D], acc[:, 0:WIN, 0:D],
                                                  stat[1][:, :].unsqueeze(2).to_broadcast(full), ALU.mult))
                link(dve, nc.vector.tensor_tensor(k.hs[:, :, :], k.hs[:, :, :], acc[:, 0:WIN, 0:D], ALU.add))

            @block.scalar
            def _(act):
                act.wait_ge(by_act, b + 1)
                nc.scalar.activation(stat[0][:, :], stat[0][:, :], ACT.Exp).then_inc(by_act, 1)

            @block.tensor
            def _(pe):
                pe.wait_ge(by_pe, p + 1)
                nc.tensor.transpose(k.psum[0][0:1, 0:P], col[:, :], k.ident[:, :]).then_inc(by_pe, 1)
                pe.wait_ge(by_pe, p + 3)
                nc.tensor.matmul(k.psum[1][:, 0:1], k.ones[0:1, :], row[:, :], start=True, stop=True).then_inc(by_pe, 1)
    k.since.passed(2, by_act)
    k.since.passed(4, by_pe)


def store_nodes(k):
    nc, out = k.nc, k.stored
    b = k.since(out)
    with nc.Block() as block:
        @block.sync
        def _(sp):
            sp.dma_start(k.out[0:(WIN - 1) * P, :].rearrange("(w p) d -> p w d", p=P), k.xs[:, 0:WIN - 1, :]).then_inc(out, 16)
            sp.dma_start(k.out[(WIN - 1) * P:NODES, :], k.xs[0:LAST, WIN - 1, :]).then_inc(out, 16)
            sp.wait_ge(out, b + 32)
    k.since.passed(32, out)

_INS = ["x", "src", "dst", "edge_attr_20", "edge_type_64", "edge_weight1", "L0_gnn_W1", "L0_gnn_b1", "L0_gnn_W2",
        "L0_gnn_b2", "L1_gnn_W_in", "L1_gnn_W_f1", "L1_gnn_b_f1", "L1_gnn_W_f2", "L1_gnn_b_f2", "L1_gnn_W_o1",
        "L1_gnn_b_o1", "L1_gnn_W_o2", "L1_gnn_b_o2", "L2_gnn_Wl", "L2_gnn_bl", "L2_gnn_Wr", "L2_gnn_br", "L2_gnn_We",
        "L2_gnn_att", "L2_gnn_bias_out", "L2_gnn_bn_gamma", "L2_gnn_bn_beta", "L3_gnn_rel_embed_weight", "L3_gnn_W"]


def kernel(**inputs):
    import numpy as np
    import concourse.bacc as bacc
    from concourse.bass_utils import run_bass_kernel_spmd

    nc = bacc.Bacc("TRN2", target_bir_lowering=False, num_devices=1)
    arrays, args = {}, []
    for name in _INS:
        a = np.asarray(inputs[name])
        a = np.ascontiguousarray(a.T if name == "L3_gnn_W" else a)
        arrays["in_" + name] = a
        args.append(nc.dram_tensor("in_" + name, a.shape, mybir.dt.from_np(a.dtype), kind="ExternalInput").ap())
    args.append(nc.dram_tensor("out_nodes", (NODES, D), F32, kind="ExternalOutput").ap())
    program(nc, *args)
    r = run_bass_kernel_spmd(nc, [arrays], core_ids=[0])
    return r.results[0]["out_nodes"]
```

```python
from contextlib import ExitStack, nullcontext

import concourse.bass as bass
from concourse import mybir

F32 = mybir.dt.float32
BF16 = mybir.dt.bfloat16
I32 = mybir.dt.int32
ALU = mybir.AluOpType
ACT = mybir.ActivationFunctionType
AX = mybir.AxisListType.X

P = 128
NODES = 6250
D = 128
EDGES = 200000
RBF = 20
NTYPE = 64
LOG2 = 0.6931471805599453

WIN = (NODES + P - 1) // P
WP = WIN + 1
LAST = NODES - (WIN - 1) * P
KG = 4
GE = KG * P
U = 4
NG = (EDGES // GE + 1 + WIN + U - 1) // U * U
T = 10
NCH = (EDGES + GE + P * T - 1) // (P * T)
J = NCH * T
EP = P * J
JC = J // 5
FULL = EDGES // J
REST = EDGES - FULL * J
RW = 24
C_WT, C_SRC, C_DST, C_TYPE = 20, 21, 22, 23
MW = 132
M_SRC, M_DST, M_TYPE = 128, 129, 130
NOWHERE = WP * P
BIG = 2.0 ** 100
LOW = -(2.0 ** 90)
FAR = float(1 << 22)
NL = NG + 3 * U
LOADS = 6
CREDIT = 8
GP = NL // KG


class Since:

    def __init__(self):
        self.counts = {}

    def __call__(self, sem):
        return self.counts.get(sem.name, 0)

    def cleared(self, sems):
        for sem in sems:
            self.counts[sem.name] = 0

    def passed(self, n, *sems):
        for sem in sems:
            self.counts[sem.name] = self(sem) + n


def flat(ap):
    return ap.rearrange("p a b -> p (a b)")


def program(nc, x, src, dst, attr, etype, weight, W1, b1, W2, b2, W_in, W_f1, b_f1, W_f2, b_f2,
            W_o1, b_o1, W_o2, b_o2, Wl, bl, Wr, br, We, att, bias_out, bn_g, bn_b, rel, WT3, out):
    since = Since()
    top = ExitStack()

    def sb(stack, name, shape, dt=F32):
        return stack.enter_context(nc.sbuf_tensor(name, shape, dt))

    def pb(stack, name, shape, dt=F32):
        return stack.enter_context(nc.psum_tensor(name, shape, dt))

    def sem(name, stack=top):
        return stack.enter_context(nc.semaphore(name))

    def dram(name, shape, dt=F32):
        return nc.dram_tensor(name, shape, dt, kind="Internal").ap()

    with top:
        erec = dram("edge_records", [2 * EP, RW])
        epos = dram("edge_positions", [2 * EP, 1], I32)
        tpos = dram("target_positions", [EP, 1], I32)
        mrec = dram("message_records", [EP, MW])
        table3 = dram("split_table", [WP * P, 3 * D], BF16)
        table = dram("node_table", [WP * P, D])
        lists = dram("group_lists", [2, 2, NL], I32)
        bases = dram("group_bases", [2, NL])

        iota_b = sb(top, "iota_b", [P, P], BF16)
        iota_w = sb(top, "iota_w", [P, WP], BF16)
        iota_i = sb(top, "iota_i", [P, P], I32)
        ident = sb(top, "ident", [P, P])
        ident_b = sb(top, "ident_b", [P, P], BF16)
        apart_b = sb(top, "apart_b", [P, P], BF16)
        before_b = sb(top, "before_b", [P, P], BF16)
        ones = sb(top, "ones", [P, P])
        ones_b = sb(top, "ones_b", [P, P], BF16)
        glist = [sb(top, f"glist{o}", [1, 2, NL], I32) for o in range(2)]
        gbase = [sb(top, f"gbase{o}", [P, NL]) for o in range(2)]
        gsame = [sb(top, f"gsame{o}", [P, NL]) for o in range(2)]
        gfresh = [sb(top, f"gfresh{o}", [P, NL]) for o in range(2)]
        weights = {}
        for name, w in dict(W1=W1, W2=W2, W_in=W_in, W_f2=W_f2, W_o1=W_o1, W_o2=W_o2, Wl=Wl, Wr=Wr,
                            WT3=WT3).items():
            weights[name] = sb(top, "w_" + name, [P, D]), w
        w_f1 = sb(top, "w_f1", [RBF, D])
        rows = {}
        for name, b in dict(b1=b1, b2=b2, b_o1=b_o1, b_o2=b_o2, bl=bl, br=br).items():
            rows[name] = sb(top, "row_" + name, [1, D]), b
        wide = {}
        for name, b in dict(b_f2=b_f2, We=We, att=att, bias_out=bias_out, bn_g=bn_g, bn_b=bn_b).items():
            wide[name] = sb(top, "wide_" + name, [P, D]), b
        bf1 = sb(top, "bf1", [P, 1])
        rel_f = sb(top, "rel_f", [NTYPE, D])
        rel3 = sb(top, "rel3", [NTYPE, 3 * D], BF16)
        relr = sb(top, "relr", [NTYPE, D])

        loaded, made, cast, chain, stored = (sem(n) for n in ("loaded", "made", "cast", "chain", "stored"))
        linked = [0]

        def link(eng, ins):
            linked[0] += 1
            ins.then_inc(chain, 1)
            eng.wait_ge(chain, linked[0])

        n_loads = len(weights) + len(rows) + len(wide) + 3
        with nc.Block() as block:
            @block.sync
            def _(sp):
                for t, w in weights.values():
                    sp.dma_start(t[:, :], w).then_inc(loaded, 16)
                for t, b in rows.values():
                    sp.dma_start(t[:, :], b.rearrange("(a n) -> a n", a=1)).then_inc(loaded, 16)
                for t, b in wide.values():
                    b = b if len(b.shape) == 2 else b.rearrange("(a n) -> a n", a=1)
                    sp.dma_start(t[:, :], b.broadcast_to([P, D])).then_inc(loaded, 16)
                sp.dma_start(w_f1[:, :], W_f1).then_inc(loaded, 16)
                sp.dma_start(bf1[:, :], b_f1.rearrange("(n a) -> n a", a=1)).then_inc(loaded, 16)
                sp.dma_start(rel_f[:, :], rel).then_inc(loaded, 16)
                sp.wait_ge(loaded, 16 * n_loads)

            @block.gpsimd
            def _(pool):
                pool.iota(iota_i[:, :], pattern=[[1, P]], base=0, channel_multiplier=0).then_inc(made, 1)
                pool.memset(ident[:, :], 0.0).then_inc(made, 1)
                pool.memset(before_b[:, :], 1.0).then_inc(made, 1)
                pool.wait_ge(made, 3)
                pool.affine_select(out=ident[:, :], in_=ident[:, :], compare_op=ALU.not_equal, fill=1.0,
                                   base=0, pattern=[[-1, P]], channel_multiplier=1).then_inc(made, 1)
                pool.affine_select(out=before_b[:, :], in_=before_b[:, :], compare_op=ALU.is_ge, fill=0.0,
                                   base=-1, pattern=[[1, P]], channel_multiplier=-1).then_inc(made, 1)

            @block.vector
            def _(dve):
                dve.wait_ge(made, 5)
                nc.vector.tensor_copy(iota_b[:, :], iota_i[:, :]).then_inc(cast, 1)
                nc.vector.tensor_copy(iota_w[:, :], iota_i[:, 0:WP]).then_inc(cast, 1)
                nc.vector.tensor_copy(ident_b[:, :], ident[:, :]).then_inc(cast, 1)
                nc.vector.tensor_scalar(apart_b[:, :], ident[:, :], BIG, -BIG, ALU.mult, ALU.add).then_inc(cast, 1)
                nc.vector.memset(ones[:, :], 1.0).then_inc(cast, 1)
                nc.vector.memset(ones_b[:, :], 1.0).then_inc(cast, 1)
                dve.wait_ge(loaded, 16 * n_loads)
                split3(nc, lambda ins: link(dve, ins), rel3[:, 0:D], rel3[:, D:2 * D], rel3[:, 2 * D:3 * D],
                       rel_f[:, :], relr[:, :])

        k = Kit()
        k.nc, k.since, k.link, k.chain, k.linked, k.sem, k.sb, k.pb = nc, since, link, chain, linked, sem, sb, pb
        k.x, k.out = x, out
        k.src, k.dst, k.attr, k.etype, k.weight = src, dst, attr, etype, weight
        k.erec, k.epos, k.tpos, k.mrec, k.table3, k.table, k.lists, k.bases = erec, epos, tpos, mrec, table3, table, lists, bases
        k.iota_b, k.iota_w, k.ident, k.ident_b, k.apart_b = iota_b, iota_w, ident, ident_b, apart_b
        k.before_b, k.ones, k.ones_b, k.glist, k.gbase = before_b, ones, ones_b, glist, gbase
        k.gsame, k.gfresh = gsame, gfresh
        k.weights, k.rows, k.wide, k.w_f1, k.bf1, k.rel3 = weights, rows, wide, w_f1, bf1, rel3
        k.banks = pb(top, "banks", [P, 8, 512])
        k.psum = [k.banks[:, i, :] for i in range(8)]
        pack_edges(k)
        k.xs = sb(top, "xs", [P, WIN, D])
        k.hs = sb(top, "hs", [P, WIN, D])
        k.acc = sb(top, "acc", [P, WP, MW])
        k.near = sb(top, "near", [P, WP, 3 * D], BF16)
        k.staging, k.staging_t = sb(top, "staging", [P, TILES * D]), sb(top, "staging_t", [P, TILES * D])
        k.stat = [sb(top, f"stat{i}", [P, WIN]) for i in range(2)]
        k.top, k.stored, k.begun, k.loading = top, stored, sem("begun"), sem("loading")
        k.stage = {n: sem(n) for n in (
            "staged", "turned", "turned_sb", "multiplied", "epilogued", "bulk_act", "bulk_pe",
            "rel_ready", "onehot_ready", "onehot_turned", "onehotT_ready", "summed", "added", "row_used",
            "attr_turned", "attrT_ready", "hidden_ready", "soft1", "soft2", "soft3", "soft4", "soft_ready",
            "filter_ready", "far_ready", "biased", "message_ready", "index_ready", "meta_ready",
            "edge_term", "near_ready", "in1", "in2", "in3", "edge_dot", "scores", "spread", "group_max", "kinds_ready", "kept",
            "exp_in", "weighed", "shrink", "prob_turned", "prob_ready")}
        k.rows_in = [sem(f"rows_in{u}") for u in range(U)]
        k.pool_done = [sem(f"pool_done{u}") for u in range(U)]

        load_nodes(k)
        layernorm_relu(k)
        publish(k, k.hs, True)
        segment_sums(k, 0)
        node_product(k, "W1", "b1", k.hs, k.hs, "relu", add=k.acc)
        node_product(k, "W2", "b2", k.hs, k.xs, "add")

        layernorm_relu(k)
        node_product(k, "W_in", None, k.hs, k.hs, "copy")
        split_near(k, k.hs)
        filter_messages(k)
        segment_sums(k, 1)
        node_product(k, "W_o1", "b_o1", k.acc, k.hs, "copy")
        shifted_softplus(k)
        node_product(k, "W_o2", "b_o2", k.hs, k.xs, "add")

        layernorm_relu(k)
        with nc.sbuf_tensor("right", [P, WIN, D], F32) as right:
            node_product(k, "Wl", "bl", k.hs, right, "copy")
            publish(k, right, False)
            node_product(k, "Wr", "br", k.hs, right, "copy")
            split_near(k, right)
        clear(k)
        attention(k, 0)
        clear(k)
        gat_output(k)

        layernorm_relu(k)
        publish(k, k.hs, False)
        split_near(k, k.hs)
        clear(k)
        attention(k, 1)
        relation_output(k)
        node_product(k, "WT3", None, k.hs, k.xs, "leaky")
        store_nodes(k)


class Kit:
    pass


def split3(nc, link, hi, mid, lo, source, rest):
    link(nc.vector.tensor_copy(hi, source))
    link(nc.vector.tensor_tensor(rest, source, hi, ALU.subtract))
    link(nc.vector.tensor_copy(mid, rest))
    link(nc.vector.tensor_tensor(rest, rest, mid, ALU.subtract))
    link(nc.vector.tensor_copy(lo, rest))


def pack_edges(k):
    nc, link, sem, sb = k.nc, k.link, k.sem, k.sb
    with ExitStack() as own:
        ends = [sb(own, n, [P, J], I32) for n in ("e_src", "e_dst", "e_type")]
        e_wt = sb(own, "e_wt", [P, J])
        win_i = sb(own, "win_i", [P, J], I32)
        win = [sb(own, f"win{o}", [P, J + 2 * T], BF16) for o in range(2)]
        at = sb(own, "at", [P, 2, JC * RBF])
        rec = sb(own, "rec", [P, 2, JC * RW])
        cleared, ends_in, packed = sem("cleared"), sem("ends_in"), sem("packed")
        attr_in = [sem(f"attr_in{s}") for s in range(2)]
        rec_out = [sem(f"rec_out{s}") for s in range(2)]
        pads = (WIN * P, NOWHERE, 0)
        nchunk = J // JC

        def split_pad(t, view, width, c0, n):
            pairs = [(t[0:FULL, 0:n * width], view[0:FULL * J * width]
                      .rearrange("(p j) -> p j", p=FULL)[:, c0 * width:(c0 + n) * width])]
            m = max(0, min(n, REST - c0))
            if m:
                lo = (FULL * J + c0) * width
                pairs.append((t[FULL:FULL + 1, 0:m * width],
                              view[lo:lo + m * width].rearrange("(a j) -> a j", a=1)))
            return pairs

        flats = [k.src, k.dst, k.etype]
        attr_flat = k.attr.rearrange("e r -> (e r)")
        n_ends = len(split_pad(e_wt, k.weight.rearrange("e a -> (e a)"), 1, 0, J)) * 4

        with nc.Block() as block:
            @block.sync
            def _(sp):
                sp.wait_ge(cleared, 6)
                for t, v in zip(ends + [e_wt], flats + [k.weight.rearrange("e a -> (e a)")]):
                    for to, of in split_pad(t, v, 1, 0, J):
                        sp.dma_start(to, of).then_inc(ends_in, 16)
                out_view = k.erec[0:EP, :].rearrange("(p j) c -> p (j c)", p=P)
                count = [0, 0]
                for c in range(nchunk):
                    if c >= 2:
                        sp.wait_ge(packed, c - 1)
                    for to, of in split_pad(at[:, c % 2, :], attr_flat, RBF, c * JC, JC):
                        sp.dma_start(to, of).then_inc(attr_in[c % 2], 16)
                    if c >= 1:
                        sp.wait_ge(packed, c)
                        sp.dma_start(out_view[:, (c - 1) * JC * RW:c * JC * RW],
                                     rec[:, (c - 1) % 2, :]).then_inc(rec_out[(c - 1) % 2], 16)
                sp.wait_ge(packed, nchunk)
                sp.dma_start(out_view[:, (nchunk - 1) * JC * RW:], rec[:, (nchunk - 1) % 2, :])\
                    .then_inc(rec_out[(nchunk - 1) % 2], 16)
                for s in range(2):
                    sp.wait_ge(rec_out[s], 16 * len(range(s, nchunk, 2)))

            @block.vector
            def _(dve):
                for t, pad in zip(ends, pads):
                    nc.vector.memset(t[:, :], pad).then_inc(cleared, 1)
                nc.vector.memset(e_wt[:, :], 0.0).then_inc(cleared, 1)
                nc.vector.memset(at[:, :, :], 0.0).then_inc(cleared, 1)
                nc.vector.memset(rec[:, :, :], 0.0).then_inc(cleared, 1)
                dve.wait_ge(ends_in, 16 * n_ends)
                for o, t in ((0, ends[1]), (1, ends[0])):
                    link(dve, nc.vector.tensor_scalar(win_i[:, :], t[:, :], 7, None, ALU.logical_shift_right))
                    link(dve, nc.vector.tensor_copy(win[o][:, 0:J], win_i[:, :]))
                    link(dve, nc.vector.memset(win[o][:, J:], float(WIN)))
                arrived = [0, 0]
                for c in range(nchunk):
                    s = c % 2
                    arrived[s] += 16 * len(split_pad(at[:, s, :], attr_flat, RBF, c * JC, JC))
                    dve.wait_ge(attr_in[s], arrived[s])
                    if c >= 2:
                        dve.wait_ge(rec_out[s], 16 * (c // 2))
                    r = rec[:, s, :].rearrange("p (j c) -> p j c", c=RW)
                    ri = r.bitcast(I32)
                    cols = slice(c * JC, (c + 1) * JC)
                    link(dve, nc.vector.tensor_copy(r[:, :, 0:RBF], at[:, s, :].rearrange("p (j c) -> p j c", c=RBF)))
                    link(dve, nc.vector.tensor_copy(r[:, :, C_WT], e_wt[:, cols]))
                    link(dve, nc.vector.tensor_copy(ri[:, :, C_SRC], ends[0][:, cols]))
                    link(dve, nc.vector.tensor_copy(ri[:, :, C_DST], ends[1][:, cols]))
                    nc.vector.tensor_copy(ri[:, :, C_TYPE], ends[2][:, cols]).then_inc(packed, 1)
                    dve.wait_ge(packed, c + 1)

        hot = sb(own, "hot", [P, 2, T, WP], BF16)
        count = [sb(own, f"count{o}", [P, WP]) for o in range(2)]
        hot_ready, hot_used, counted = sem("hot_ready"), sem("hot_used"), sem("counted")
        first = [sb(own, f"first{o}", [P, WP]) for o in range(2)]

        def one_hot(o, col, s):
            return nc.vector.tensor_tensor(
                hot[:, s, :, :], win[o][:, col].unsqueeze(2).to_broadcast([P, T, WP]),
                k.iota_w[:, :].unsqueeze(1).to_broadcast([P, T, WP]), ALU.is_equal)

        cols = lambda ch: bass.ds(ch * T, T)
        for o in range(2):
            with nc.Block() as block:
                @block.vector
                def _(dve):
                    h0 = k.since(hot_used)
                    for s in range(2):
                        one_hot(o, cols(s), s).then_inc(hot_ready, 1)
                    with dve.Fori(2, NCH - 1, 2) as c:
                        for s in range(2):
                            dve.wait_ge(hot_used, h0 + c + (s - 1))
                            one_hot(o, cols(c + s), s).then_inc(hot_ready, 1)
                    dve.wait_ge(hot_used, h0 + NCH - 2)
                    one_hot(o, cols(NCH - 1), 0).then_inc(hot_ready, 1)
                    dve.wait_ge(hot_used, h0 + NCH)
                    nc.vector.tensor_reduce(count[o][:, :], k.psum[0][:, 0:T * WP].rearrange("p (t w) -> p w t", w=WP),
                                            AX, ALU.add).then_inc(counted, 1)
                    dve.wait_ge(counted, o + 1)

                @block.tensor
                def _(pe):
                    h0 = k.since(hot_ready)

                    def add(s, **f):
                        return nc.tensor.matmul(k.psum[0][:, 0:T * WP], k.ones_b[:, :],
                                                hot[:, s, :, :].rearrange("p t w -> p (t w)"), **f)
                    pe.wait_ge(hot_ready, h0 + 1)
                    add(0, start=True, stop=False).then_inc(hot_used, 1)
                    pe.wait_ge(hot_ready, h0 + 2)
                    add(1, start=False, stop=False).then_inc(hot_used, 1)
                    with pe.Fori(2, NCH - 1, 2) as c:
                        for s in range(2):
                            pe.wait_ge(hot_ready, h0 + c + (s + 1))
                            add(s, start=False, stop=False).then_inc(hot_used, 1)
                    pe.wait_ge(hot_ready, h0 + NCH)
                    add(0, start=False, stop=True).then_inc(hot_used, 1)
            k.since.passed(NCH, hot_ready, hot_used)

        drops, dropped = sb(own, "drops", [P, J - 1], BF16), sb(own, "dropped", [P, 2])
        mixed, mixed_i = sb(own, "mixed", [P, 1]), sb(own, "mixed_i", [P, 1], I32)
        turned_up, found = sem("turned_up"), sem("found")
        with nc.Block() as block:
            @block.tensor
            def _(pe):
                nc.tensor.matmul(k.psum[0][0:P - 1, 0:1], k.ident_b[:, 1:P], win[0][:, 0:1], start=True, stop=True)\
                    .then_inc(turned_up, 1)
                pe.wait_ge(found, 1)
                nc.tensor.matmul(k.psum[1][:, 0:2], k.ones[:, :], dropped[:, :], start=True, stop=True).then_inc(turned_up, 1)

            @block.vector
            def _(dve):
                link(dve, nc.vector.tensor_tensor(drops[:, :], win[0][:, 0:J - 1], win[0][:, 1:J], ALU.is_gt))
                link(dve, nc.vector.memset(dropped[:, :], 0.0))
                link(dve, nc.vector.tensor_reduce(dropped[:, 0:1], drops[:, :], AX, ALU.max))
                dve.wait_ge(turned_up, 1)
                link(dve, nc.vector.tensor_tensor(dropped[0:P - 1, 1:2], win[0][0:P - 1, J - 1:J], k.psum[0][0:P - 1, 0:1],
                                                  ALU.is_gt))
                dve.sem_inc(found, 1)
                dve.wait_ge(turned_up, 2)
                link(dve, nc.vector.tensor_reduce(mixed[:, :], k.psum[1][:, 0:2], AX, ALU.max))
                link(dve, nc.vector.tensor_scalar(mixed[:, :], mixed[:, :], 1.0, None, ALU.min))
                link(dve, nc.vector.tensor_copy(mixed_i[:, :], mixed[:, :]))

        a = [sb(own, f"scan{i}", [P, WP]) for i in range(2)]
        groups, groups_i = sb(own, "groups", [P, WP]), sb(own, "groups_i", [P, WP], I32)
        gi_i, gi = sb(own, "gi_i", [GP, KG], I32), sb(own, "gi", [GP, KG])
        past = sb(own, "past", [GP, KG, WIN])
        took = sb(own, "took", [GP, KG, WIN])
        gw, gs = [sb(own, f"gw{o}", [GP, KG]) for o in range(2)], [sb(own, f"gs{o}", [GP, KG]) for o in range(2)]
        gw_i, gs_i = [sb(own, f"gwi{o}", [GP, KG], I32) for o in range(2)], [sb(own, f"gsi{o}", [GP, KG], I32) for o in range(2)]
        gb = [sb(own, f"gb{o}", [GP, KG]) for o in range(2)]
        run = sb(own, "run", [P, WP])
        numbered, listed, list_out, list_in = sem("numbered"), sem("listed"), sem("list_out"), sem("list_in")

        def scan(dve, source, n):
            cur, other = source, 0
            step = 1
            while step < n:
                nxt = a[other]
                link(dve, nc.vector.tensor_copy(nxt[:, 0:step], cur[:, 0:step]))
                link(dve, nc.vector.tensor_tensor(nxt[:, step:n], cur[:, step:n], cur[:, 0:n - step], ALU.add))
                cur, other, step = nxt, 1 - other, 2 * step
            return cur

        with nc.Block() as block:
            @block.gpsimd
            def _(pool):
                pool.iota(gi_i[:, :], pattern=[[1, KG]], base=0, channel_multiplier=KG).then_inc(numbered, 1)

            @block.vector
            def _(dve):
                dve.wait_ge(numbered, 1)
                link(dve, nc.vector.tensor_copy(gi[:, :], gi_i[:, :]))
                for o in range(2):
                    ends_at = scan(dve, count[o], WP)
                    link(dve, nc.vector.tensor_tensor(first[o][:, :], ends_at[:, 0:WP], count[o][:, :], ALU.subtract))
                    link(dve, nc.vector.tensor_scalar(groups_i[:, :], count[o][:, :], float(GE - 1), None, ALU.add))
                    link(dve, nc.vector.tensor_scalar(groups_i[:, :], groups_i[:, :], GE.bit_length() - 1, None,
                                                      ALU.logical_shift_right))
                    link(dve, nc.vector.tensor_copy(groups[:, :], groups_i[:, :]))
                    upto = scan(dve, groups, WIN)
                    link(dve, nc.vector.tensor_tensor(past[:, :, :], gi[:, :].unsqueeze(2).to_broadcast([GP, KG, WIN]),
                                                      upto[0:GP, 0:WIN].unsqueeze(1).to_broadcast([GP, KG, WIN]), ALU.is_ge))
                    link(dve, nc.vector.tensor_reduce(gw[o][:, :], past[:, :, :], AX, ALU.add))
                    link(dve, nc.vector.scalar_tensor_tensor(groups[:, 0:WIN], groups[:, 0:WIN], -float(GE),
                                                             count[o][:, 0:WIN], ALU.mult, ALU.add))
                    link(dve, nc.vector.tensor_tensor(took[:, :, :], past[:, :, :],
                                                      groups[0:GP, 0:WIN].unsqueeze(1).to_broadcast([GP, KG, WIN]), ALU.mult))
                    link(dve, nc.vector.tensor_reduce(gs[o][:, :], took[:, :, :], AX, ALU.add))
                    link(dve, nc.vector.scalar_tensor_tensor(gs[o][:, :], gi[:, :], float(GE), gs[o][:, :], ALU.mult, ALU.add))
                    link(dve, nc.vector.tensor_scalar(gs[o][:, :], gs[o][:, :], float(EDGES), None, ALU.min))
                    if o == 0:
                        link(dve, nc.vector.scalar_tensor_tensor(gs[o][:, :], mixed[0:GP, :].to_broadcast([GP, KG]), float(EP),
                                                                 gs[o][:, :], ALU.mult, ALU.add))
                    link(dve, nc.vector.tensor_copy(gs_i[o][:, :], gs[o][:, :]))
                    link(dve, nc.vector.tensor_copy(gw_i[o][:, :], gw[o][:, :]))
                    link(dve, nc.vector.tensor_scalar(gb[o][:, :], gw[o][:, :], float(P), None, ALU.mult))
                dve.sem_inc(listed, 1)

            @block.sync
            def _(sp):
                sp.wait_ge(listed, 1)
                for o in range(2):
                    for i, t in enumerate((gw_i[o], gs_i[o])):
                        sp.dma_start(k.lists[o, i, :].rearrange("(p q) -> p q", p=GP), t[:, :]).then_inc(list_out, 16)
                    sp.dma_start(k.bases[o, :].rearrange("(p q) -> p q", p=GP), gb[o][:, :]).then_inc(list_out, 16)
                sp.wait_ge(list_out, 96)
                for o in range(2):
                    sp.dma_start(k.glist[o][:, :, :], k.lists[o, :, :].rearrange("(a i) g -> a i g", a=1)).then_inc(list_in, 16)
                    sp.dma_start(k.gbase[o][:, :], k.bases[o:o + 1, :].broadcast_to([P, NL])).then_inc(list_in, 16)
                sp.wait_ge(list_in, 64)

        with nc.Block() as block:
            @block.vector
            def _(dve):
                for o in range(2):
                    base, same = k.gbase[o], k.gsame[o]
                    link(dve, nc.vector.memset(same[:, 0:1], 0.0))
                    link(dve, nc.vector.tensor_tensor(same[:, 1:], base[:, 1:], base[:, 0:NL - 1], ALU.is_equal))
                    link(dve, nc.vector.tensor_scalar(k.gfresh[o][:, :], same[:, :], -BIG, BIG, ALU.mult, ALU.add))

        pos = sb(own, "pos", [P, J])
        pos_i = sb(own, "pos_i", [P, J], I32)
        place = sb(own, "place", [P, 2, T, WP])

        def if_mixed(eng):
            return eng.If(eng.value_load(mixed_i[0:1, 0:1], min_val=0, max_val=1) > 0)

        def positions(o, to, when):
            ready, ranked, placed, based, own_place, reduced, pos_ready, pos_out = (
                sem(f"{n}{o}") for n in ("window_hot", "ranked", "placed", "based", "own_place", "reduced", "pos_ready",
                                         "pos_out"))
            with nc.Block() as block:
                @block.vector
                def _(dve):
                    def rank(c, s):
                        dve.wait_ge(ranked, c + (s + 1))
                        dve.wait_ge(based, c + (s + 2))
                        nc.vector.tensor_tensor(place[:, s, :, :], k.psum[2 * s][:, 0:T * WP].rearrange("p (t w) -> p t w", w=WP),
                                                run[:, :].unsqueeze(1).to_broadcast([P, T, WP]), ALU.add).then_inc(placed, 1)
                        dve.wait_ge(placed, c + (s + 1))
                        nc.vector.tensor_tensor(run[:, :], run[:, :], k.psum[2 * s + 1][:, 0:WP], ALU.add).then_inc(based, 1)
                        dve.wait_ge(ready, c + (s + 1))
                        nc.vector.tensor_tensor(place[:, s, :, :], place[:, s, :, :], hot[:, s, :, :], ALU.mult)\
                            .then_inc(own_place, 1)
                        dve.wait_ge(own_place, c + (s + 1))
                        nc.vector.tensor_reduce(pos[:, cols(c + s)], place[:, s, :, :], AX, ALU.add).then_inc(reduced, 1)

                    with when(dve):
                        nc.vector.tensor_copy(run[:, :], first[o][:, :]).then_inc(based, 2)
                        for s in range(2):
                            one_hot(o, cols(s), s).then_inc(ready, 1)
                        with dve.Fori(0, NCH - 1, 2) as c:
                            for s in range(2):
                                rank(c, s)
                                one_hot(o, cols(c + (s + 2)), s).then_inc(ready, 1)
                        rank(NCH - 1, 0)
                        dve.wait_ge(reduced, NCH)
                        if o == 0:
                            nc.vector.tensor_scalar(pos[:, :], pos[:, :], float(EP), None, ALU.add).then_inc(reduced, 1)
                            dve.wait_ge(reduced, NCH + 1)
                            nc.vector.tensor_scalar(away[:, :], win[0][:, 0:J], float(WIN), FAR, ALU.is_ge, ALU.mult)\
                                .then_inc(reduced, 1)
                            dve.wait_ge(reduced, NCH + 2)
                            nc.vector.tensor_tensor(pos[:, :], pos[:, :], away[:, :], ALU.add).then_inc(reduced, 1)
                            dve.wait_ge(reduced, NCH + 3)
                        nc.vector.tensor_copy(pos_i[:, :], pos[:, :]).then_inc(pos_ready, 1)

                @block.tensor
                def _(pe):
                    def rank(c, s):
                        pe.wait_ge(ready, c + (s + 1))
                        pe.wait_ge(based, c + (s + 1))
                        f = hot[:, s, :, :].rearrange("p t w -> p (t w)")
                        nc.tensor.matmul(k.psum[2 * s][:, 0:T * WP], k.before_b[:, :], f, start=True, stop=False)
                        for t in range(T - 1):
                            n = T - 1 - t
                            nc.tensor.matmul(k.psum[2 * s][:, (t + 1) * WP:T * WP].rearrange("p (t w) -> p t w", w=WP),
                                             k.ones_b[:, :], hot[:, s, t:t + 1, :].to_broadcast([P, n, WP]),
                                             start=False, stop=t == T - 2)
                        for t in range(T):
                            last = nc.tensor.matmul(k.psum[2 * s + 1][:, 0:WP], k.ones_b[:, :], hot[:, s, t, :],
                                                    start=t == 0, stop=t == T - 1)
                        last.then_inc(ranked, 1)

                    with when(pe):
                        with pe.Fori(0, NCH - 1, 2) as c:
                            for s in range(2):
                                rank(c, s)
                        rank(NCH - 1, 0)

                @block.sync
                def _(sp):
                    with when(sp):
                        sp.wait_ge(pos_ready, 1)
                        sp.dma_start(to.rearrange("(p j) a -> p (j a)", p=P), pos_i[:, :]).then_inc(pos_out, 16)
                        sp.wait_ge(pos_out, 16)

        positions(1, k.epos[0:EP, :], lambda eng: nullcontext())
        away = at[:, :, :].rearrange("p s n -> p (s n)")[:, 0:J]
        positions(0, k.tpos, if_mixed)

        part, part_to, part_pos = sb(own, "part", [P, T, RW]), sb(own, "part_to", [P, T], I32), sb(own, "part_pos", [P, T, 1], I32)
        pads_out, part_in, part_out, part_free, scattering = (
            sem(n) for n in ("pads_out", "part_in", "part_out", "part_free", "scattering"))
        with nc.Block() as block:
            @block.sync
            def _(sp):
                with if_mixed(sp):
                    for t in (k.erec, k.epos):
                        sp.dma_start(t[EP + EDGES:2 * EP, :], t[EDGES:EP, :]).then_inc(pads_out, 16)
                    with sp.Fori(0, NCH, 1) as c:
                        sp.wait_ge(part_free, c + 1)
                        for to, of, width in ((part[:, :, :].rearrange("p t c -> p (t c)"), k.erec[0:EP, :], RW),
                                              (part_to[:, :], k.tpos, 1),
                                              (part_pos[:, :, :].rearrange("p t c -> p (t c)"), k.epos[0:EP, :], 1)):
                            sp.dma_start(to, of.rearrange("(p j) c -> p (j c)", p=P)[:, bass.ds(c * (T * width), T * width)])\
                                .then_inc(part_in, 16)
                    sp.wait_ge(pads_out, 32)

            @block.gpsimd
            def _(pool):
                with if_mixed(pool):
                    pool.sem_inc(part_free, 1)
                    with pool.Fori(0, NCH, 1) as c:
                        pool.wait_ge(part_in, c * 48 + 48)
                        pool.sem_inc(scattering, 1)
                        for t in range(T):
                            for to, of in ((k.erec, part[:, t, :]), (k.epos, part_pos[:, t, :])):
                                pool.indirect_dma_start(to[:, :], bass.IndirectOffsetOnAxis(ap=part_to[:, t:t + 1], axis=0),
                                                        of, None, bounds_check=2 * EP - 1, oob_is_err=False)\
                                    .then_inc(part_out, 16)
                        pool.wait_ge(part_out, c * (2 * T * 16) + 2 * T * 16)
                        pool.sem_inc(part_free, 1)



def load_nodes(k):
    nc, link, xs = k.nc, k.link, k.xs
    zeroed, x_in = k.sem("zeroed"), k.sem("x_in")
    k.valid = k.sb(k.top, "valid", [P, 1])
    valid_i = k.sb(k.top, "valid_i", [P, 1], I32)
    with nc.Block() as block:
        @block.vector
        def _(dve):
            nc.vector.memset(xs[:, WIN - 1, :], 0.0).then_inc(zeroed, 1)
            dve.wait_ge(x_in, 1)
            link(dve, nc.vector.tensor_copy(k.valid[:, :], valid_i[:, :]))
            link(dve, nc.vector.tensor_scalar(k.valid[:, :], k.valid[:, :], float(LAST), None, ALU.is_lt))
            link(dve, nc.vector.memset(k.near[:, WIN, :], 0.0))

        @block.gpsimd
        def _(pool):
            pool.iota(valid_i[:, :], pattern=[[0, 1]], base=0, channel_multiplier=1).then_inc(x_in, 1)

        @block.sync
        def _(sp):
            sp.wait_ge(zeroed, 1)
            sp.wait_ge(x_in, 1)
            sp.dma_start(xs[:, 0:WIN - 1, :], k.x[0:(WIN - 1) * P, :].rearrange("(w p) d -> p w d", p=P)).then_inc(x_in, 16)
            sp.dma_start(xs[0:LAST, WIN - 1, :], k.x[(WIN - 1) * P:NODES, :]).then_inc(x_in, 16)
            sp.wait_ge(x_in, 33)


def layernorm_relu(k):
    nc, link, xs, hs = k.nc, k.link, k.xs, k.hs
    sq = k.acc[:, 0:WIN, 0:D]
    stat = k.stat
    by_act = k.stage["bulk_act"]
    b = k.since(by_act)
    with nc.Block() as block:
        @block.vector
        def _(dve):
            link(dve, nc.vector.tensor_reduce(stat[0][:, :], xs[:, :, :], AX, ALU.add))
            link(dve, nc.vector.tensor_scalar(stat[0][:, :], stat[0][:, :], 1.0 / D, None, ALU.mult))
            link(dve, nc.vector.tensor_tensor(hs[:, :, :], xs[:, :, :], stat[0][:, :].unsqueeze(2).to_broadcast([P, WIN, D]),
                                              ALU.subtract))
            link(dve, nc.vector.tensor_tensor(sq, hs[:, :, :], hs[:, :, :], ALU.mult))
            link(dve, nc.vector.tensor_reduce(stat[1][:, :], sq, AX, ALU.add))
            nc.vector.tensor_scalar(stat[1][:, :], stat[1][:, :], 1.0 / D, 1e-5, ALU.mult, ALU.add).then_inc(by_act, 1)
            dve.wait_ge(by_act, b + 2)
            link(dve, nc.vector.reciprocal(stat[1][:, :], stat[1][:, :]))
            link(dve, nc.vector.scalar_tensor_tensor(hs[:, :, :], hs[:, :, :], 0.0,
                                                     stat[1][:, :].unsqueeze(2).to_broadcast([P, WIN, D]), ALU.max, ALU.mult))

        @block.scalar
        def _(act):
            act.wait_ge(by_act, b + 1)
            nc.scalar.activation(stat[1][:, :], stat[1][:, :], ACT.Sqrt).then_inc(by_act, 1)
    k.since.passed(2, by_act)


def split_near(k, t):
    nc = k.nc
    with nc.Block() as block:
        @block.vector
        def _(dve):
            parts = [k.near[:, 0:WIN, i * D:(i + 1) * D] for i in range(3)]
            split3(nc, lambda ins: k.link(dve, ins), *parts, t[:, :, :], k.acc[:, 0:WIN, 0:D])


def publish(k, t, split):
    nc = k.nc
    if split:
        split_near(k, t)
    out = k.stored
    b = k.since(out)
    with nc.Block() as block:
        @block.sync
        def _(sp):
            if split:
                sp.dma_start(k.table3.rearrange("(w p) c -> p w c", p=P), k.near[:, :, :]).then_inc(out, 16)
                sp.wait_ge(out, b + 16)
            else:
                sp.dma_start(k.table[0:WIN * P, :].rearrange("(w p) c -> p w c", p=P), t[:, :, :]).then_inc(out, 16)
                sp.dma_start(k.table[WIN * P:WP * P, :], k.ones[:, :]).then_inc(out, 16)
                sp.wait_ge(out, b + 32)
    k.since.passed(16 if split else 32, out)


TILES = 7


def node_product(k, W, bias, src, dst, how, add=None):
    assert WIN % TILES == 0
    nc, n = k.nc, TILES * D
    staged, turned, turned_sb, multiplied, epilogued = (k.stage[x] for x in ("staged", "turned", "turned_sb", "multiplied", "epilogued"))
    s, t, ts, m, e = (k.since(x) for x in (staged, turned, turned_sb, multiplied, epilogued))
    all_banks = k.banks[:, :, :].rearrange("p b c -> p (b c)")
    w_sb = k.weights[W][0]
    row = k.rows[bias][0] if bias else None
    turns = WIN // TILES
    with nc.Block() as block:
        @block.vector
        def _(dve):
            dve.sem_inc(epilogued, 1)
            with dve.Fori(0, turns) as i:
                win = bass.ds(i * TILES, TILES)
                st = k.staging[:, :].rearrange("p (w d) -> p w d", d=D)
                dve.wait_ge(epilogued, e + 1 + i * 2)
                if add is None:
                    nc.vector.tensor_scalar(st, src[:, win, 0:D], 1.0, None, ALU.mult).then_inc(staged, 1)
                else:
                    nc.vector.tensor_tensor(st, src[:, win, 0:D], add[:, win, 0:D], ALU.add).then_inc(staged, 1)
                ps = all_banks[:, 1024:1024 + n].rearrange("p (w d) -> p w d", d=D)
                dve.wait_ge(multiplied, m + i + 1)
                if how == "relu":
                    nc.vector.tensor_scalar(dst[:, win, :], ps, 0.0, None, ALU.max).then_inc(epilogued, 2)
                elif how == "copy":
                    nc.vector.tensor_scalar(dst[:, win, :], ps, 1.0, None, ALU.mult).then_inc(epilogued, 2)
                elif how == "add":
                    nc.vector.tensor_tensor(dst[:, win, :], ps, dst[:, win, :], ALU.add).then_inc(epilogued, 2)
                else:
                    nc.vector.tensor_scalar(st, ps, 0.2, None, ALU.mult).then_inc(epilogued, 1)
                    dve.wait_ge(epilogued, e + i * 2 + 2)
                    nc.vector.tensor_tensor(st, st, ps, ALU.max).then_inc(k.stage["bulk_pe"], 1)
                    dve.wait_ge(k.stage["bulk_pe"], k.since(k.stage["bulk_pe"]) + i + 1)
                    nc.vector.tensor_tensor(dst[:, win, :], st, dst[:, win, :], ALU.add).then_inc(epilogued, 1)
            dve.wait_ge(epilogued, e + 1 + 2 * turns)

        @block.tensor
        def _(pe):
            with pe.Fori(0, turns) as i:
                pe.wait_ge(staged, s + i + 1)
                for w in range(TILES):
                    last = nc.tensor.transpose(all_banks[:, w * D:(w + 1) * D], k.staging[:, w * D:(w + 1) * D], k.ident[:, :])
                last.then_inc(turned, 1)
                pe.wait_ge(turned_sb, ts + i + 1)
                for w in range(TILES):
                    o = all_banks[:, 1024 + w * D:1024 + (w + 1) * D]
                    last = nc.tensor.matmul(o, k.staging_t[:, w * D:(w + 1) * D], w_sb[:, :], start=True, stop=row is None)
                    if row is not None:
                        last = nc.tensor.matmul(o, k.ones[0:1, :], row[:, :], start=False, stop=True)
                last.then_inc(multiplied, 1)

        @block.scalar
        def _(act):
            with act.Fori(0, turns) as i:
                act.wait_ge(turned, t + i + 1)
                nc.scalar.activation(k.staging_t[:, :], all_banks[:, 0:n], ACT.Copy).then_inc(turned_sb, 1)
    k.since.passed(turns, staged, turned, turned_sb, multiplied)
    k.since.passed(2 * turns + 1, epilogued)
    if how == "leaky":
        k.since.passed(turns, k.stage["bulk_pe"])


def shifted_softplus(k):
    nc, link, hs = k.nc, k.link, k.hs
    soft = k.acc[:, 0:WIN, 0:D]
    by_act = k.stage["bulk_act"]
    b = k.since(by_act)
    with nc.Block() as block:
        @block.scalar
        def _(act):
            nc.scalar.activation(soft, hs[:, :, :], ACT.Abs).then_inc(by_act, 1)
            act.wait_ge(by_act, b + 1)
            nc.scalar.activation(soft, soft, ACT.Exp, scale=-1.0).then_inc(by_act, 1)
            act.wait_ge(by_act, b + 2)
            nc.scalar.activation(soft, soft, ACT.Ln, bias=1.0).then_inc(by_act, 1)

        @block.vector
        def _(dve):
            dve.wait_ge(by_act, b + 3)
            link(dve, nc.vector.tensor_scalar(hs[:, :, :], hs[:, :, :], 0.0, -LOG2, ALU.max, ALU.add))
            link(dve, nc.vector.tensor_tensor(hs[:, :, :], hs[:, :, :], soft, ALU.add))
    k.since.passed(3, by_act)



def clear(k):
    sems = [*k.stage.values(), *k.rows_in]
    nums = [s.num for s in sems]
    assert nums == list(range(nums[0], nums[0] + len(nums)))
    with k.nc.Block() as block:
        @block.vector
        def _(dve):
            dve.sem_clear(range(nums[0], nums[-1] + 1))
    k.since.cleared(sems)


class Counts:

    def __init__(self, eng):
        self.eng, self.kept = eng, {}

    def turn(self):
        self.kept = {}

    def __call__(self, g, n, times=1):
        if isinstance(g, int):
            return g * times + n
        if (n, times) not in self.kept:
            self.kept[n, times] = self.eng.snap(g * times + n)
        return self.kept[n, times]


def skewed(eng, *stages, counts=None):
    most = max(lead for lead, _ in stages)
    for n in range(-most, 0):
        for lead, stage in stages:
            if n + lead >= 0:
                stage(0, n + lead)
    with eng.Fori(0, NG, U) as g:
        if counts:
            counts.turn()
        for u in range(U):
            for lead, stage in stages:
                stage(g, u + lead)


def landed(g, ahead, each=16):
    return g * (each // U) + (ahead // U + 1) * each


def in_slot(u, lead):
    return len(range(u, NG + lead, U))


def per_slot(since, sems, each, lead):
    for u, sem in enumerate(sems):
        since.passed(each * in_slot(u, lead), sem)


def window(eng, k, o, g):
    return bass.ds(eng.value_load(k.glist[o][0:1, 0, bass.ds(g, 1)], min_val=0, max_val=WIN), 1)


def first_edge(eng, k, o, g):
    return eng.value_load(k.glist[o][0:1, 1, bass.ds(g, 1)], min_val=0, max_val=EDGES + (EP if o == 0 else 0))


def segment_sums(k, o):
    nc, st = k.nc, k.stage
    rel_ready, onehot_ready, summed, added = (st[x] for x in ("rel_ready", "onehot_ready", "summed", "added"))
    width, key = (RW, C_DST) if o == 0 else (MW, M_SRC)
    records = k.erec if o == 0 else k.mrec
    s_rel, s_hot, s_sum, s_add = (k.since(x) for x in (rel_ready, onehot_ready, summed, added))
    s_row, s_pool = [k.since(x) for x in k.rows_in], [k.since(x) for x in k.pool_done]
    lead = 1
    with ExitStack() as own:
        rows = k.sb(own, f"sum_rows{o}", [P, U, KG, width])
        rel = k.sb(own, f"sum_rel{o}", [P, U, KG])
        hot = k.sb(own, f"sum_hot{o}", [P, U, KG, P], BF16 if o == 0 else F32)
        far = k.sb(own, "sum_far", [P, U, KG, 3 * D], BF16) if o == 0 else None
        with nc.Block() as block:
            @block.sync
            def _(sp):
                def load(g, a):
                    sp.wait_ge(summed, s_sum + g + a + 1)
                    e0 = first_edge(sp, k, o, g + a)
                    sp.dma_start(rows[:, a % U, :, :].rearrange("p q c -> p (q c)"),
                                 records[bass.ds(e0, GE), :].rearrange("(p q) c -> p (q c)", q=KG))\
                        .then_inc(k.rows_in[a % U], 16)
                skewed(sp, (lead, load))

            if o == 0:
                @block.gpsimd
                def _(pool):
                    def gather(g, a):
                        pool.wait_ge(k.rows_in[a], s_row[a] + landed(g, a))
                        pool.wait_ge(summed, s_sum + g + a + 1)
                        pool.sem_inc(k.begun, 1)
                        for q in range(KG):
                            pool.indirect_dma_start(
                                far[:, a, q, :], None, k.table3[:, :],
                                bass.IndirectOffsetOnAxis(ap=rows[:, a, q, C_SRC:C_SRC + 1].bitcast(I32), axis=0))\
                                .then_inc(k.pool_done[a], 16)
                    skewed(pool, (0, gather))

            @block.vector
            def _(dve):
                nc.vector.memset(k.acc[:, :, :], 0.0).then_inc(added, 2)

                def one_hot(g, a):
                    u = a % U
                    dve.wait_ge(k.rows_in[u], s_row[u] + landed(g, a))
                    dve.wait_ge(summed, s_sum + g + a + 1)
                    nc.vector.tensor_scalar(rel[:, u, :], rows[:, u, :, key].bitcast(I32), k.gbase[o][:, bass.ds(g + a, 1)],
                                            None, ALU.subtract).then_inc(rel_ready, 1)
                    dve.wait_ge(rel_ready, s_rel + g + a + 1)
                    for q in range(KG):
                        last = nc.vector.tensor_scalar(hot[:, u, q, :], k.iota_b[:, :], rel[:, u, q:q + 1], None, ALU.is_equal)
                    last.then_inc(onehot_ready, 1)

                def add(g, a):
                    w = window(dve, k, o, g + a)
                    dve.wait_ge(summed, s_sum + U + g + a + 1)
                    dve.wait_ge(added, s_add + 2 + g + a)
                    nc.vector.tensor_tensor(k.acc[:, w, 0:D], k.psum[a % 2][:, 0:D].unsqueeze(1), k.acc[:, w, 0:D],
                                            ALU.add).then_inc(added, 1)
                skewed(dve, (lead, one_hot), (0, add))

            @block.tensor
            def _(pe):
                pe.sem_inc(summed, U)

                def total(g, a):
                    pe.wait_ge(onehot_ready, s_hot + g + a + 1)
                    pe.wait_ge(added, s_add + g + a + 1)
                    if o == 0:
                        pe.wait_ge(k.pool_done[a], s_pool[a] + landed(g, a, 16 * KG))
                    for q in range(KG):
                        for part in range(3 if o == 0 else 1):
                            rhs = far[:, a, q, part * D:(part + 1) * D] if o == 0 else rows[:, a, q, 0:D]
                            last = nc.tensor.matmul(k.psum[a % 2][:, 0:D], hot[:, a, q, :], rhs,
                                                    start=q == 0 and part == 0, stop=q == KG - 1 and part == (2 if o == 0 else 0))
                    last.then_inc(summed, 1)
                skewed(pe, (0, total))
    k.since.passed(NG + lead, rel_ready, onehot_ready)
    k.since.passed(NG + U, summed)
    k.since.passed(NG + 2, added)
    per_slot(k.since, k.rows_in, 16, lead)
    if o == 0:
        per_slot(k.since, k.pool_done, 16 * KG, 0)


def filter_messages(k):
    nc, st = k.nc, k.stage
    names = ("rel_ready", "onehot_ready", "onehot_turned", "onehotT_ready", "attr_turned", "attrT_ready", "hidden_ready",
             "soft1", "soft2", "soft3", "soft4", "soft_ready", "filter_ready", "far_ready", "biased", "index_ready",
             "message_ready")
    (rel_ready, onehot_ready, onehot_turned, onehotT_ready, attr_turned, attrT_ready, hidden_ready, soft1, soft2, soft3,
     soft4, soft_ready, filter_ready, far_ready, biased, index_ready, message_ready) = (st[x] for x in names)
    at = {st[x].name: k.since(st[x]) for x in names}
    s_row, s_pool = [k.since(x) for x in k.rows_in], [k.since(x) for x in k.pool_done]
    w_f2, b_f2 = k.weights["W_f2"][0], k.wide["b_f2"][0]
    pads = EP - EDGES
    with ExitStack() as own:
        sb = lambda name, shape, dt=F32: k.sb(own, name, shape, dt)
        rows, pos = sb("f_rows", [P, U, KG, RW]), sb("f_pos", [P, U, KG], I32)
        rel, hot = sb("f_rel", [P, U, KG]), sb("f_hot", [P, U, KG, P], BF16)
        hot_t, attr_t = sb("f_hot_t", [P, U, GE], BF16), sb("f_attr_t", [RBF, 2, GE])
        soft, sp_t = sb("f_soft", [P, 2, GE]), sb("f_sp", [P, 2, GE])
        tmp, index, off = sb("f_tmp", [P, KG, D]), sb("f_index", [P, U, KG], I32), sb("f_off", [P, KG])
        msg = sb("f_msg", [P, U, KG, MW])
        pad = sb("f_pad", [pads // 8, 8, MW])
        pad_i = pad[:, :, :].bitcast(I32)
        hot_ps = k.psum[0].bitcast(BF16)[:, 0:GE]
        attr_ps = k.psum[1][0:RBF, :]
        hidden_ps, far_ps, filter_ps = k.psum[2:4], k.psum[4:6], k.psum[6:8]
        padded = k.sem("padded")

        with nc.Block() as block:
            @block.sync
            def _(sp):
                sp.wait_ge(padded, 2)
                sp.dma_start(k.mrec[EDGES:EP, :].rearrange("(p j) c -> p j c", j=8), pad[:, :, :]).then_inc(padded, 16)

                def load(g, a):
                    u = a % U
                    sp.wait_ge(message_ready, at[message_ready.name] + g + a + 1)
                    e0 = first_edge(sp, k, 0, g + a)
                    sp.dma_start(rows[:, u, :, :].rearrange("p q c -> p (q c)"),
                                 k.erec[bass.ds(e0, GE), :].rearrange("(p q) c -> p (q c)", q=KG)).then_inc(k.rows_in[u], 16)
                    sp.dma_start(pos[:, u, :], k.epos[bass.ds(e0, GE), :].rearrange("(p q) c -> p (q c)", q=KG))\
                        .then_inc(k.rows_in[u], 16)
                skewed(sp, (3, load))
                sp.wait_ge(padded, 18)

            @block.gpsimd
            def _(pool):
                def scatter(g, a):
                    pool.wait_ge(message_ready, at[message_ready.name] + U + g + a + 1)
                    pool.sem_inc(k.begun, 1)
                    for q in range(KG):
                        pool.indirect_dma_start(
                            k.mrec[:, :], bass.IndirectOffsetOnAxis(ap=index[:, a, q:q + 1], axis=0), msg[:, a, q, :], None,
                            bounds_check=EDGES - 1, oob_is_err=False).then_inc(k.pool_done[a], 16)
                skewed(pool, (0, scatter))
                for u in range(U):
                    pool.wait_ge(k.pool_done[u], s_pool[u] + 16 * KG * NG // U)

            @block.vector
            def _(dve):
                nc.vector.memset(pad[:, :, :], 0.0).then_inc(padded, 1)
                dve.wait_ge(padded, 1)
                nc.vector.memset(pad_i[:, :, M_SRC:M_SRC + 1], NOWHERE).then_inc(padded, 1)
                nc.vector.memset(msg[:, :, :, :], 0.0).then_inc(message_ready, U)
                dve.wait_ge(message_ready, at[message_ready.name] + U)
                dve.sem_inc(soft_ready, 2)
                dve.sem_inc(index_ready, 1)

                def one_hot(g, a):
                    u = a % U
                    dve.wait_ge(k.rows_in[u], s_row[u] + landed(g, a, 32))
                    nc.vector.tensor_scalar(rel[:, u, :], rows[:, u, :, C_DST].bitcast(I32), k.gbase[0][:, bass.ds(g + a, 1)],
                                            None, ALU.subtract).then_inc(rel_ready, 1)
                    dve.wait_ge(rel_ready, at[rel_ready.name] + g + a + 1)
                    for q in range(KG):
                        last = nc.vector.tensor_scalar(hot[:, u, q, :], k.iota_b[:, :], rel[:, u, q:q + 1], None, ALU.is_equal)
                    last.then_inc(onehot_ready, 1)

                def softplus(g, a):
                    b = a % 2
                    dve.wait_ge(soft1, at[soft1.name] + g + a + 1)
                    nc.vector.tensor_scalar(sp_t[:, b, :], hidden_ps[b], k.bf1[:, :], 0.0, ALU.add, ALU.max).then_inc(soft4, 1)
                    dve.wait_ge(soft4, at[soft4.name] + g + a + 1)
                    dve.wait_ge(soft3, at[soft3.name] + g + a + 1)
                    nc.vector.scalar_tensor_tensor(sp_t[:, b, :], sp_t[:, b, :], -LOG2, soft[:, b, :], ALU.add, ALU.add)\
                        .then_inc(soft_ready, 1)

                def message(g, a):
                    u, b = a % U, a % 2
                    dve.wait_ge(index_ready, at[index_ready.name] + 1 + 2 * (g + a))
                    nc.vector.tensor_scalar(off[:, :], rel[:, u, :], float(P), FAR, ALU.is_ge, ALU.mult).then_inc(index_ready, 1)
                    dve.wait_ge(index_ready, at[index_ready.name] + 2 * (g + a) + 2)
                    dve.wait_ge(k.pool_done[u], s_pool[u] + landed(g, a, 16 * KG) - 16 * KG)
                    nc.vector.tensor_tensor(index[:, u, :], off[:, :], pos[:, u, :], ALU.add).then_inc(index_ready, 1)
                    nc.vector.tensor_copy(msg[:, u, :, M_SRC:M_SRC + 3].bitcast(I32), rows[:, u, :, C_SRC:C_SRC + 3].bitcast(I32))
                    dve.wait_ge(filter_ready, at[filter_ready.name] + g + a + 1)
                    dve.wait_ge(message_ready, at[message_ready.name] + U + g + a)
                    nc.vector.tensor_tensor(tmp[:, :, :], filter_ps[b].rearrange("p (q d) -> p q d", d=D),
                                            b_f2[:, :].unsqueeze(1).to_broadcast([P, KG, D]), ALU.add).then_inc(biased, 1)
                    dve.wait_ge(biased, at[biased.name] + g + a + 1)
                    dve.wait_ge(far_ready, at[far_ready.name] + g + a + 1)
                    for q in range(KG):
                        last = nc.vector.scalar_tensor_tensor(msg[:, u, q, 0:D], tmp[:, q, :], rows[:, u, q, C_WT:C_WT + 1],
                                                              far_ps[b][:, q * D:(q + 1) * D], ALU.mult, ALU.mult)
                    last.then_inc(message_ready, 1)
                skewed(dve, (1, softplus), (3, one_hot), (0, message))

            @block.scalar
            def _(act):
                act.sem_inc(onehotT_ready, 1)
                act.sem_inc(attrT_ready, 1)

                def turn(g, a):
                    u, b = a % U, a % 2
                    act.wait_ge(onehot_turned, at[onehot_turned.name] + g + a + 1)
                    nc.scalar.activation(hot_t[:, u, :], hot_ps, ACT.Copy).then_inc(onehotT_ready, 1)
                    act.wait_ge(attr_turned, at[attr_turned.name] + g + a + 1)
                    nc.scalar.activation(attr_t[:, b, :], attr_ps, ACT.Copy).then_inc(attrT_ready, 1)

                def soften(g, a):
                    b = a % 2
                    act.wait_ge(hidden_ready, at[hidden_ready.name] + g + a + 1)
                    nc.scalar.activation(soft[:, b, :], hidden_ps[b], ACT.Abs, bias=k.bf1[:, :]).then_inc(soft1, 1)
                    act.wait_ge(soft1, at[soft1.name] + g + a + 1)
                    nc.scalar.activation(soft[:, b, :], soft[:, b, :], ACT.Exp, scale=-1.0).then_inc(soft2, 1)
                    act.wait_ge(soft2, at[soft2.name] + g + a + 1)
                    nc.scalar.activation(soft[:, b, :], soft[:, b, :], ACT.Ln, bias=1.0).then_inc(soft3, 1)
                skewed(act, (3, turn), (2, soften))

            @block.tensor
            def _(pe):
                def turn(g, a):
                    u = a % U
                    pe.wait_ge(onehot_ready, at[onehot_ready.name] + g + a + 1)
                    pe.wait_ge(onehotT_ready, at[onehotT_ready.name] + g + a + 1)
                    for q in range(KG):
                        last = nc.tensor.transpose(hot_ps[:, q * P:(q + 1) * P], hot[:, u, q, :], k.ident_b[:, :])
                    last.then_inc(onehot_turned, 1)
                    pe.wait_ge(attrT_ready, at[attrT_ready.name] + g + a + 1)
                    for q in range(KG):
                        last = nc.tensor.transpose(attr_ps[:, q * P:(q + 1) * P], rows[:, u, q, 0:RBF], k.ident[:, :])
                    last.then_inc(attr_turned, 1)

                def filters(g, a):
                    b = a % 2
                    pe.wait_ge(message_ready, at[message_ready.name] + U - 1 + g + a)
                    near_rows(pe, k, 0, g + a, far_ps[b], hot_t[:, a % U, :], onehotT_ready, at[onehotT_ready.name] + 1 + g + a + 1)\
                        .then_inc(far_ready, 1)
                    pe.wait_ge(soft_ready, at[soft_ready.name] + 2 + g + a + 1)
                    for q in range(KG):
                        last = nc.tensor.matmul(filter_ps[b][:, q * D:(q + 1) * D], sp_t[:, b, q * P:(q + 1) * P], w_f2[:, :],
                                                start=True, stop=True)
                    last.then_inc(filter_ready, 1)

                def hidden(g, a):
                    b = a % 2
                    pe.wait_ge(attrT_ready, at[attrT_ready.name] + 1 + g + a + 1)
                    pe.wait_ge(soft_ready, at[soft_ready.name] + g + a + 1)
                    nc.tensor.matmul(hidden_ps[b], k.w_f1[:, :], attr_t[:, b, :], start=True, stop=True).then_inc(hidden_ready, 1)
                skewed(pe, (2, hidden), (3, turn), (1, filters))
    since = k.since
    since.passed(NG + 2, hidden_ready, soft1, soft2, soft3)
    since.passed(NG + 3, rel_ready, onehot_ready, onehot_turned, attr_turned, soft_ready)
    since.passed(NG + 4, onehotT_ready, attrT_ready)
    since.passed(NG + 1, soft4, filter_ready, far_ready)
    since.passed(NG, biased)
    since.passed(2 * NG + 1, index_ready)
    since.passed(NG + U, message_ready)
    per_slot(since, k.rows_in, 32, 3)
    per_slot(since, k.pool_done, 16 * KG, 0)


def near_rows(pe, k, o, g, ps, hot_t, ready, value, stop=True):
    nc = k.nc
    w = window(pe, k, o, g)
    pe.wait_ge(ready, value)
    for q in range(KG):
        for part in range(3):
            last = nc.tensor.matmul(ps[:, q * D:(q + 1) * D], hot_t[:, q * P:(q + 1) * P], k.near[:, w, part * D:(part + 1) * D]
                                    .rearrange("p a d -> p (a d)"), start=part == 0, stop=stop and part == 2)
    return last


def attention(k, layer):
    nc, st, o = k.nc, k.stage, layer
    HOT, SCORE, MAX, SUM, ADD = 4, 3, 2, 1, 0
    leads = dict(rel_ready=HOT, kinds_ready=HOT, onehot_ready=HOT, onehot_turned=HOT, onehotT_ready=HOT, edge_term=HOT,
                 near_ready=HOT, in1=SCORE, in2=SCORE, in3=SCORE, edge_dot=SCORE, scores=SCORE, spread=MAX, group_max=MAX,
                 exp_in=MAX, weighed=MAX, shrink=MAX, prob_turned=MAX, prob_ready=SUM, summed=SUM, added=ADD)
    (rel_ready, kinds_ready, onehot_ready, onehot_turned, onehotT_ready, edge_term, near_ready, in1, in2, in3, edge_dot,
     scores, spread, group_max, exp_in, weighed, shrink, prob_turned, prob_ready, summed, added) = (st[x] for x in leads)
    lead_of = {st[x].name: lead for x, lead in leads.items()}
    kept = st["kept"]

    def wait(eng, now, sem, g, a, behind=0):
        eng.wait_ge(sem, now(g, a - behind + 1 + CREDIT - lead_of[sem.name]))

    def start(eng, *sems):
        for sem in sems:
            eng.sem_inc(sem, CREDIT - lead_of[sem.name])

    s_pool = k.since(k.pool_done[0])
    assert all(k.since(x) == s_pool for x in k.pool_done) and not any(k.since(x) for x in k.rows_in)
    width, key, other = (RW, C_DST, C_SRC) if o == 0 else (MW, M_SRC, M_DST)
    records = k.erec if o == 0 else k.mrec
    HW = P if o == 0 else P + NTYPE
    We, att = k.wide["We"][0], k.wide["att"][0]
    XW = D + 4
    with ExitStack() as own:
        sb = lambda name, shape, dt=F32: k.sb(own, f"{name}{o}", shape, dt)
        rows, rel, hide = sb("a_rows", [P, U, KG, width]), sb("a_rel", [P, U, KG]), sb("a_hide", [P, U, KG])
        kind = sb("a_kind", [P, U, KG])
        hot, hot_t = sb("a_hot", [P, 2, KG, HW], BF16), sb("a_hot_t", [P, U, GE], BF16)
        kind_t = sb("a_kind_t", [NTYPE, 2, GE], BF16) if o else None
        far = sb("a_far", [P, U, KG, XW])
        term = sb("a_term", [P, 2, KG, D])
        work = sb("a_work", [P, KG, D])
        raw, score = sb("a_raw", [P, KG]), sb("a_score", [P, U, KG])
        gmax = sb("a_gmax", [P, 1])
        before, bounded, factor = sb("a_before", [P, U]), sb("a_bounded", [P, U]), sb("a_factor", [P, U])
        cur = sb("a_cur", [P, U, XW])
        prob_t, prob = sb("a_prob_t", [P, 2, GE]), sb("a_prob", [P, 2, GE])
        hot_ps = k.psum[0].bitcast(BF16)
        near_ps, spread_ps, prob_ps, sum_ps = k.psum[1:3], k.psum[3:5], k.psum[5], k.psum[6:8]

        with nc.Block() as block:
            @block.sync
            def _(sp):
                now = Counts(sp)
                sp.sem_inc(kept, 16 * U)

                def load(g, a):
                    wait(sp, now, scores, g, a, U)
                    e0 = first_edge(sp, k, o, g + a)
                    sp.dma_start(rows[:, a % U, :, :].rearrange("p q c -> p (q c)"),
                                 records[bass.ds(e0, GE), :].rearrange("(p q) c -> p (q c)", q=KG)).then_inc(k.rows_in[a % U], 16)

                def keep(g, a):
                    wait(sp, now, added, g, a)
                    sp.sem_inc(k.loading, 1)
                    sp.wait_ge(kept, now(g, 16 * (U + a), 16))
                    sp.sem_inc(k.loading, 1)
                    w = window(sp, k, o, g + a)
                    sp.dma_start(k.acc[:, w, 0:D + 2], cur[:, a % U, 0:D + 2].unsqueeze(1)).then_inc(kept, 16)
                skewed(sp, (LOADS, load), (ADD, keep), counts=now)
                for u in range(U):
                    sp.wait_ge(k.rows_in[u], in_slot(u, LOADS) * 16)
                sp.wait_ge(kept, 16 * (U + NG))

            @block.gpsimd
            def _(pool):
                now = Counts(pool)

                def gather(g, a):
                    u = a % U
                    pool.wait_ge(k.rows_in[u], now(g, 16 * (a // U + 1), 16 // U))
                    wait(pool, now, summed, g, a, U)
                    pool.sem_inc(k.begun, 1)
                    for q in range(KG):
                        pool.indirect_dma_start(
                            far[:, u, q, 0:D], None, k.table[:, :],
                            bass.IndirectOffsetOnAxis(ap=rows[:, u, q, other:other + 1].bitcast(I32), axis=0))\
                            .then_inc(k.pool_done[u], 16)
                skewed(pool, (HOT, gather), counts=now)

            @block.vector
            def _(dve):
                now = Counts(dve)
                k.link(dve, nc.vector.memset(k.acc[:, :, :], 0.0))
                k.link(dve, nc.vector.memset(k.acc[:, :, D + 1:D + 2], -LOW))
                k.link(dve, nc.vector.memset(cur[:, :, :], 0.0))
                k.link(dve, nc.vector.memset(cur[:, :, D + 1:D + 2], -LOW))
                k.link(dve, nc.vector.memset(far[:, :, :, :], 1.0))
                start(dve, rel_ready, onehot_ready, scores, group_max, exp_in, added, edge_dot,
                      *((kinds_ready,) if o else (in1, in2, in3)))

                def one_hot(g, a):
                    u, b, n = a % U, a % 2, g + a
                    dve.wait_ge(k.rows_in[u], now(g, 16 * (a // U + 1), 16 // U))
                    nc.vector.tensor_scalar(rel[:, u, :], rows[:, u, :, key].bitcast(I32), k.gbase[o][:, bass.ds(n, 1)],
                                            None, ALU.subtract).then_inc(rel_ready, 1)
                    if o:
                        nc.vector.tensor_copy(kind[:, u, :], rows[:, u, :, M_TYPE].bitcast(I32)).then_inc(kinds_ready, 1)
                    wait(dve, now, kinds_ready if o else rel_ready, g, a)
                    wait(dve, now, onehot_turned, g, a, 2)
                    for q in range(KG):
                        last = nc.vector.tensor_scalar(hot[:, b, q, 0:P], k.iota_b[:, :], rel[:, u, q:q + 1], None, ALU.is_equal)
                        if o:
                            last = nc.vector.tensor_scalar(hot[:, b, q, P:HW], k.iota_b[:, 0:NTYPE], kind[:, u, q:q + 1], None,
                                                           ALU.is_equal)
                    nc.vector.tensor_scalar(hide[:, u, :], rel[:, u, :], float(P), -BIG, ALU.is_ge, ALU.mult).then_inc(onehot_ready, 1)

                def meet(g, a):
                    u, b = a % U, a % 2
                    dve.wait_ge(k.pool_done[u], now(g, s_pool + 16 * KG * (a // U + 1), 16 * KG // U))
                    wait(dve, now, near_ready, g, a)
                    nc.vector.tensor_tensor(work[:, :, :], near_ps[b].rearrange("p (q d) -> p q d", d=D), far[:, u, :, 0:D],
                                            ALU.add).then_inc(in1, 1)
                    wait(dve, now, in1, g, a)
                    wait(dve, now, edge_term, g, a)
                    nc.vector.tensor_tensor(term[:, b, :, :], work[:, :, :], term[:, b, :, :], ALU.add).then_inc(in2, 1)

                def score_edges(g, a):
                    u, b = a % U, a % 2
                    if o == 0:
                        wait(dve, now, in2, g, a)
                        nc.vector.scalar_tensor_tensor(term[:, b, :, :], term[:, b, :, :], 0.2, term[:, b, :, :], ALU.mult, ALU.max)\
                            .then_inc(in3, 1)
                        wait(dve, now, in3, g, a)
                    else:
                        dve.wait_ge(k.pool_done[u], now(g, s_pool + 16 * KG * (a // U + 1), 16 * KG // U))
                        wait(dve, now, edge_term, g, a)
                    for q in range(KG):
                        last = nc.vector.scalar_tensor_tensor(
                            work[:, q, :], term[:, b, q, :], 1.0, far[:, u, q, 0:D] if o else att[:, :], ALU.mult, ALU.mult,
                            accum_out=raw[:, q:q + 1])
                    last.then_inc(edge_dot, 1)
                    wait(dve, now, edge_dot, g, a)
                    nc.vector.tensor_tensor(score[:, u, :], raw[:, :], hide[:, u, :], ALU.add).then_inc(scores, 1)

                def node_max(g, a):
                    u, b, f = a % U, a % 2, bass.ds(g + a, 1)
                    past = cur[:, (u - 1) % U, D + 1:D + 2]
                    wait(dve, now, exp_in, g, a, 1)
                    dve.wait_ge(kept, now(g, 16 * (U + a - U + 1), 16))
                    nc.vector.tensor_scalar(before[:, u:u + 1], past, k.gfresh[o][:, f], None, ALU.add)
                    nc.vector.tensor_scalar(bounded[:, u:u + 1], past, k.gfresh[o][:, f], -LOW, ALU.add, ALU.min)
                    wait(dve, now, spread, g, a)
                    nc.vector.tensor_reduce(gmax[:, :], spread_ps[b], AX, ALU.max).then_inc(group_max, 1)
                    wait(dve, now, group_max, g, a)
                    nc.vector.scalar_tensor_tensor(cur[:, u, D + 1:D + 2], gmax[:, :], -1.0, bounded[:, u:u + 1], ALU.mult, ALU.min)\
                        .then_inc(exp_in, 1)

                def add(g, a):
                    u, b = a % U, a % 2
                    wait(dve, now, summed, g, a)
                    wait(dve, now, shrink, g, a)
                    wait(dve, now, added, g, a, 1)
                    nc.vector.scalar_tensor_tensor(cur[:, u, 0:D + 1], cur[:, (u - 1) % U, 0:D + 1], factor[:, u:u + 1],
                                                   sum_ps[b][:, 0:D + 1], ALU.mult, ALU.add).then_inc(added, 1)
                skewed(dve, *(() if o else ((SCORE, meet),)), (HOT, one_hot), (MAX, node_max), (ADD, add), (SCORE, score_edges),
                       counts=now)

            @block.scalar
            def _(act):
                now = Counts(act)
                start(act, onehotT_ready, edge_term, weighed, shrink, prob_ready)

                def take_prob(g, a):
                    b = a % 2
                    wait(act, now, prob_turned, g, a)
                    wait(act, now, summed, g, a, 2)
                    nc.scalar.activation(prob[:, b, :], prob_ps, ACT.Copy).then_inc(prob_ready, 1)

                def turn(g, a):
                    u, b = a % U, a % 2
                    wait(act, now, onehot_turned, g, a)
                    if o:
                        nc.scalar.activation(kind_t[:, b, :], hot_ps[0:NTYPE, GE:2 * GE], ACT.Copy)
                    nc.scalar.activation(hot_t[:, u, :], hot_ps[:, 0:GE], ACT.Copy).then_inc(onehotT_ready, 1)

                def weigh(g, a):
                    u, b = a % U, a % 2
                    wait(act, now, exp_in, g, a)
                    nc.scalar.activation(prob_t[:, b, :], spread_ps[b], ACT.Exp, bias=cur[:, u, D + 1:D + 2]).then_inc(weighed, 1)
                    wait(act, now, added, g, a, U)
                    nc.scalar.activation(factor[:, u:u + 1], before[:, u:u + 1], ACT.Exp, scale=-1.0,
                                         bias=cur[:, u, D + 1:D + 2]).then_inc(shrink, 1)

                def terms(g, a):
                    u, b = a % U, a % 2
                    wait(act, now, scores, g, a, 2)
                    if o == 0:
                        for q in range(KG):
                            last = nc.scalar.activation(term[:, b, q, :], We[:, :], ACT.Copy, scale=rows[:, u, q, C_WT:C_WT + 1])
                        last.then_inc(edge_term, 1)
                    else:
                        wait(act, now, near_ready, g, a)
                        nc.scalar.activation(term[:, b, :, :], near_ps[b].rearrange("p (q d) -> p q d", d=D), ACT.Tanh)\
                            .then_inc(edge_term, 1)
                skewed(act, (SUM, take_prob), (HOT, turn), (MAX, weigh), (HOT, terms),
                       counts=now)

            @block.tensor
            def _(pe):
                now = Counts(pe)
                start(pe, onehot_turned, near_ready, spread, prob_turned, summed)

                def spreads(g, a):
                    u, b = a % U, a % 2
                    wait(pe, now, scores, g, a)
                    nc.tensor.matmul(spread_ps[b], k.apart_b[:, :], hot_t[:, u, :], start=True, stop=False, skip_group_check=True)
                    for q in range(KG):
                        last = nc.tensor.matmul(spread_ps[b][:, q * P:(q + 1) * P], score[:, u, q:q + 1].to_broadcast([P, P]),
                                                k.ident[:, :], start=False, stop=q == KG - 1, skip_group_check=True)
                    last.then_inc(spread, 1)

                def turn(g, a):
                    b = a % 2
                    wait(pe, now, onehot_ready, g, a)
                    wait(pe, now, onehotT_ready, g, a, 1)
                    for q in range(KG):
                        last = nc.tensor.transpose(hot_ps[:, q * P:(q + 1) * P], hot[:, b, q, 0:P], k.ident_b[:, :])
                        if o:
                            last = nc.tensor.transpose(hot_ps[0:NTYPE, GE + q * P:GE + (q + 1) * P], hot[:, b, q, P:HW],
                                                       k.ident_b[:, :])
                    last.then_inc(onehot_turned, 1)

                def sums(g, a):
                    u, b = a % U, a % 2
                    wait(pe, now, prob_ready, g, a)
                    wait(pe, now, added, g, a, 2)
                    for q in range(KG):
                        last = nc.tensor.matmul(sum_ps[b][:, 0:D + 1], prob[:, b, q * P:(q + 1) * P], far[:, u, q, 0:D + 1],
                                                start=q == 0, stop=q == KG - 1)
                    last.then_inc(summed, 1)

                def rows_near(g, a):
                    u, b, n = a % U, a % 2, g + a
                    wait(pe, now, scores, g, a, 2)
                    if o == 0:
                        near_rows(pe, k, o, n, near_ps[b], hot_t[:, u, :], onehotT_ready, now(g, a + 1 + CREDIT - HOT))\
                            .then_inc(near_ready, 1)
                        return
                    w = window(pe, k, o, n)
                    wait(pe, now, onehotT_ready, g, a)
                    for q in range(KG):
                        cols = slice(q * P, (q + 1) * P)
                        for part in range(3):
                            nc.tensor.matmul(near_ps[b][:, cols], hot_t[:, u, cols], k.near[:, w, part * D:(part + 1) * D]
                                             .rearrange("p a d -> p (a d)"), start=part == 0, stop=False)
                        for part in range(3):
                            last = nc.tensor.matmul(near_ps[b][:, cols], kind_t[:, b, cols], k.rel3[:, part * D:(part + 1) * D],
                                                    start=False, stop=part == 2)
                    last.then_inc(near_ready, 1)

                def turn_prob(g, a):
                    b = a % 2
                    wait(pe, now, weighed, g, a)
                    for q in range(KG):
                        last = nc.tensor.transpose(prob_ps[:, q * P:(q + 1) * P], prob_t[:, b, q * P:(q + 1) * P], k.ident[:, :])
                    last.then_inc(prob_turned, 1)
                skewed(pe, (MAX, spreads), (SUM, sums), (HOT, turn), (HOT, rows_near), (MAX, turn_prob), counts=now)
    k.since.passed(CREDIT + NG, *(x for x in map(st.get, leads)))
    per_slot(k.since, k.rows_in, 16, LOADS)
    per_slot(k.since, k.pool_done, 16 * KG, HOT)


def gat_output(k):
    nc, link, hs, acc, stat = k.nc, k.link, k.hs, k.acc, k.stat
    by_act, by_pe = k.stage["bulk_act"], k.stage["bulk_pe"]
    b, p = k.since(by_act), k.since(by_pe)
    full = [P, WIN, D]
    spread = lambda t: t.unsqueeze(1).to_broadcast(full)
    with ExitStack() as own:
        part, mean = k.sb(own, "bn_part", [P, D]), k.sb(own, "bn_mean", [P, D])
        scale = k.sb(own, "bn_scale", [P, D])
        with nc.Block() as block:
            @block.vector
            def _(dve):
                link(dve, nc.vector.tensor_scalar(stat[0][:, :], acc[:, 0:WIN, D], 1e-16, None, ALU.add))
                link(dve, nc.vector.reciprocal(stat[0][:, :], stat[0][:, :]))
                link(dve, nc.vector.tensor_tensor(acc[:, 0:WIN, 0:D], acc[:, 0:WIN, 0:D], stat[0][:, :].unsqueeze(2).to_broadcast(full), ALU.mult))
                link(dve, nc.vector.tensor_tensor(hs[:, :, :], hs[:, :, :], acc[:, 0:WIN, 0:D], ALU.add))
                nc.vector.tensor_tensor(hs[:, :, :], hs[:, :, :], spread(k.wide["bias_out"][0][:, :]), ALU.add).then_inc(by_act, 1)
                dve.wait_ge(by_act, b + 2)
                for i, t in enumerate((hs[:, :, :], acc[:, 0:WIN, 0:D])):
                    if i:
                        link(dve, nc.vector.tensor_tensor(t, hs[:, :, :], hs[:, :, :], ALU.mult))
                    link(dve, nc.vector.tensor_scalar(t[:, WIN - 1, :], t[:, WIN - 1, :], k.valid[:, :], None, ALU.mult))
                    nc.vector.tensor_reduce(part[:, :], t.rearrange("p w d -> p d w"), AX, ALU.add).then_inc(by_pe, 1)
                    dve.wait_ge(by_pe, p + 2 * i + 2)
                    if i == 0:
                        link(dve, nc.vector.tensor_scalar(mean[:, :], k.psum[0][:, 0:D], 1.0 / NODES, None, ALU.mult))
                        link(dve, nc.vector.tensor_tensor(hs[:, :, :], hs[:, :, :], spread(mean[:, :]), ALU.subtract))
                    else:
                        nc.vector.tensor_scalar(scale[:, :], k.psum[0][:, 0:D], 1.0 / NODES, 1e-5, ALU.mult, ALU.add).then_inc(by_act, 1)
                dve.wait_ge(by_act, b + 4)
                link(dve, nc.vector.reciprocal(scale[:, :], scale[:, :]))
                link(dve, nc.vector.tensor_tensor(scale[:, :], scale[:, :], k.wide["bn_g"][0][:, :], ALU.mult))
                link(dve, nc.vector.tensor_tensor(hs[:, :, :], hs[:, :, :], spread(scale[:, :]), ALU.mult))
                link(dve, nc.vector.tensor_tensor(hs[:, :, :], hs[:, :, :], spread(k.wide["bn_b"][0][:, :]), ALU.add))
                link(dve, nc.vector.tensor_tensor(k.xs[:, :, :], k.xs[:, :, :], hs[:, :, :], ALU.add))

            @block.scalar
            def _(act):
                act.wait_ge(by_act, b + 1)
                nc.scalar.activation(hs[:, :, :], hs[:, :, :], ACT.Gelu).then_inc(by_act, 1)
                act.wait_ge(by_act, b + 3)
                nc.scalar.activation(scale[:, :], scale[:, :], ACT.Sqrt).then_inc(by_act, 1)

            @block.tensor
            def _(pe):
                for i in range(2):
                    pe.wait_ge(by_pe, p + 2 * i + 1)
                    nc.tensor.matmul(k.psum[0][:, 0:D], k.ones[:, :], part[:, :], start=True, stop=True).then_inc(by_pe, 1)
    k.since.passed(4, by_act, by_pe)


def relation_output(k):
    nc, link, acc, stat = k.nc, k.link, k.acc, k.stat
    by_act, by_pe = k.stage["bulk_act"], k.stage["bulk_pe"]
    b, p = k.since(by_act), k.since(by_pe)
    full = [P, WIN, D]
    with ExitStack() as own:
        col, row, top = k.sb(own, "top_col", [P, 1]), k.sb(own, "top_row", [1, 1]), k.sb(own, "top_all", [P, 1])
        with nc.Block() as block:
            @block.vector
            def _(dve):
                nc.vector.tensor_reduce(col[:, :], acc[:, 0:WIN, D + 1], AX, ALU.min).then_inc(by_pe, 1)
                dve.wait_ge(by_pe, p + 2)
                nc.vector.tensor_reduce(row[:, :], k.psum[0][0:1, 0:P], AX, ALU.min).then_inc(by_pe, 1)
                dve.wait_ge(by_pe, p + 4)
                link(dve, nc.vector.tensor_copy(top[:, :], k.psum[1][:, 0:1]))
                link(dve, nc.vector.tensor_scalar(stat[0][:, :], acc[:, 0:WIN, D + 1], -1.0, None, ALU.mult))
                nc.vector.tensor_scalar(stat[0][:, :], stat[0][:, :], top[:, :], 0.0, ALU.add, ALU.min).then_inc(by_act, 1)
                dve.wait_ge(by_act, b + 2)
                link(dve, nc.vector.tensor_tensor(stat[1][:, :], acc[:, 0:WIN, D], stat[0][:, :], ALU.mult))
                link(dve, nc.vector.tensor_scalar(stat[1][:, :], stat[1][:, :], 1e-10, None, ALU.add))
                link(dve, nc.vector.reciprocal(stat[1][:, :], stat[1][:, :]))
                link(dve, nc.vector.tensor_tensor(stat[1][:, :], stat[1][:, :], stat[0][:, :], ALU.mult))
                link(dve, nc.vector.tensor_tensor(acc[:, 0:WIN, 0:D], acc[:, 0:WIN, 0:D],
                                                  stat[1][:, :].unsqueeze(2).to_broadcast(full), ALU.mult))
                link(dve, nc.vector.tensor_tensor(k.hs[:, :, :], k.hs[:, :, :], acc[:, 0:WIN, 0:D], ALU.add))

            @block.scalar
            def _(act):
                act.wait_ge(by_act, b + 1)
                nc.scalar.activation(stat[0][:, :], stat[0][:, :], ACT.Exp).then_inc(by_act, 1)

            @block.tensor
            def _(pe):
                pe.wait_ge(by_pe, p + 1)
                nc.tensor.transpose(k.psum[0][0:1, 0:P], col[:, :], k.ident[:, :]).then_inc(by_pe, 1)
                pe.wait_ge(by_pe, p + 3)
                nc.tensor.matmul(k.psum[1][:, 0:1], k.ones[0:1, :], row[:, :], start=True, stop=True).then_inc(by_pe, 1)
    k.since.passed(2, by_act)
    k.since.passed(4, by_pe)


def store_nodes(k):
    nc, out = k.nc, k.stored
    b = k.since(out)
    with nc.Block() as block:
        @block.sync
        def _(sp):
            sp.dma_start(k.out[0:(WIN - 1) * P, :].rearrange("(w p) d -> p w d", p=P), k.xs[:, 0:WIN - 1, :]).then_inc(out, 16)
            sp.dma_start(k.out[(WIN - 1) * P:NODES, :], k.xs[0:LAST, WIN - 1, :]).then_inc(out, 16)
            sp.wait_ge(out, b + 32)
    k.since.passed(32, out)

_INS = ["x", "src", "dst", "edge_attr_20", "edge_type_64", "edge_weight1", "L0_gnn_W1", "L0_gnn_b1", "L0_gnn_W2",
        "L0_gnn_b2", "L1_gnn_W_in", "L1_gnn_W_f1", "L1_gnn_b_f1", "L1_gnn_W_f2", "L1_gnn_b_f2", "L1_gnn_W_o1",
        "L1_gnn_b_o1", "L1_gnn_W_o2", "L1_gnn_b_o2", "L2_gnn_Wl", "L2_gnn_bl", "L2_gnn_Wr", "L2_gnn_br", "L2_gnn_We",
        "L2_gnn_att", "L2_gnn_bias_out", "L2_gnn_bn_gamma", "L2_gnn_bn_beta", "L3_gnn_rel_embed_weight", "L3_gnn_W"]


def kernel(**inputs):
    import numpy as np
    import concourse.bacc as bacc
    from concourse.bass_utils import run_bass_kernel_spmd

    nc = bacc.Bacc("TRN2", target_bir_lowering=False, num_devices=1)
    arrays, args = {}, []
    for name in _INS:
        a = np.asarray(inputs[name])
        a = np.ascontiguousarray(a.T if name == "L3_gnn_W" else a)
        arrays["in_" + name] = a
        args.append(nc.dram_tensor("in_" + name, a.shape, mybir.dt.from_np(a.dtype), kind="ExternalInput").ap())
    args.append(nc.dram_tensor("out_nodes", (NODES, D), F32, kind="ExternalOutput").ap())
    program(nc, *args)
    r = run_bass_kernel_spmd(nc, [arrays], core_ids=[0])
    return r.results[0]["out_nodes"]
```

```python
from contextlib import ExitStack, nullcontext

import concourse.bass as bass
from concourse import mybir

F32 = mybir.dt.float32
BF16 = mybir.dt.bfloat16
I32 = mybir.dt.int32
ALU = mybir.AluOpType
ACT = mybir.ActivationFunctionType
AX = mybir.AxisListType.X

P = 128
NODES = 6250
D = 128
EDGES = 200000
RBF = 20
NTYPE = 64
LOG2 = 0.6931471805599453

WIN = (NODES + P - 1) // P
WP = WIN + 1
LAST = NODES - (WIN - 1) * P
KG = 4
GE = KG * P
U = 4
NG = (EDGES // GE + 1 + WIN + U - 1) // U * U
T = 10
NCH = (EDGES + GE + P * T - 1) // (P * T)
J = NCH * T
EP = P * J
JC = J // 5
FULL = EDGES // J
REST = EDGES - FULL * J
RW = 24
C_WT, C_SRC, C_DST, C_TYPE = 20, 21, 22, 23
MW = 132
M_SRC, M_DST, M_TYPE = 128, 129, 130
NOWHERE = WP * P
BIG = 2.0 ** 100
LOW = -(2.0 ** 90)
FAR = float(1 << 22)
NL = NG + 5 * U
LOADS = 6
CREDIT = 10
GP = NL // KG


class Since:

    def __init__(self):
        self.counts = {}

    def __call__(self, sem):
        return self.counts.get(sem.name, 0)

    def cleared(self, sems):
        for sem in sems:
            self.counts[sem.name] = 0

    def passed(self, n, *sems):
        for sem in sems:
            self.counts[sem.name] = self(sem) + n


def program(nc, x, src, dst, attr, etype, weight, W1, b1, W2, b2, W_in, W_f1, b_f1, W_f2, b_f2,
            W_o1, b_o1, W_o2, b_o2, Wl, bl, Wr, br, We, att, bias_out, bn_g, bn_b, rel, WT3, out):
    since = Since()
    top = ExitStack()

    def sb(stack, name, shape, dt=F32):
        return stack.enter_context(nc.sbuf_tensor(name, shape, dt))

    def pb(stack, name, shape, dt=F32):
        return stack.enter_context(nc.psum_tensor(name, shape, dt))

    def sem(name, stack=top):
        return stack.enter_context(nc.semaphore(name))

    def dram(name, shape, dt=F32):
        return nc.dram_tensor(name, shape, dt, kind="Internal").ap()

    with top:
        erec = dram("edge_records", [2 * EP, RW])
        epos = dram("edge_positions", [2 * EP, 1], I32)
        tpos = dram("target_positions", [EP, 1], I32)
        mrec = dram("message_records", [EP, MW])
        table3 = dram("split_table", [WP * P, 3 * D], BF16)
        table = dram("node_table", [WP * P, D])
        lists = dram("group_lists", [2, 2, NL], I32)
        bases = dram("group_bases", [2, NL])

        iota_b = sb(top, "iota_b", [P, P], BF16)
        iota_w = sb(top, "iota_w", [P, WP], BF16)
        iota_i = sb(top, "iota_i", [P, P], I32)
        ident = sb(top, "ident", [P, P])
        ident_b = sb(top, "ident_b", [P, P], BF16)
        apart_b = sb(top, "apart_b", [P, P], BF16)
        before_b = sb(top, "before_b", [P, P], BF16)
        ones = sb(top, "ones", [P, P])
        ones_b = sb(top, "ones_b", [P, P], BF16)
        glist = [sb(top, f"glist{o}", [1, 2, NL], I32) for o in range(2)]
        gbase = [sb(top, f"gbase{o}", [P, NL]) for o in range(2)]
        gsame = [sb(top, f"gsame{o}", [P, NL]) for o in range(2)]
        gfresh = [sb(top, f"gfresh{o}", [P, NL]) for o in range(2)]
        weights = {}
        for name, w in dict(W1=W1, W2=W2, W_in=W_in, W_f2=W_f2, W_o1=W_o1, W_o2=W_o2, Wl=Wl, Wr=Wr,
                            WT3=WT3).items():
            weights[name] = sb(top, "w_" + name, [P, D]), w
        w_f1 = sb(top, "w_f1", [RBF, D])
        rows = {}
        for name, b in dict(b1=b1, b2=b2, b_o1=b_o1, b_o2=b_o2, bl=bl, br=br).items():
            rows[name] = sb(top, "row_" + name, [1, D]), b
        wide = {}
        for name, b in dict(b_f2=b_f2, We=We, att=att, bias_out=bias_out, bn_g=bn_g, bn_b=bn_b).items():
            wide[name] = sb(top, "wide_" + name, [P, D]), b
        bf1 = sb(top, "bf1", [P, 1])
        rel_f = sb(top, "rel_f", [NTYPE, D])
        rel3 = sb(top, "rel3", [NTYPE, 3 * D], BF16)
        relr = sb(top, "relr", [NTYPE, D])

        loaded, made, cast, chain, stored = (sem(n) for n in ("loaded", "made", "cast", "chain", "stored"))
        linked = [0]

        def link(eng, ins):
            linked[0] += 1
            ins.then_inc(chain, 1)
            eng.wait_ge(chain, linked[0])

        n_loads = len(weights) + len(rows) + len(wide) + 3
        with nc.Block() as block:
            @block.sync
            def _(sp):
                for t, w in weights.values():
                    sp.dma_start(t[:, :], w).then_inc(loaded, 16)
                for t, b in rows.values():
                    sp.dma_start(t[:, :], b.rearrange("(a n) -> a n", a=1)).then_inc(loaded, 16)
                for t, b in wide.values():
                    b = b if len(b.shape) == 2 else b.rearrange("(a n) -> a n", a=1)
                    sp.dma_start(t[:, :], b.broadcast_to([P, D])).then_inc(loaded, 16)
                sp.dma_start(w_f1[:, :], W_f1).then_inc(loaded, 16)
                sp.dma_start(bf1[:, :], b_f1.rearrange("(n a) -> n a", a=1)).then_inc(loaded, 16)
                sp.dma_start(rel_f[:, :], rel).then_inc(loaded, 16)
                sp.wait_ge(loaded, 16 * n_loads)

            @block.gpsimd
            def _(pool):
                pool.iota(iota_i[:, :], pattern=[[1, P]], base=0, channel_multiplier=0).then_inc(made, 1)
                pool.memset(ident[:, :], 0.0).then_inc(made, 1)
                pool.memset(before_b[:, :], 1.0).then_inc(made, 1)
                pool.wait_ge(made, 3)
                pool.affine_select(out=ident[:, :], in_=ident[:, :], compare_op=ALU.not_equal, fill=1.0,
                                   base=0, pattern=[[-1, P]], channel_multiplier=1).then_inc(made, 1)
                pool.affine_select(out=before_b[:, :], in_=before_b[:, :], compare_op=ALU.is_ge, fill=0.0,
                                   base=-1, pattern=[[1, P]], channel_multiplier=-1).then_inc(made, 1)

            @block.vector
            def _(dve):
                dve.wait_ge(made, 5)
                nc.vector.tensor_copy(iota_b[:, :], iota_i[:, :]).then_inc(cast, 1)
                nc.vector.tensor_copy(iota_w[:, :], iota_i[:, 0:WP]).then_inc(cast, 1)
                nc.vector.tensor_copy(ident_b[:, :], ident[:, :]).then_inc(cast, 1)
                nc.vector.tensor_scalar(apart_b[:, :], ident[:, :], BIG, -BIG, ALU.mult, ALU.add).then_inc(cast, 1)
                nc.vector.memset(ones[:, :], 1.0).then_inc(cast, 1)
                nc.vector.memset(ones_b[:, :], 1.0).then_inc(cast, 1)
                dve.wait_ge(loaded, 16 * n_loads)
                split3(nc, lambda ins: link(dve, ins), rel3[:, 0:D], rel3[:, D:2 * D], rel3[:, 2 * D:3 * D],
                       rel_f[:, :], relr[:, :])

        k = Kit()
        k.nc, k.since, k.link, k.chain, k.linked, k.sem, k.sb, k.pb = nc, since, link, chain, linked, sem, sb, pb
        k.x, k.out = x, out
        k.src, k.dst, k.attr, k.etype, k.weight = src, dst, attr, etype, weight
        k.erec, k.epos, k.tpos, k.mrec, k.table3, k.table, k.lists, k.bases = erec, epos, tpos, mrec, table3, table, lists, bases
        k.iota_b, k.iota_w, k.ident, k.ident_b, k.apart_b = iota_b, iota_w, ident, ident_b, apart_b
        k.before_b, k.ones, k.ones_b, k.glist, k.gbase = before_b, ones, ones_b, glist, gbase
        k.gsame, k.gfresh = gsame, gfresh
        k.weights, k.rows, k.wide, k.w_f1, k.bf1, k.rel3 = weights, rows, wide, w_f1, bf1, rel3
        k.banks = pb(top, "banks", [P, 8, 512])
        k.psum = [k.banks[:, i, :] for i in range(8)]
        pack_edges(k)
        k.xs = sb(top, "xs", [P, WIN, D])
        k.hs = sb(top, "hs", [P, WIN, D])
        k.acc = sb(top, "acc", [P, WP, MW])
        k.near = sb(top, "near", [P, WP, 3 * D], BF16)
        k.staging, k.staging_t = sb(top, "staging", [P, TILES * D]), sb(top, "staging_t", [P, TILES * D])
        k.stat = [sb(top, f"stat{i}", [P, WIN]) for i in range(2)]
        k.top, k.stored, k.begun, k.loading = top, stored, sem("begun"), sem("loading")
        k.stage = {n: sem(n) for n in (
            "staged", "turned", "turned_sb", "multiplied", "epilogued", "bulk_act", "bulk_pe",
            "rel_ready", "onehot_ready", "onehot_turned", "onehotT_ready", "summed", "added",
            "attr_turned", "attrT_ready", "hidden_ready", "size_ready", "exps_ready", "logs_ready", "positive_ready",
            "soft_ready", "off_ready",
            "filter_ready", "far_ready", "biased", "message_ready", "index_ready",
            "edge_term", "near_ready", "in1", "in2", "in3", "edge_dot", "scores", "spread", "group_max", "kinds_ready", "kept",
            "exp_in", "weighed", "shrink", "prob_turned", "prob_ready")}
        k.rows_in = [sem(f"rows_in{u}") for u in range(U)]
        k.pool_done = [sem(f"pool_done{u}") for u in range(U)]

        load_nodes(k)
        layernorm_relu(k)
        publish(k, k.hs, True)
        segment_sums(k, 0)
        node_product(k, "W1", "b1", k.hs, k.hs, "relu", add=k.acc)
        node_product(k, "W2", "b2", k.hs, k.xs, "add")

        layernorm_relu(k)
        node_product(k, "W_in", None, k.hs, k.hs, "copy")
        split_near(k, k.hs)
        clear(k)
        filter_messages(k)
        clear(k)
        segment_sums(k, 1)
        node_product(k, "W_o1", "b_o1", k.acc, k.hs, "copy")
        shifted_softplus(k)
        node_product(k, "W_o2", "b_o2", k.hs, k.xs, "add")

        layernorm_relu(k)
        with nc.sbuf_tensor("right", [P, WIN, D], F32) as right:
            node_product(k, "Wl", "bl", k.hs, right, "copy")
            publish(k, right, False)
            node_product(k, "Wr", "br", k.hs, right, "copy")
            split_near(k, right)
        clear(k)
        attention(k, 0)
        clear(k)
        gat_output(k)

        layernorm_relu(k)
        publish(k, k.hs, False)
        split_near(k, k.hs)
        clear(k)
        attention(k, 1)
        relation_output(k)
        node_product(k, "WT3", None, k.hs, k.xs, "leaky")
        store_nodes(k)


class Kit:
    pass


def split3(nc, link, hi, mid, lo, source, rest):
    link(nc.vector.tensor_copy(hi, source))
    link(nc.vector.tensor_tensor(rest, source, hi, ALU.subtract))
    link(nc.vector.tensor_copy(mid, rest))
    link(nc.vector.tensor_tensor(rest, rest, mid, ALU.subtract))
    link(nc.vector.tensor_copy(lo, rest))


def pack_edges(k):
    nc, link, sem, sb = k.nc, k.link, k.sem, k.sb
    with ExitStack() as own:
        ends = [sb(own, n, [P, J], I32) for n in ("e_src", "e_dst", "e_type")]
        e_wt = sb(own, "e_wt", [P, J])
        win_i = sb(own, "win_i", [P, J], I32)
        win = [sb(own, f"win{o}", [P, J + 2 * T], BF16) for o in range(2)]
        at = sb(own, "at", [P, 2, JC * RBF])
        rec = sb(own, "rec", [P, 2, JC * RW])
        cleared, ends_in, packed = sem("cleared"), sem("ends_in"), sem("packed")
        attr_in = [sem(f"attr_in{s}") for s in range(2)]
        rec_out = [sem(f"rec_out{s}") for s in range(2)]
        pads = (WIN * P, NOWHERE, 0)
        nchunk = J // JC

        def split_pad(t, view, width, c0, n):
            pairs = [(t[0:FULL, 0:n * width], view[0:FULL * J * width]
                      .rearrange("(p j) -> p j", p=FULL)[:, c0 * width:(c0 + n) * width])]
            m = max(0, min(n, REST - c0))
            if m:
                lo = (FULL * J + c0) * width
                pairs.append((t[FULL:FULL + 1, 0:m * width],
                              view[lo:lo + m * width].rearrange("(a j) -> a j", a=1)))
            return pairs

        flats = [k.src, k.dst, k.etype]
        attr_flat = k.attr.rearrange("e r -> (e r)")
        n_ends = len(split_pad(e_wt, k.weight.rearrange("e a -> (e a)"), 1, 0, J)) * 4

        with nc.Block() as block:
            @block.sync
            def _(sp):
                sp.wait_ge(cleared, 6)
                for t, v in zip(ends + [e_wt], flats + [k.weight.rearrange("e a -> (e a)")]):
                    for to, of in split_pad(t, v, 1, 0, J):
                        sp.dma_start(to, of).then_inc(ends_in, 16)
                out_view = k.erec[0:EP, :].rearrange("(p j) c -> p (j c)", p=P)
                count = [0, 0]
                for c in range(nchunk):
                    if c >= 2:
                        sp.wait_ge(packed, c - 1)
                    for to, of in split_pad(at[:, c % 2, :], attr_flat, RBF, c * JC, JC):
                        sp.dma_start(to, of).then_inc(attr_in[c % 2], 16)
                    if c >= 1:
                        sp.wait_ge(packed, c)
                        sp.dma_start(out_view[:, (c - 1) * JC * RW:c * JC * RW],
                                     rec[:, (c - 1) % 2, :]).then_inc(rec_out[(c - 1) % 2], 16)
                sp.wait_ge(packed, nchunk)
                sp.dma_start(out_view[:, (nchunk - 1) * JC * RW:], rec[:, (nchunk - 1) % 2, :])\
                    .then_inc(rec_out[(nchunk - 1) % 2], 16)
                for s in range(2):
                    sp.wait_ge(rec_out[s], 16 * len(range(s, nchunk, 2)))

            @block.vector
            def _(dve):
                for t, pad in zip(ends, pads):
                    nc.vector.memset(t[:, :], pad).then_inc(cleared, 1)
                nc.vector.memset(e_wt[:, :], 0.0).then_inc(cleared, 1)
                nc.vector.memset(at[:, :, :], 0.0).then_inc(cleared, 1)
                nc.vector.memset(rec[:, :, :], 0.0).then_inc(cleared, 1)
                dve.wait_ge(ends_in, 16 * n_ends)
                for o, t in ((0, ends[1]), (1, ends[0])):
                    link(dve, nc.vector.tensor_scalar(win_i[:, :], t[:, :], 7, None, ALU.logical_shift_right))
                    link(dve, nc.vector.tensor_copy(win[o][:, 0:J], win_i[:, :]))
                    link(dve, nc.vector.memset(win[o][:, J:], float(WIN)))
                arrived = [0, 0]
                for c in range(nchunk):
                    s = c % 2
                    arrived[s] += 16 * len(split_pad(at[:, s, :], attr_flat, RBF, c * JC, JC))
                    dve.wait_ge(attr_in[s], arrived[s])
                    if c >= 2:
                        dve.wait_ge(rec_out[s], 16 * (c // 2))
                    r = rec[:, s, :].rearrange("p (j c) -> p j c", c=RW)
                    ri = r.bitcast(I32)
                    cols = slice(c * JC, (c + 1) * JC)
                    link(dve, nc.vector.tensor_copy(r[:, :, 0:RBF], at[:, s, :].rearrange("p (j c) -> p j c", c=RBF)))
                    link(dve, nc.vector.tensor_copy(r[:, :, C_WT], e_wt[:, cols]))
                    link(dve, nc.vector.tensor_copy(ri[:, :, C_SRC], ends[0][:, cols]))
                    link(dve, nc.vector.tensor_copy(ri[:, :, C_DST], ends[1][:, cols]))
                    nc.vector.tensor_copy(ri[:, :, C_TYPE], ends[2][:, cols]).then_inc(packed, 1)
                    dve.wait_ge(packed, c + 1)

        hot = sb(own, "hot", [P, 2, T, WP], BF16)
        count = [sb(own, f"count{o}", [P, WP]) for o in range(2)]
        hot_ready, hot_used, counted = sem("hot_ready"), sem("hot_used"), sem("counted")
        first = [sb(own, f"first{o}", [P, WP]) for o in range(2)]

        def one_hot(o, col, s):
            return nc.vector.tensor_tensor(
                hot[:, s, :, :], win[o][:, col].unsqueeze(2).to_broadcast([P, T, WP]),
                k.iota_w[:, :].unsqueeze(1).to_broadcast([P, T, WP]), ALU.is_equal)

        cols = lambda ch: bass.ds(ch * T, T)
        for o in range(2):
            with nc.Block() as block:
                @block.vector
                def _(dve):
                    h0 = k.since(hot_used)
                    for s in range(2):
                        one_hot(o, cols(s), s).then_inc(hot_ready, 1)
                    with dve.Fori(2, NCH - 1, 2) as c:
                        for s in range(2):
                            dve.wait_ge(hot_used, h0 + c + (s - 1))
                            one_hot(o, cols(c + s), s).then_inc(hot_ready, 1)
                    dve.wait_ge(hot_used, h0 + NCH - 2)
                    one_hot(o, cols(NCH - 1), 0).then_inc(hot_ready, 1)
                    dve.wait_ge(hot_used, h0 + NCH)
                    nc.vector.tensor_reduce(count[o][:, :], k.psum[0][:, 0:T * WP].rearrange("p (t w) -> p w t", w=WP),
                                            AX, ALU.add).then_inc(counted, 1)
                    dve.wait_ge(counted, o + 1)

                @block.tensor
                def _(pe):
                    h0 = k.since(hot_ready)

                    def add(s, **f):
                        return nc.tensor.matmul(k.psum[0][:, 0:T * WP], k.ones_b[:, :],
                                                hot[:, s, :, :].rearrange("p t w -> p (t w)"), **f)
                    pe.wait_ge(hot_ready, h0 + 1)
                    add(0, start=True, stop=False).then_inc(hot_used, 1)
                    pe.wait_ge(hot_ready, h0 + 2)
                    add(1, start=False, stop=False).then_inc(hot_used, 1)
                    with pe.Fori(2, NCH - 1, 2) as c:
                        for s in range(2):
                            pe.wait_ge(hot_ready, h0 + c + (s + 1))
                            add(s, start=False, stop=False).then_inc(hot_used, 1)
                    pe.wait_ge(hot_ready, h0 + NCH)
                    add(0, start=False, stop=True).then_inc(hot_used, 1)
            k.since.passed(NCH, hot_ready, hot_used)

        drops, dropped = sb(own, "drops", [P, J - 1], BF16), sb(own, "dropped", [P, 2])
        mixed, mixed_i = sb(own, "mixed", [P, 1]), sb(own, "mixed_i", [P, 1], I32)
        turned_up, found = sem("turned_up"), sem("found")
        with nc.Block() as block:
            @block.tensor
            def _(pe):
                nc.tensor.matmul(k.psum[0][0:P - 1, 0:1], k.ident_b[:, 1:P], win[0][:, 0:1], start=True, stop=True)\
                    .then_inc(turned_up, 1)
                pe.wait_ge(found, 1)
                nc.tensor.matmul(k.psum[1][:, 0:2], k.ones[:, :], dropped[:, :], start=True, stop=True).then_inc(turned_up, 1)

            @block.vector
            def _(dve):
                link(dve, nc.vector.tensor_tensor(drops[:, :], win[0][:, 0:J - 1], win[0][:, 1:J], ALU.is_gt))
                link(dve, nc.vector.memset(dropped[:, :], 0.0))
                link(dve, nc.vector.tensor_reduce(dropped[:, 0:1], drops[:, :], AX, ALU.max))
                dve.wait_ge(turned_up, 1)
                link(dve, nc.vector.tensor_tensor(dropped[0:P - 1, 1:2], win[0][0:P - 1, J - 1:J], k.psum[0][0:P - 1, 0:1],
                                                  ALU.is_gt))
                dve.sem_inc(found, 1)
                dve.wait_ge(turned_up, 2)
                link(dve, nc.vector.tensor_reduce(mixed[:, :], k.psum[1][:, 0:2], AX, ALU.max))
                link(dve, nc.vector.tensor_scalar(mixed[:, :], mixed[:, :], 1.0, None, ALU.min))
                link(dve, nc.vector.tensor_copy(mixed_i[:, :], mixed[:, :]))

        a = [sb(own, f"scan{i}", [P, WP]) for i in range(2)]
        groups, groups_i = sb(own, "groups", [P, WP]), sb(own, "groups_i", [P, WP], I32)
        gi_i, gi = sb(own, "gi_i", [GP, KG], I32), sb(own, "gi", [GP, KG])
        past = sb(own, "past", [GP, KG, WIN])
        took = sb(own, "took", [GP, KG, WIN])
        gw, gs = [sb(own, f"gw{o}", [GP, KG]) for o in range(2)], [sb(own, f"gs{o}", [GP, KG]) for o in range(2)]
        gw_i, gs_i = [sb(own, f"gwi{o}", [GP, KG], I32) for o in range(2)], [sb(own, f"gsi{o}", [GP, KG], I32) for o in range(2)]
        gb = [sb(own, f"gb{o}", [GP, KG]) for o in range(2)]
        run = sb(own, "run", [P, WP])
        numbered, listed, list_out, list_in = sem("numbered"), sem("listed"), sem("list_out"), sem("list_in")

        def scan(dve, source, n):
            cur, other = source, 0
            step = 1
            while step < n:
                nxt = a[other]
                link(dve, nc.vector.tensor_copy(nxt[:, 0:step], cur[:, 0:step]))
                link(dve, nc.vector.tensor_tensor(nxt[:, step:n], cur[:, step:n], cur[:, 0:n - step], ALU.add))
                cur, other, step = nxt, 1 - other, 2 * step
            return cur

        with nc.Block() as block:
            @block.gpsimd
            def _(pool):
                pool.iota(gi_i[:, :], pattern=[[1, KG]], base=0, channel_multiplier=KG).then_inc(numbered, 1)

            @block.vector
            def _(dve):
                dve.wait_ge(numbered, 1)
                link(dve, nc.vector.tensor_copy(gi[:, :], gi_i[:, :]))
                for o in range(2):
                    ends_at = scan(dve, count[o], WP)
                    link(dve, nc.vector.tensor_tensor(first[o][:, :], ends_at[:, 0:WP], count[o][:, :], ALU.subtract))
                    link(dve, nc.vector.tensor_scalar(groups_i[:, :], count[o][:, :], float(GE - 1), None, ALU.add))
                    link(dve, nc.vector.tensor_scalar(groups_i[:, :], groups_i[:, :], GE.bit_length() - 1, None,
                                                      ALU.logical_shift_right))
                    link(dve, nc.vector.tensor_copy(groups[:, :], groups_i[:, :]))
                    upto = scan(dve, groups, WIN)
                    link(dve, nc.vector.tensor_tensor(past[:, :, :], gi[:, :].unsqueeze(2).to_broadcast([GP, KG, WIN]),
                                                      upto[0:GP, 0:WIN].unsqueeze(1).to_broadcast([GP, KG, WIN]), ALU.is_ge))
                    link(dve, nc.vector.tensor_reduce(gw[o][:, :], past[:, :, :], AX, ALU.add))
                    link(dve, nc.vector.scalar_tensor_tensor(groups[:, 0:WIN], groups[:, 0:WIN], -float(GE),
                                                             count[o][:, 0:WIN], ALU.mult, ALU.add))
                    link(dve, nc.vector.tensor_tensor(took[:, :, :], past[:, :, :],
                                                      groups[0:GP, 0:WIN].unsqueeze(1).to_broadcast([GP, KG, WIN]), ALU.mult))
                    link(dve, nc.vector.tensor_reduce(gs[o][:, :], took[:, :, :], AX, ALU.add))
                    link(dve, nc.vector.scalar_tensor_tensor(gs[o][:, :], gi[:, :], float(GE), gs[o][:, :], ALU.mult, ALU.add))
                    link(dve, nc.vector.tensor_scalar(gs[o][:, :], gs[o][:, :], float(EDGES), None, ALU.min))
                    if o == 0:
                        link(dve, nc.vector.scalar_tensor_tensor(gs[o][:, :], mixed[0:GP, :].to_broadcast([GP, KG]), float(EP),
                                                                 gs[o][:, :], ALU.mult, ALU.add))
                    link(dve, nc.vector.tensor_copy(gs_i[o][:, :], gs[o][:, :]))
                    link(dve, nc.vector.tensor_copy(gw_i[o][:, :], gw[o][:, :]))
                    link(dve, nc.vector.tensor_scalar(gb[o][:, :], gw[o][:, :], float(P), None, ALU.mult))
                dve.sem_inc(listed, 1)

            @block.sync
            def _(sp):
                sp.wait_ge(listed, 1)
                for o in range(2):
                    for i, t in enumerate((gw_i[o], gs_i[o])):
                        sp.dma_start(k.lists[o, i, :].rearrange("(p q) -> p q", p=GP), t[:, :]).then_inc(list_out, 16)
                    sp.dma_start(k.bases[o, :].rearrange("(p q) -> p q", p=GP), gb[o][:, :]).then_inc(list_out, 16)
                sp.wait_ge(list_out, 96)
                for o in range(2):
                    sp.dma_start(k.glist[o][:, :, :], k.lists[o, :, :].rearrange("(a i) g -> a i g", a=1)).then_inc(list_in, 16)
                    sp.dma_start(k.gbase[o][:, :], k.bases[o:o + 1, :].broadcast_to([P, NL])).then_inc(list_in, 16)
                sp.wait_ge(list_in, 64)

        with nc.Block() as block:
            @block.vector
            def _(dve):
                for o in range(2):
                    base, same = k.gbase[o], k.gsame[o]
                    link(dve, nc.vector.memset(same[:, 0:1], 0.0))
                    link(dve, nc.vector.tensor_tensor(same[:, 1:], base[:, 1:], base[:, 0:NL - 1], ALU.is_equal))
                    link(dve, nc.vector.tensor_scalar(k.gfresh[o][:, :], same[:, :], -BIG, BIG, ALU.mult, ALU.add))

        pos = sb(own, "pos", [P, J])
        pos_i = sb(own, "pos_i", [P, J], I32)
        place = sb(own, "place", [P, 2, T, WP])

        def if_mixed(eng):
            return eng.If(eng.value_load(mixed_i[0:1, 0:1], min_val=0, max_val=1) > 0)

        def positions(o, to, when):
            ready, ranked, placed, based, own_place, reduced, pos_ready, pos_out = (
                sem(f"{n}{o}") for n in ("window_hot", "ranked", "placed", "based", "own_place", "reduced", "pos_ready",
                                         "pos_out"))
            with nc.Block() as block:
                @block.vector
                def _(dve):
                    def rank(c, s):
                        dve.wait_ge(ranked, c + (s + 1))
                        dve.wait_ge(based, c + (s + 2))
                        nc.vector.tensor_tensor(place[:, s, :, :], k.psum[2 * s][:, 0:T * WP].rearrange("p (t w) -> p t w", w=WP),
                                                run[:, :].unsqueeze(1).to_broadcast([P, T, WP]), ALU.add).then_inc(placed, 1)
                        dve.wait_ge(placed, c + (s + 1))
                        nc.vector.tensor_tensor(run[:, :], run[:, :], k.psum[2 * s + 1][:, 0:WP], ALU.add).then_inc(based, 1)
                        dve.wait_ge(ready, c + (s + 1))
                        nc.vector.tensor_tensor(place[:, s, :, :], place[:, s, :, :], hot[:, s, :, :], ALU.mult)\
                            .then_inc(own_place, 1)
                        dve.wait_ge(own_place, c + (s + 1))
                        nc.vector.tensor_reduce(pos[:, cols(c + s)], place[:, s, :, :], AX, ALU.add).then_inc(reduced, 1)

                    with when(dve):
                        nc.vector.tensor_copy(run[:, :], first[o][:, :]).then_inc(based, 2)
                        for s in range(2):
                            one_hot(o, cols(s), s).then_inc(ready, 1)
                        with dve.Fori(0, NCH - 1, 2) as c:
                            for s in range(2):
                                rank(c, s)
                                one_hot(o, cols(c + (s + 2)), s).then_inc(ready, 1)
                        rank(NCH - 1, 0)
                        dve.wait_ge(reduced, NCH)
                        if o == 0:
                            nc.vector.tensor_scalar(pos[:, :], pos[:, :], float(EP), None, ALU.add).then_inc(reduced, 1)
                            dve.wait_ge(reduced, NCH + 1)
                            nc.vector.tensor_scalar(away[:, :], win[0][:, 0:J], float(WIN), FAR, ALU.is_ge, ALU.mult)\
                                .then_inc(reduced, 1)
                            dve.wait_ge(reduced, NCH + 2)
                            nc.vector.tensor_tensor(pos[:, :], pos[:, :], away[:, :], ALU.add).then_inc(reduced, 1)
                            dve.wait_ge(reduced, NCH + 3)
                        nc.vector.tensor_copy(pos_i[:, :], pos[:, :]).then_inc(pos_ready, 1)

                @block.tensor
                def _(pe):
                    def rank(c, s):
                        pe.wait_ge(ready, c + (s + 1))
                        pe.wait_ge(based, c + (s + 1))
                        f = hot[:, s, :, :].rearrange("p t w -> p (t w)")
                        nc.tensor.matmul(k.psum[2 * s][:, 0:T * WP], k.before_b[:, :], f, start=True, stop=False)
                        for t in range(T - 1):
                            n = T - 1 - t
                            nc.tensor.matmul(k.psum[2 * s][:, (t + 1) * WP:T * WP].rearrange("p (t w) -> p t w", w=WP),
                                             k.ones_b[:, :], hot[:, s, t:t + 1, :].to_broadcast([P, n, WP]),
                                             start=False, stop=t == T - 2)
                        for t in range(T):
                            last = nc.tensor.matmul(k.psum[2 * s + 1][:, 0:WP], k.ones_b[:, :], hot[:, s, t, :],
                                                    start=t == 0, stop=t == T - 1)
                        last.then_inc(ranked, 1)

                    with when(pe):
                        with pe.Fori(0, NCH - 1, 2) as c:
                            for s in range(2):
                                rank(c, s)
                        rank(NCH - 1, 0)

                @block.sync
                def _(sp):
                    with when(sp):
                        sp.wait_ge(pos_ready, 1)
                        sp.dma_start(to.rearrange("(p j) a -> p (j a)", p=P), pos_i[:, :]).then_inc(pos_out, 16)
                        sp.wait_ge(pos_out, 16)

        positions(1, k.epos[0:EP, :], lambda eng: nullcontext())
        away = at[:, :, :].rearrange("p s n -> p (s n)")[:, 0:J]
        positions(0, k.tpos, if_mixed)

        part, part_to, part_pos = sb(own, "part", [P, T, RW]), sb(own, "part_to", [P, T], I32), sb(own, "part_pos", [P, T, 1], I32)
        pads_out, part_in, part_out, part_free, scattering = (
            sem(n) for n in ("pads_out", "part_in", "part_out", "part_free", "scattering"))
        with nc.Block() as block:
            @block.sync
            def _(sp):
                with if_mixed(sp):
                    for t in (k.erec, k.epos):
                        sp.dma_start(t[EP + EDGES:2 * EP, :], t[EDGES:EP, :]).then_inc(pads_out, 16)
                    with sp.Fori(0, NCH, 1) as c:
                        sp.wait_ge(part_free, c + 1)
                        for to, of, width in ((part[:, :, :].rearrange("p t c -> p (t c)"), k.erec[0:EP, :], RW),
                                              (part_to[:, :], k.tpos, 1),
                                              (part_pos[:, :, :].rearrange("p t c -> p (t c)"), k.epos[0:EP, :], 1)):
                            sp.dma_start(to, of.rearrange("(p j) c -> p (j c)", p=P)[:, bass.ds(c * (T * width), T * width)])\
                                .then_inc(part_in, 16)
                    sp.wait_ge(pads_out, 32)

            @block.gpsimd
            def _(pool):
                with if_mixed(pool):
                    pool.sem_inc(part_free, 1)
                    with pool.Fori(0, NCH, 1) as c:
                        pool.wait_ge(part_in, c * 48 + 48)
                        pool.sem_inc(scattering, 1)
                        for t in range(T):
                            for to, of in ((k.erec, part[:, t, :]), (k.epos, part_pos[:, t, :])):
                                pool.indirect_dma_start(to[:, :], bass.IndirectOffsetOnAxis(ap=part_to[:, t:t + 1], axis=0),
                                                        of, None, bounds_check=2 * EP - 1, oob_is_err=False)\
                                    .then_inc(part_out, 16)
                        pool.wait_ge(part_out, c * (2 * T * 16) + 2 * T * 16)
                        pool.sem_inc(part_free, 1)



def load_nodes(k):
    nc, link, xs = k.nc, k.link, k.xs
    zeroed, x_in = k.sem("zeroed"), k.sem("x_in")
    k.valid = k.sb(k.top, "valid", [P, 1])
    valid_i = k.sb(k.top, "valid_i", [P, 1], I32)
    with nc.Block() as block:
        @block.vector
        def _(dve):
            nc.vector.memset(xs[:, WIN - 1, :], 0.0).then_inc(zeroed, 1)
            dve.wait_ge(x_in, 1)
            link(dve, nc.vector.tensor_copy(k.valid[:, :], valid_i[:, :]))
            link(dve, nc.vector.tensor_scalar(k.valid[:, :], k.valid[:, :], float(LAST), None, ALU.is_lt))
            link(dve, nc.vector.memset(k.near[:, WIN, :], 0.0))

        @block.gpsimd
        def _(pool):
            pool.iota(valid_i[:, :], pattern=[[0, 1]], base=0, channel_multiplier=1).then_inc(x_in, 1)

        @block.sync
        def _(sp):
            sp.wait_ge(zeroed, 1)
            sp.wait_ge(x_in, 1)
            sp.dma_start(xs[:, 0:WIN - 1, :], k.x[0:(WIN - 1) * P, :].rearrange("(w p) d -> p w d", p=P)).then_inc(x_in, 16)
            sp.dma_start(xs[0:LAST, WIN - 1, :], k.x[(WIN - 1) * P:NODES, :]).then_inc(x_in, 16)
            sp.wait_ge(x_in, 33)


def layernorm_relu(k):
    nc, link, xs, hs = k.nc, k.link, k.xs, k.hs
    sq = k.acc[:, 0:WIN, 0:D]
    stat = k.stat
    by_act = k.stage["bulk_act"]
    b = k.since(by_act)
    with nc.Block() as block:
        @block.vector
        def _(dve):
            link(dve, nc.vector.tensor_reduce(stat[0][:, :], xs[:, :, :], AX, ALU.add))
            link(dve, nc.vector.tensor_scalar(stat[0][:, :], stat[0][:, :], 1.0 / D, None, ALU.mult))
            link(dve, nc.vector.tensor_tensor(hs[:, :, :], xs[:, :, :], stat[0][:, :].unsqueeze(2).to_broadcast([P, WIN, D]),
                                              ALU.subtract))
            link(dve, nc.vector.tensor_tensor(sq, hs[:, :, :], hs[:, :, :], ALU.mult))
            link(dve, nc.vector.tensor_reduce(stat[1][:, :], sq, AX, ALU.add))
            nc.vector.tensor_scalar(stat[1][:, :], stat[1][:, :], 1.0 / D, 1e-5, ALU.mult, ALU.add).then_inc(by_act, 1)
            dve.wait_ge(by_act, b + 2)
            link(dve, nc.vector.reciprocal(stat[1][:, :], stat[1][:, :]))
            link(dve, nc.vector.scalar_tensor_tensor(hs[:, :, :], hs[:, :, :], 0.0,
                                                     stat[1][:, :].unsqueeze(2).to_broadcast([P, WIN, D]), ALU.max, ALU.mult))

        @block.scalar
        def _(act):
            act.wait_ge(by_act, b + 1)
            nc.scalar.activation(stat[1][:, :], stat[1][:, :], ACT.Sqrt).then_inc(by_act, 1)
    k.since.passed(2, by_act)


def split_near(k, t):
    nc = k.nc
    with nc.Block() as block:
        @block.vector
        def _(dve):
            parts = [k.near[:, 0:WIN, i * D:(i + 1) * D] for i in range(3)]
            split3(nc, lambda ins: k.link(dve, ins), *parts, t[:, :, :], k.acc[:, 0:WIN, 0:D])


def publish(k, t, split):
    nc = k.nc
    if split:
        split_near(k, t)
    out = k.stored
    b = k.since(out)
    with nc.Block() as block:
        @block.sync
        def _(sp):
            if split:
                sp.dma_start(k.table3.rearrange("(w p) c -> p w c", p=P), k.near[:, :, :]).then_inc(out, 16)
                sp.wait_ge(out, b + 16)
            else:
                sp.dma_start(k.table[0:WIN * P, :].rearrange("(w p) c -> p w c", p=P), t[:, :, :]).then_inc(out, 16)
                sp.dma_start(k.table[WIN * P:WP * P, :], k.ones[:, :]).then_inc(out, 16)
                sp.wait_ge(out, b + 32)
    k.since.passed(16 if split else 32, out)


TILES = 7


def node_product(k, W, bias, src, dst, how, add=None):
    assert WIN % TILES == 0
    nc, n = k.nc, TILES * D
    staged, turned, turned_sb, multiplied, epilogued = (k.stage[x] for x in ("staged", "turned", "turned_sb", "multiplied", "epilogued"))
    s, t, ts, m, e = (k.since(x) for x in (staged, turned, turned_sb, multiplied, epilogued))
    all_banks = k.banks[:, :, :].rearrange("p b c -> p (b c)")
    w_sb = k.weights[W][0]
    row = k.rows[bias][0] if bias else None
    turns = WIN // TILES
    with nc.Block() as block:
        @block.vector
        def _(dve):
            dve.sem_inc(epilogued, 1)
            with dve.Fori(0, turns) as i:
                win = bass.ds(i * TILES, TILES)
                st = k.staging[:, :].rearrange("p (w d) -> p w d", d=D)
                dve.wait_ge(epilogued, e + 1 + i * 2)
                if add is None:
                    nc.vector.tensor_scalar(st, src[:, win, 0:D], 1.0, None, ALU.mult).then_inc(staged, 1)
                else:
                    nc.vector.tensor_tensor(st, src[:, win, 0:D], add[:, win, 0:D], ALU.add).then_inc(staged, 1)
                ps = all_banks[:, 1024:1024 + n].rearrange("p (w d) -> p w d", d=D)
                dve.wait_ge(multiplied, m + i + 1)
                if how == "relu":
                    nc.vector.tensor_scalar(dst[:, win, :], ps, 0.0, None, ALU.max).then_inc(epilogued, 2)
                elif how == "copy":
                    nc.vector.tensor_scalar(dst[:, win, :], ps, 1.0, None, ALU.mult).then_inc(epilogued, 2)
                elif how == "add":
                    nc.vector.tensor_tensor(dst[:, win, :], ps, dst[:, win, :], ALU.add).then_inc(epilogued, 2)
                else:
                    nc.vector.tensor_scalar(st, ps, 0.2, None, ALU.mult).then_inc(epilogued, 1)
                    dve.wait_ge(epilogued, e + i * 2 + 2)
                    nc.vector.tensor_tensor(st, st, ps, ALU.max).then_inc(k.stage["bulk_pe"], 1)
                    dve.wait_ge(k.stage["bulk_pe"], k.since(k.stage["bulk_pe"]) + i + 1)
                    nc.vector.tensor_tensor(dst[:, win, :], st, dst[:, win, :], ALU.add).then_inc(epilogued, 1)
            dve.wait_ge(epilogued, e + 1 + 2 * turns)

        @block.tensor
        def _(pe):
            with pe.Fori(0, turns) as i:
                pe.wait_ge(staged, s + i + 1)
                for w in range(TILES):
                    last = nc.tensor.transpose(all_banks[:, w * D:(w + 1) * D], k.staging[:, w * D:(w + 1) * D], k.ident[:, :])
                last.then_inc(turned, 1)
                pe.wait_ge(turned_sb, ts + i + 1)
                for w in range(TILES):
                    o = all_banks[:, 1024 + w * D:1024 + (w + 1) * D]
                    last = nc.tensor.matmul(o, k.staging_t[:, w * D:(w + 1) * D], w_sb[:, :], start=True, stop=row is None)
                    if row is not None:
                        last = nc.tensor.matmul(o, k.ones[0:1, :], row[:, :], start=False, stop=True)
                last.then_inc(multiplied, 1)

        @block.scalar
        def _(act):
            with act.Fori(0, turns) as i:
                act.wait_ge(turned, t + i + 1)
                nc.scalar.activation(k.staging_t[:, :], all_banks[:, 0:n], ACT.Copy).then_inc(turned_sb, 1)
    k.since.passed(turns, staged, turned, turned_sb, multiplied)
    k.since.passed(2 * turns + 1, epilogued)
    if how == "leaky":
        k.since.passed(turns, k.stage["bulk_pe"])


def shifted_softplus(k):
    nc, link, hs = k.nc, k.link, k.hs
    soft = k.acc[:, 0:WIN, 0:D]
    by_act = k.stage["bulk_act"]
    b = k.since(by_act)
    with nc.Block() as block:
        @block.scalar
        def _(act):
            nc.scalar.activation(soft, hs[:, :, :], ACT.Abs).then_inc(by_act, 1)
            act.wait_ge(by_act, b + 1)
            nc.scalar.activation(soft, soft, ACT.Exp, scale=-1.0).then_inc(by_act, 1)
            act.wait_ge(by_act, b + 2)
            nc.scalar.activation(soft, soft, ACT.Ln, bias=1.0).then_inc(by_act, 1)

        @block.vector
        def _(dve):
            dve.wait_ge(by_act, b + 3)
            link(dve, nc.vector.tensor_scalar(hs[:, :, :], hs[:, :, :], 0.0, -LOG2, ALU.max, ALU.add))
            link(dve, nc.vector.tensor_tensor(hs[:, :, :], hs[:, :, :], soft, ALU.add))
    k.since.passed(3, by_act)



def clear(k):
    sems = [*k.stage.values(), *k.rows_in]
    nums = [s.num for s in sems]
    assert nums == list(range(nums[0], nums[0] + len(nums)))
    with k.nc.Block() as block:
        @block.vector
        def _(dve):
            dve.sem_clear(range(nums[0], nums[-1] + 1))
    k.since.cleared(sems)


class Counts:

    def __init__(self, eng):
        self.eng, self.kept = eng, {}

    def turn(self):
        self.kept = {}

    def __call__(self, g, n, times=1):
        if isinstance(g, int):
            return g * times + n
        if (n, times) not in self.kept:
            self.kept[n, times] = self.eng.snap(g * times + n)
        return self.kept[n, times]


class Stages:

    def __init__(self, k, leads):
        self.sems = [k.stage[name] for name in leads]
        self.lead = dict(zip([sem.name for sem in self.sems], leads.values()))
        assert not any(k.since(sem) for sem in self.sems)
        k.since.passed(1, *self.sems)

    def start(self, eng, *sems):
        for sem in sems:
            eng.sem_inc(sem, CREDIT - self.lead[sem.name])

    def wait(self, eng, now, sem, g, a, behind=0):
        eng.wait_ge(sem, now(g, a - behind + 1 + CREDIT - self.lead[sem.name]))


def skewed(eng, *stages, counts=None, turn=U):
    most = max(lead for lead, _ in stages)
    for n in range(-most, 0):
        for lead, stage in stages:
            if n + lead >= 0:
                stage(0, n + lead)
    with eng.Fori(0, NG, turn) as g:
        if counts:
            counts.turn()
        for u in range(turn):
            for lead, stage in stages:
                stage(g, u + lead)


def in_slot(u, lead):
    return len(range(u, NG + lead, U))


def per_slot(since, sems, each, lead):
    for u, sem in enumerate(sems):
        since.passed(each * in_slot(u, lead), sem)


def window(eng, k, o, g):
    return bass.ds(eng.value_load(k.glist[o][0:1, 0, bass.ds(g, 1)], min_val=0, max_val=WIN), 1)


def first_edge(eng, k, o, g):
    return eng.value_load(k.glist[o][0:1, 1, bass.ds(g, 1)], min_val=0, max_val=EDGES + (EP if o == 0 else 0))


def segment_sums(k, o):
    nc, st = k.nc, k.stage
    rel_ready, onehot_ready, summed, added, kept = (st[x] for x in ("rel_ready", "onehot_ready", "summed", "added", "kept"))
    width, key = (RW, C_DST) if o == 0 else (MW, M_SRC)
    records = k.erec if o == 0 else k.mrec
    s_rel, s_hot, s_sum, s_add, s_kept = (k.since(x) for x in (rel_ready, onehot_ready, summed, added, kept))
    s_row, s_pool = [k.since(x) for x in k.rows_in], [k.since(x) for x in k.pool_done]
    LOAD, HOT, SUM, ADD = 1, 1, 0, 0
    with ExitStack() as own:
        rows = k.sb(own, f"sum_rows{o}", [P, U, KG, width])
        rel = k.sb(own, f"sum_rel{o}", [P, U, KG])
        hot = k.sb(own, f"sum_hot{o}", [P, U, KG, P], BF16 if o == 0 else F32)
        far = k.sb(own, "sum_far", [P, U, KG, 3 * D], BF16) if o == 0 else None
        cur = k.sb(own, f"sum_cur{o}", [P, U, D])
        with nc.Block() as block:
            @block.sync
            def _(sp):
                now = Counts(sp)

                def load(g, a):
                    sp.wait_ge(summed, now(g, s_sum + a + 1))
                    e0 = first_edge(sp, k, o, g + a)
                    sp.dma_start(rows[:, a % U, :, :].rearrange("p q c -> p (q c)"),
                                 records[bass.ds(e0, GE), :].rearrange("(p q) c -> p (q c)", q=KG))\
                        .then_inc(k.rows_in[a % U], 16)
                skewed(sp, (LOAD, load), counts=now, turn=2 * U)

            if o == 0:
                @block.gpsimd
                def _(pool):
                    now = Counts(pool)

                    def gather(g, a):
                        u = a % U
                        pool.wait_ge(k.rows_in[u], now(g, s_row[u] + 16 * (a // U + 1), 16 // U))
                        pool.wait_ge(summed, now(g, s_sum + a + 1))
                        pool.sem_inc(k.begun, 1)
                        for q in range(KG):
                            pool.indirect_dma_start(
                                far[:, u, q, :], None, k.table3[:, :],
                                bass.IndirectOffsetOnAxis(ap=rows[:, u, q, C_SRC:C_SRC + 1].bitcast(I32), axis=0))\
                                .then_inc(k.pool_done[u], 16)
                    skewed(pool, (SUM, gather), counts=now, turn=2 * U)

            @block.vector
            def _(dve):
                nc.vector.memset(cur[:, :, :], 0.0)
                nc.vector.memset(k.acc[:, :, :], 0.0).then_inc(added, 2)

                now = Counts(dve)

                def one_hot(g, a):
                    u = a % U
                    dve.wait_ge(k.rows_in[u], now(g, s_row[u] + 16 * (a // U + 1), 16 // U))
                    dve.wait_ge(summed, now(g, s_sum + a + 1))
                    nc.vector.tensor_scalar(rel[:, u, :], rows[:, u, :, key].bitcast(I32), k.gbase[o][:, bass.ds(g + a, 1)],
                                            None, ALU.subtract).then_inc(rel_ready, 1)
                    dve.wait_ge(rel_ready, now(g, s_rel + a + 1))
                    for q in range(KG):
                        last = nc.vector.tensor_scalar(hot[:, u, q, :], k.iota_b[:, :], rel[:, u, q:q + 1], None, ALU.is_equal)
                    last.then_inc(onehot_ready, 1)

                def add(g, a):
                    u = a % U
                    dve.wait_ge(summed, now(g, s_sum + U + a + 1))
                    dve.wait_ge(added, now(g, s_add + 2 + a))
                    dve.wait_ge(kept, now(g, s_kept + a + 1))
                    nc.vector.scalar_tensor_tensor(cur[:, u, :], cur[:, (u - 1) % U, :], k.gsame[o][:, bass.ds(g + a, 1)],
                                                   k.psum[a % 2][:, 0:D], ALU.mult, ALU.add).then_inc(added, 1)
                skewed(dve, (HOT, one_hot), (ADD, add), counts=now, turn=2 * U)

            @block.scalar
            def _(act):
                now = Counts(act)
                act.sem_inc(kept, U)

                def keep(g, a):
                    act.wait_ge(added, now(g, s_add + 2 + a + 1))
                    act.sem_inc(k.loading, 1)
                    act.wait_ge(kept, now(g, s_kept + U + a))
                    act.sem_inc(k.loading, 1)
                    w = window(act, k, o, g + a)
                    nc.scalar.activation(k.acc[:, w, 0:D], cur[:, a % U, :].unsqueeze(1), ACT.Copy).then_inc(kept, 1)
                skewed(act, (ADD, keep), counts=now, turn=2 * U)

            @block.tensor
            def _(pe):
                pe.sem_inc(summed, U)

                now = Counts(pe)

                def total(g, a):
                    u = a % U
                    pe.wait_ge(onehot_ready, now(g, s_hot + a + 1))
                    pe.wait_ge(added, now(g, s_add + a + 1))
                    if o == 0:
                        pe.wait_ge(k.pool_done[u], now(g, s_pool[u] + 16 * KG * (a // U + 1), 16 * KG // U))
                    for q in range(KG):
                        for part in range(3 if o == 0 else 1):
                            rhs = far[:, u, q, part * D:(part + 1) * D] if o == 0 else rows[:, u, q, 0:D]
                            last = nc.tensor.matmul(k.psum[a % 2][:, 0:D], hot[:, u, q, :], rhs,
                                                    start=q == 0 and part == 0, stop=q == KG - 1 and part == (2 if o == 0 else 0))
                    last.then_inc(summed, 1)
                skewed(pe, (SUM, total), counts=now, turn=2 * U)
    k.since.passed(NG + HOT, rel_ready, onehot_ready)
    k.since.passed(NG + U, summed, kept)
    k.since.passed(NG + 2, added)
    per_slot(k.since, k.rows_in, 16, LOAD)
    if o == 0:
        per_slot(k.since, k.pool_done, 16 * KG, 0)


def filter_messages(k):
    nc, st = k.nc, k.stage
    ATTR, HIDDEN, POSITIVE, HOT, TURN, SOFT, FILTER, MESSAGE = 6, 5, 4, 4, 3, 2, 1, 0
    LOAD, SLOTS = 7, 2 * U
    stages = Stages(k, dict(
        attr_turned=ATTR, attrT_ready=ATTR, hidden_ready=HIDDEN, size_ready=HIDDEN, exps_ready=HIDDEN, logs_ready=HIDDEN,
        positive_ready=POSITIVE, rel_ready=HOT, onehot_ready=HOT, onehot_turned=TURN, onehotT_ready=TURN, soft_ready=SOFT,
        far_ready=FILTER, filter_ready=FILTER, off_ready=MESSAGE, index_ready=MESSAGE, biased=MESSAGE, message_ready=MESSAGE))
    (attr_turned, attrT_ready, hidden_ready, size_ready, exps_ready, logs_ready, positive_ready, rel_ready, onehot_ready,
     onehot_turned, onehotT_ready, soft_ready, far_ready, filter_ready, off_ready, index_ready, biased, message_ready) = \
        stages.sems
    wait, start = stages.wait, stages.start
    s_pool = k.since(k.pool_done[0])
    assert all(k.since(x) == s_pool for x in k.pool_done)
    w_f2, b_f2 = k.weights["W_f2"][0], k.wide["b_f2"][0]
    pads = EP - EDGES
    with ExitStack() as own:
        sb = lambda name, shape, dt=F32: k.sb(own, name, shape, dt)
        rows, pos = sb("f_rows", [P, SLOTS, KG, RW]), sb("f_pos", [P, SLOTS, KG], I32)
        rows_in = [k.sem(f"f_rows_in{u}", own) for u in range(SLOTS)]
        rel, hot = sb("f_rel", [P, SLOTS, KG]), sb("f_hot", [P, U, KG, P], BF16)
        hot_t, attr_t = sb("f_hot_t", [P, U, GE], BF16), sb("f_attr_t", [RBF, 2, GE])
        size, logs, positive, soft = (sb(n, [P, s, GE]) for n, s in (("f_size", U), ("f_logs", U), ("f_pos_part", U), ("f_soft", 2)))
        tmp, index, off = sb("f_tmp", [P, KG, D]), sb("f_index", [P, U, KG], I32), sb("f_off", [P, KG])
        msg = sb("f_msg", [P, U, KG, MW])
        pad = sb("f_pad", [pads // 8, 1, MW])
        pad_i = pad[:, :, :].bitcast(I32)
        hot_ps = k.psum[0].bitcast(BF16)[:, 0:GE]
        attr_ps = k.psum[1][0:RBF, :]
        hidden_ps, far_ps, filter_ps = k.psum[2:4], k.psum[4:6], k.psum[6:8]
        padded = k.sem("padded")

        def loaded(now, g, a):
            return now(g, 32 * (a // SLOTS + 1), 32 // SLOTS)

        with nc.Block() as block:
            @block.sync
            def _(sp):
                now = Counts(sp)
                sp.wait_ge(padded, 2)
                sp.dma_start(k.mrec[EDGES:EP, :].rearrange("(p j) c -> p j c", j=8),
                             pad[:, :, :].to_broadcast([pads // 8, 8, MW])).then_inc(padded, 16)

                def load(g, a):
                    u = a % SLOTS
                    wait(sp, now, message_ready, g, a, SLOTS)
                    e0 = first_edge(sp, k, 0, g + a)
                    sp.dma_start(rows[:, u, :, :].rearrange("p q c -> p (q c)"),
                                 k.erec[bass.ds(e0, GE), :].rearrange("(p q) c -> p (q c)", q=KG)).then_inc(rows_in[u], 16)
                    sp.dma_start(pos[:, u, :], k.epos[bass.ds(e0, GE), :].rearrange("(p q) c -> p (q c)", q=KG))\
                        .then_inc(rows_in[u], 16)
                skewed(sp, (LOAD, load), counts=now, turn=SLOTS)
                sp.wait_ge(padded, 18)
                for u in range(SLOTS):
                    sp.wait_ge(rows_in[u], 32 * len(range(u, NG + LOAD, SLOTS)))

            @block.gpsimd
            def _(pool):
                now = Counts(pool)

                def scatter(g, a):
                    u = a % U
                    wait(pool, now, message_ready, g, a)
                    pool.sem_inc(k.begun, 1)
                    for q in range(KG):
                        pool.indirect_dma_start(
                            k.mrec[:, :], bass.IndirectOffsetOnAxis(ap=index[:, u, q:q + 1], axis=0), msg[:, u, q, :], None,
                            bounds_check=EDGES - 1, oob_is_err=False).then_inc(k.pool_done[u], 16)
                skewed(pool, (MESSAGE, scatter), counts=now, turn=SLOTS)
                for u in range(U):
                    pool.wait_ge(k.pool_done[u], s_pool + 16 * KG * NG // U)

            @block.vector
            def _(dve):
                now = Counts(dve)
                nc.vector.memset(pad[:, :, :], 0.0).then_inc(padded, 1)
                dve.wait_ge(padded, 1)
                nc.vector.memset(pad_i[:, :, M_SRC:M_SRC + 1], NOWHERE).then_inc(padded, 1)
                k.link(dve, nc.vector.memset(msg[:, :, :, :], 0.0))
                start(dve, positive_ready, rel_ready, onehot_ready, soft_ready, off_ready, index_ready, biased, message_ready)

                def one_hot(g, a):
                    u, s = a % U, a % SLOTS
                    dve.wait_ge(rows_in[s], loaded(now, g, a))
                    nc.vector.tensor_scalar(rel[:, s, :], rows[:, s, :, C_DST].bitcast(I32),
                                            k.gbase[0][:, bass.ds(g + a, 1)], None, ALU.subtract).then_inc(rel_ready, 1)
                    wait(dve, now, rel_ready, g, a)
                    wait(dve, now, onehot_turned, g, a, U)
                    for q in range(KG):
                        last = nc.vector.tensor_scalar(hot[:, u, q, :], k.iota_b[:, :], rel[:, s, q:q + 1], None, ALU.is_equal)
                    last.then_inc(onehot_ready, 1)

                def positives(g, a):
                    b, u = a % 2, a % U
                    wait(dve, now, size_ready, g, a)
                    wait(dve, now, soft_ready, g, a, U)
                    nc.vector.tensor_scalar(positive[:, u, :], hidden_ps[b], k.bf1[:, :], 0.0, ALU.add, ALU.max)\
                        .then_inc(positive_ready, 1)

                def softplus(g, a):
                    b, u = a % 2, a % U
                    wait(dve, now, positive_ready, g, a)
                    wait(dve, now, logs_ready, g, a)
                    wait(dve, now, filter_ready, g, a, 2)
                    nc.vector.scalar_tensor_tensor(soft[:, b, :], positive[:, u, :], -LOG2, logs[:, u, :], ALU.add, ALU.add)\
                        .then_inc(soft_ready, 1)

                def message(g, a):
                    u, b, s = a % U, a % 2, a % SLOTS
                    wait(dve, now, index_ready, g, a, 1)
                    nc.vector.tensor_scalar(off[:, :], rel[:, s, :], float(P), FAR, ALU.is_ge, ALU.mult).then_inc(off_ready, 1)
                    wait(dve, now, off_ready, g, a)
                    dve.wait_ge(k.pool_done[u], now(g, s_pool + 16 * KG * (a // U), 16 * KG // U))
                    nc.vector.tensor_tensor(index[:, u, :], off[:, :], pos[:, s, :], ALU.add).then_inc(index_ready, 1)
                    nc.vector.tensor_copy(msg[:, u, :, M_SRC:M_SRC + 3].bitcast(I32), rows[:, s, :, C_SRC:C_SRC + 3].bitcast(I32))
                    wait(dve, now, filter_ready, g, a)
                    wait(dve, now, message_ready, g, a, 1)
                    nc.vector.tensor_tensor(tmp[:, :, :], filter_ps[b].rearrange("p (q d) -> p q d", d=D),
                                            b_f2[:, :].unsqueeze(1).to_broadcast([P, KG, D]), ALU.add).then_inc(biased, 1)
                    wait(dve, now, biased, g, a)
                    wait(dve, now, far_ready, g, a)
                    for q in range(KG):
                        last = nc.vector.scalar_tensor_tensor(msg[:, u, q, 0:D], tmp[:, q, :], rows[:, s, q, C_WT:C_WT + 1],
                                                              far_ps[b][:, q * D:(q + 1) * D], ALU.mult, ALU.mult)
                    last.then_inc(message_ready, 1)
                skewed(dve, (SOFT, softplus), (HOT, one_hot), (POSITIVE, positives), (MESSAGE, message), counts=now, turn=SLOTS)

            @block.scalar
            def _(act):
                now = Counts(act)
                start(act, attrT_ready, size_ready, exps_ready, logs_ready, onehotT_ready)

                def turn_attr(g, a):
                    wait(act, now, attr_turned, g, a)
                    nc.scalar.activation(attr_t[:, a % 2, :], attr_ps, ACT.Copy).then_inc(attrT_ready, 1)

                def turn(g, a):
                    wait(act, now, onehot_turned, g, a)
                    nc.scalar.activation(hot_t[:, a % U, :], hot_ps, ACT.Copy).then_inc(onehotT_ready, 1)

                def sizes(g, a):
                    u = a % U
                    if a % 2 == 0 and a >= 2:
                        pair = slice((a - 2) % U, (a - 2) % U + 2)
                        wait(act, now, exps_ready, g, a, 1)
                        wait(act, now, soft_ready, g, a, 1 + U)
                        nc.scalar.activation(logs[:, pair, :], size[:, pair, :], ACT.Ln, bias=1.0).then_inc(logs_ready, 2)
                    wait(act, now, hidden_ready, g, a)
                    wait(act, now, logs_ready, g, a - a % 2, U - 1)
                    nc.scalar.activation(size[:, u, :], hidden_ps[a % 2], ACT.Abs, bias=k.bf1[:, :]).then_inc(size_ready, 1)
                    if a % 2:
                        pair = slice(u - 1, u + 1)
                        wait(act, now, size_ready, g, a)
                        nc.scalar.activation(size[:, pair, :], size[:, pair, :], ACT.Exp, scale=-1.0).then_inc(exps_ready, 2)
                skewed(act, (ATTR, turn_attr), (TURN, turn), (HIDDEN, sizes), counts=now, turn=SLOTS)

            @block.tensor
            def _(pe):
                now = Counts(pe)
                start(pe, attr_turned, hidden_ready, onehot_turned, far_ready, filter_ready)

                def turn(g, a):
                    wait(pe, now, onehot_ready, g, a)
                    wait(pe, now, onehotT_ready, g, a, 1)
                    for q in range(KG):
                        last = nc.tensor.transpose(hot_ps[:, q * P:(q + 1) * P], hot[:, a % U, q, :], k.ident_b[:, :])
                    last.then_inc(onehot_turned, 1)

                def turn_attr(g, a):
                    pe.wait_ge(rows_in[a % SLOTS], loaded(now, g, a))
                    wait(pe, now, attrT_ready, g, a, 1)
                    for q in range(KG):
                        last = nc.tensor.transpose(attr_ps[:, q * P:(q + 1) * P], rows[:, a % SLOTS, q, 0:RBF], k.ident[:, :])
                    last.then_inc(attr_turned, 1)

                def filters(g, a):
                    b = a % 2
                    wait(pe, now, message_ready, g, a, 2)
                    near_rows(pe, k, 0, g + a, far_ps[b], hot_t[:, a % U, :], onehotT_ready, now(g, a + 1 + CREDIT - TURN))\
                        .then_inc(far_ready, 1)
                    wait(pe, now, soft_ready, g, a)
                    for q in range(KG):
                        last = nc.tensor.matmul(filter_ps[b][:, q * D:(q + 1) * D], soft[:, b, q * P:(q + 1) * P], w_f2[:, :],
                                                start=True, stop=True)
                    last.then_inc(filter_ready, 1)

                def hidden(g, a):
                    b = a % 2
                    wait(pe, now, attrT_ready, g, a)
                    wait(pe, now, positive_ready, g, a, 2)
                    nc.tensor.matmul(hidden_ps[b], k.w_f1[:, :], attr_t[:, b, :], start=True, stop=True).then_inc(hidden_ready, 1)
                skewed(pe, (HIDDEN, hidden), (ATTR, turn_attr), (TURN, turn), (FILTER, filters), counts=now, turn=SLOTS)
    per_slot(k.since, k.pool_done, 16 * KG, MESSAGE)


def near_rows(pe, k, o, g, ps, hot_t, ready, value, stop=True):
    nc = k.nc
    w = window(pe, k, o, g)
    pe.wait_ge(ready, value)
    for q in range(KG):
        for part in range(3):
            last = nc.tensor.matmul(ps[:, q * D:(q + 1) * D], hot_t[:, q * P:(q + 1) * P], k.near[:, w, part * D:(part + 1) * D]
                                    .rearrange("p a d -> p (a d)"), start=part == 0, stop=stop and part == 2)
    return last


def attention(k, layer):
    nc, st, o = k.nc, k.stage, layer
    HOT, TURN, SCORE, MAX, SUM, ADD = 5, 4, 3, 2, 1, 0
    NEAR = TURN if o == 0 else SCORE
    stages = Stages(k, dict(rel_ready=HOT, kinds_ready=HOT, onehot_ready=HOT, onehot_turned=TURN, onehotT_ready=TURN,
                            edge_term=NEAR, near_ready=NEAR, in1=SCORE, in2=SCORE, in3=SCORE, edge_dot=SCORE, scores=SCORE,
                            spread=MAX, group_max=MAX, exp_in=MAX, weighed=MAX, shrink=MAX, prob_turned=MAX, prob_ready=SUM,
                            summed=SUM, added=ADD))
    (rel_ready, kinds_ready, onehot_ready, onehot_turned, onehotT_ready, edge_term, near_ready, in1, in2, in3, edge_dot,
     scores, spread, group_max, exp_in, weighed, shrink, prob_turned, prob_ready, summed, added) = stages.sems
    wait, start = stages.wait, stages.start
    kept = st["kept"]

    s_pool = k.since(k.pool_done[0])
    assert all(k.since(x) == s_pool for x in k.pool_done) and not any(k.since(x) for x in k.rows_in)
    width, key, other = (RW, C_DST, C_SRC) if o == 0 else (MW, M_SRC, M_DST)
    records = k.erec if o == 0 else k.mrec
    HW = P if o == 0 else P + NTYPE
    We, att = k.wide["We"][0], k.wide["att"][0]
    XW = D + 4
    with ExitStack() as own:
        sb = lambda name, shape, dt=F32: k.sb(own, f"{name}{o}", shape, dt)
        rows, rel, hide = sb("a_rows", [P, U, KG, width]), sb("a_rel", [P, U, KG]), sb("a_hide", [P, U, KG])
        kind = sb("a_kind", [P, U, KG])
        hot, hot_t = sb("a_hot", [P, U, KG, HW], BF16), sb("a_hot_t", [P, U, GE], BF16)
        kind_t = sb("a_kind_t", [NTYPE, 2, GE], BF16) if o else None
        far = sb("a_far", [P, U, KG, XW])
        term = sb("a_term", [P, 2, KG, D])
        work = sb("a_work", [P, KG, D])
        raw, score = sb("a_raw", [P, KG]), sb("a_score", [P, U, KG])
        gmax = sb("a_gmax", [P, 1])
        before, bounded, factor = sb("a_before", [P, U]), sb("a_bounded", [P, U]), sb("a_factor", [P, U])
        cur = sb("a_cur", [P, U, XW])
        prob_t, prob = sb("a_prob_t", [P, 2, GE]), sb("a_prob", [P, 2, GE])
        hot_ps = k.psum[0].bitcast(BF16)
        near_ps, spread_ps, prob_ps, sum_ps = k.psum[1:3], k.psum[3:5], k.psum[5], k.psum[6:8]

        with nc.Block() as block:
            @block.sync
            def _(sp):
                now = Counts(sp)
                sp.sem_inc(kept, 16 * U)

                def load(g, a):
                    wait(sp, now, scores, g, a, U)
                    e0 = first_edge(sp, k, o, g + a)
                    sp.dma_start(rows[:, a % U, :, :].rearrange("p q c -> p (q c)"),
                                 records[bass.ds(e0, GE), :].rearrange("(p q) c -> p (q c)", q=KG)).then_inc(k.rows_in[a % U], 16)

                def keep(g, a):
                    wait(sp, now, added, g, a)
                    sp.sem_inc(k.loading, 1)
                    sp.wait_ge(kept, now(g, 16 * (U + a), 16))
                    sp.sem_inc(k.loading, 1)
                    w = window(sp, k, o, g + a)
                    sp.dma_start(k.acc[:, w, 0:D + 2], cur[:, a % U, 0:D + 2].unsqueeze(1)).then_inc(kept, 16)
                skewed(sp, (LOADS, load), (ADD, keep), counts=now, turn=2 * U)
                for u in range(U):
                    sp.wait_ge(k.rows_in[u], in_slot(u, LOADS) * 16)
                sp.wait_ge(kept, 16 * (U + NG))

            @block.gpsimd
            def _(pool):
                now = Counts(pool)

                def gather(g, a):
                    u = a % U
                    pool.wait_ge(k.rows_in[u], now(g, 16 * (a // U + 1), 16 // U))
                    wait(pool, now, summed, g, a, U)
                    pool.sem_inc(k.begun, 1)
                    for q in range(KG):
                        pool.indirect_dma_start(
                            far[:, u, q, 0:D], None, k.table[:, :],
                            bass.IndirectOffsetOnAxis(ap=rows[:, u, q, other:other + 1].bitcast(I32), axis=0))\
                            .then_inc(k.pool_done[u], 16)
                skewed(pool, (TURN, gather), counts=now, turn=2 * U)

            @block.vector
            def _(dve):
                now = Counts(dve)
                k.link(dve, nc.vector.memset(k.acc[:, :, :], 0.0))
                k.link(dve, nc.vector.memset(k.acc[:, :, D + 1:D + 2], -LOW))
                k.link(dve, nc.vector.memset(cur[:, :, :], 0.0))
                k.link(dve, nc.vector.memset(cur[:, :, D + 1:D + 2], -LOW))
                k.link(dve, nc.vector.memset(far[:, :, :, :], 1.0))
                start(dve, rel_ready, onehot_ready, scores, group_max, exp_in, added, edge_dot,
                      *((kinds_ready,) if o else (in1, in2, in3)))

                def one_hot(g, a):
                    u, n = a % U, g + a
                    dve.wait_ge(k.rows_in[u], now(g, 16 * (a // U + 1), 16 // U))
                    nc.vector.tensor_scalar(rel[:, u, :], rows[:, u, :, key].bitcast(I32), k.gbase[o][:, bass.ds(n, 1)],
                                            None, ALU.subtract).then_inc(rel_ready, 1)
                    if o:
                        nc.vector.tensor_copy(kind[:, u, :], rows[:, u, :, M_TYPE].bitcast(I32)).then_inc(kinds_ready, 1)
                    wait(dve, now, kinds_ready if o else rel_ready, g, a)
                    wait(dve, now, onehot_turned, g, a, U)
                    for q in range(KG):
                        last = nc.vector.tensor_scalar(hot[:, u, q, 0:P], k.iota_b[:, :], rel[:, u, q:q + 1], None, ALU.is_equal)
                        if o:
                            last = nc.vector.tensor_scalar(hot[:, u, q, P:HW], k.iota_b[:, 0:NTYPE], kind[:, u, q:q + 1], None,
                                                           ALU.is_equal)
                    nc.vector.tensor_scalar(hide[:, u, :], rel[:, u, :], float(P), -BIG, ALU.is_ge, ALU.mult).then_inc(onehot_ready, 1)

                def meet(g, a):
                    u, b = a % U, a % 2
                    dve.wait_ge(k.pool_done[u], now(g, s_pool + 16 * KG * (a // U + 1), 16 * KG // U))
                    wait(dve, now, near_ready, g, a)
                    nc.vector.tensor_tensor(work[:, :, :], near_ps[b].rearrange("p (q d) -> p q d", d=D), far[:, u, :, 0:D],
                                            ALU.add).then_inc(in1, 1)
                    wait(dve, now, in1, g, a)
                    wait(dve, now, edge_term, g, a)
                    nc.vector.tensor_tensor(term[:, b, :, :], work[:, :, :], term[:, b, :, :], ALU.add).then_inc(in2, 1)

                def score_edges(g, a):
                    u, b = a % U, a % 2
                    if o == 0:
                        wait(dve, now, in2, g, a)
                        nc.vector.scalar_tensor_tensor(term[:, b, :, :], term[:, b, :, :], 0.2, term[:, b, :, :], ALU.mult, ALU.max)\
                            .then_inc(in3, 1)
                        wait(dve, now, in3, g, a)
                    else:
                        dve.wait_ge(k.pool_done[u], now(g, s_pool + 16 * KG * (a // U + 1), 16 * KG // U))
                        wait(dve, now, edge_term, g, a)
                    for q in range(KG):
                        last = nc.vector.scalar_tensor_tensor(
                            work[:, q, :], term[:, b, q, :], 1.0, far[:, u, q, 0:D] if o else att[:, :], ALU.mult, ALU.mult,
                            accum_out=raw[:, q:q + 1])
                    last.then_inc(edge_dot, 1)
                    wait(dve, now, edge_dot, g, a)
                    nc.vector.tensor_tensor(score[:, u, :], raw[:, :], hide[:, u, :], ALU.add).then_inc(scores, 1)

                def node_max(g, a):
                    u, b, f = a % U, a % 2, bass.ds(g + a, 1)
                    past = cur[:, (u - 1) % U, D + 1:D + 2]
                    wait(dve, now, exp_in, g, a, 1)
                    dve.wait_ge(kept, now(g, 16 * (U + a - U + 1), 16))
                    nc.vector.tensor_scalar(before[:, u:u + 1], past, k.gfresh[o][:, f], None, ALU.add)
                    nc.vector.tensor_scalar(bounded[:, u:u + 1], past, k.gfresh[o][:, f], -LOW, ALU.add, ALU.min)
                    wait(dve, now, spread, g, a)
                    nc.vector.tensor_reduce(gmax[:, :], spread_ps[b], AX, ALU.max).then_inc(group_max, 1)
                    wait(dve, now, group_max, g, a)
                    nc.vector.scalar_tensor_tensor(cur[:, u, D + 1:D + 2], gmax[:, :], -1.0, bounded[:, u:u + 1], ALU.mult, ALU.min)\
                        .then_inc(exp_in, 1)

                def add(g, a):
                    u, b = a % U, a % 2
                    wait(dve, now, summed, g, a)
                    wait(dve, now, shrink, g, a)
                    wait(dve, now, added, g, a, 1)
                    nc.vector.scalar_tensor_tensor(cur[:, u, 0:D + 1], cur[:, (u - 1) % U, 0:D + 1], factor[:, u:u + 1],
                                                   sum_ps[b][:, 0:D + 1], ALU.mult, ALU.add).then_inc(added, 1)
                skewed(dve, *(((SCORE, meet), (HOT, one_hot), (MAX, node_max), (ADD, add)) if o == 0 else
                              ((HOT, one_hot), (MAX, node_max), (ADD, add))), (SCORE, score_edges),
                       counts=now, turn=2 * U)

            @block.scalar
            def _(act):
                now = Counts(act)
                start(act, onehotT_ready, edge_term, weighed, shrink, prob_ready)

                def take_prob(g, a):
                    b = a % 2
                    wait(act, now, prob_turned, g, a)
                    wait(act, now, summed, g, a, 2)
                    nc.scalar.activation(prob[:, b, :], prob_ps, ACT.Copy).then_inc(prob_ready, 1)

                def turn(g, a):
                    u, b = a % U, a % 2
                    wait(act, now, onehot_turned, g, a)
                    if o:
                        nc.scalar.activation(kind_t[:, b, :], hot_ps[0:NTYPE, GE:2 * GE], ACT.Copy)
                    nc.scalar.activation(hot_t[:, u, :], hot_ps[:, 0:GE], ACT.Copy).then_inc(onehotT_ready, 1)

                def weigh(g, a):
                    u, b = a % U, a % 2
                    wait(act, now, exp_in, g, a)
                    nc.scalar.activation(prob_t[:, b, :], spread_ps[b], ACT.Exp, bias=cur[:, u, D + 1:D + 2]).then_inc(weighed, 1)
                    wait(act, now, added, g, a, U)
                    nc.scalar.activation(factor[:, u:u + 1], before[:, u:u + 1], ACT.Exp, scale=-1.0,
                                         bias=cur[:, u, D + 1:D + 2]).then_inc(shrink, 1)

                def terms(g, a):
                    u, b = a % U, a % 2
                    wait(act, now, scores, g, a, 2)
                    if o == 0:
                        for q in range(KG):
                            last = nc.scalar.activation(term[:, b, q, :], We[:, :], ACT.Copy, scale=rows[:, u, q, C_WT:C_WT + 1])
                        last.then_inc(edge_term, 1)
                    else:
                        wait(act, now, near_ready, g, a)
                        nc.scalar.activation(term[:, b, :, :], near_ps[b].rearrange("p (q d) -> p q d", d=D), ACT.Tanh)\
                            .then_inc(edge_term, 1)
                skewed(act, (SUM, take_prob), *(((TURN, turn), (MAX, weigh), (NEAR, terms)) if o == 0 else
                                               ((NEAR, terms), (MAX, weigh), (TURN, turn))),
                       counts=now, turn=2 * U)

            @block.tensor
            def _(pe):
                now = Counts(pe)
                start(pe, onehot_turned, near_ready, spread, prob_turned, summed)

                def spreads(g, a):
                    u, b = a % U, a % 2
                    wait(pe, now, scores, g, a)
                    nc.tensor.matmul(spread_ps[b], k.apart_b[:, :], hot_t[:, u, :], start=True, stop=False, skip_group_check=True)
                    for q in range(KG):
                        last = nc.tensor.matmul(spread_ps[b][:, q * P:(q + 1) * P], score[:, u, q:q + 1].to_broadcast([P, P]),
                                                k.ident[:, :], start=False, stop=q == KG - 1, skip_group_check=True)
                    last.then_inc(spread, 1)

                def turn(g, a):
                    u = a % U
                    wait(pe, now, onehot_ready, g, a)
                    wait(pe, now, onehotT_ready, g, a, 1)
                    for q in range(KG):
                        last = nc.tensor.transpose(hot_ps[:, q * P:(q + 1) * P], hot[:, u, q, 0:P], k.ident_b[:, :])
                        if o:
                            last = nc.tensor.transpose(hot_ps[0:NTYPE, GE + q * P:GE + (q + 1) * P], hot[:, u, q, P:HW],
                                                       k.ident_b[:, :])
                    last.then_inc(onehot_turned, 1)

                def sums(g, a):
                    u, b = a % U, a % 2
                    wait(pe, now, prob_ready, g, a)
                    wait(pe, now, added, g, a, 2)
                    for q in range(KG):
                        last = nc.tensor.matmul(sum_ps[b][:, 0:D + 1], prob[:, b, q * P:(q + 1) * P], far[:, u, q, 0:D + 1],
                                                start=q == 0, stop=q == KG - 1)
                    last.then_inc(summed, 1)

                def rows_near(g, a):
                    u, b, n = a % U, a % 2, g + a
                    wait(pe, now, scores, g, a, 2)
                    if o == 0:
                        near_rows(pe, k, o, n, near_ps[b], hot_t[:, u, :], onehotT_ready, now(g, a + 1 + CREDIT - TURN))\
                            .then_inc(near_ready, 1)
                        return
                    w = window(pe, k, o, n)
                    wait(pe, now, onehotT_ready, g, a)
                    for q in range(KG):
                        cols = slice(q * P, (q + 1) * P)
                        for part in range(3):
                            nc.tensor.matmul(near_ps[b][:, cols], hot_t[:, u, cols], k.near[:, w, part * D:(part + 1) * D]
                                             .rearrange("p a d -> p (a d)"), start=part == 0, stop=False)
                        for part in range(3):
                            last = nc.tensor.matmul(near_ps[b][:, cols], kind_t[:, b, cols], k.rel3[:, part * D:(part + 1) * D],
                                                    start=False, stop=part == 2)
                    last.then_inc(near_ready, 1)

                def turn_prob(g, a):
                    b = a % 2
                    wait(pe, now, weighed, g, a)
                    for q in range(KG):
                        last = nc.tensor.transpose(prob_ps[:, q * P:(q + 1) * P], prob_t[:, b, q * P:(q + 1) * P], k.ident[:, :])
                    last.then_inc(prob_turned, 1)
                skewed(pe, (MAX, spreads), *(((SUM, sums), (TURN, turn), (NEAR, rows_near)) if o == 0 else
                                             ((NEAR, rows_near), (SUM, sums), (TURN, turn))),
                       (MAX, turn_prob), counts=now, turn=2 * U)
    per_slot(k.since, k.rows_in, 16, LOADS)
    per_slot(k.since, k.pool_done, 16 * KG, TURN)


def gat_output(k):
    nc, link, hs, acc, stat = k.nc, k.link, k.hs, k.acc, k.stat
    by_act, by_pe = k.stage["bulk_act"], k.stage["bulk_pe"]
    b, p = k.since(by_act), k.since(by_pe)
    full = [P, WIN, D]
    spread = lambda t: t.unsqueeze(1).to_broadcast(full)
    with ExitStack() as own:
        part, mean = k.sb(own, "bn_part", [P, D]), k.sb(own, "bn_mean", [P, D])
        scale = k.sb(own, "bn_scale", [P, D])
        with nc.Block() as block:
            @block.vector
            def _(dve):
                link(dve, nc.vector.tensor_scalar(stat[0][:, :], acc[:, 0:WIN, D], 1e-16, None, ALU.add))
                link(dve, nc.vector.reciprocal(stat[0][:, :], stat[0][:, :]))
                link(dve, nc.vector.tensor_tensor(acc[:, 0:WIN, 0:D], acc[:, 0:WIN, 0:D],
                                                  stat[0][:, :].unsqueeze(2).to_broadcast(full), ALU.mult))
                link(dve, nc.vector.tensor_tensor(hs[:, :, :], hs[:, :, :], acc[:, 0:WIN, 0:D], ALU.add))
                nc.vector.tensor_tensor(hs[:, :, :], hs[:, :, :], spread(k.wide["bias_out"][0][:, :]), ALU.add).then_inc(by_act, 1)
                dve.wait_ge(by_act, b + 2)
                for i, t in enumerate((hs[:, :, :], acc[:, 0:WIN, 0:D])):
                    if i:
                        link(dve, nc.vector.tensor_tensor(t, hs[:, :, :], hs[:, :, :], ALU.mult))
                    link(dve, nc.vector.tensor_scalar(t[:, WIN - 1, :], t[:, WIN - 1, :], k.valid[:, :], None, ALU.mult))
                    nc.vector.tensor_reduce(part[:, :], t.rearrange("p w d -> p d w"), AX, ALU.add).then_inc(by_pe, 1)
                    dve.wait_ge(by_pe, p + 2 * i + 2)
                    if i == 0:
                        link(dve, nc.vector.tensor_scalar(mean[:, :], k.psum[0][:, 0:D], 1.0 / NODES, None, ALU.mult))
                        link(dve, nc.vector.tensor_tensor(hs[:, :, :], hs[:, :, :], spread(mean[:, :]), ALU.subtract))
                    else:
                        nc.vector.tensor_scalar(scale[:, :], k.psum[0][:, 0:D], 1.0 / NODES, 1e-5, ALU.mult, ALU.add).then_inc(by_act, 1)
                dve.wait_ge(by_act, b + 4)
                link(dve, nc.vector.reciprocal(scale[:, :], scale[:, :]))
                link(dve, nc.vector.tensor_tensor(scale[:, :], scale[:, :], k.wide["bn_g"][0][:, :], ALU.mult))
                link(dve, nc.vector.tensor_tensor(hs[:, :, :], hs[:, :, :], spread(scale[:, :]), ALU.mult))
                link(dve, nc.vector.tensor_tensor(hs[:, :, :], hs[:, :, :], spread(k.wide["bn_b"][0][:, :]), ALU.add))
                link(dve, nc.vector.tensor_tensor(k.xs[:, :, :], k.xs[:, :, :], hs[:, :, :], ALU.add))

            @block.scalar
            def _(act):
                act.wait_ge(by_act, b + 1)
                nc.scalar.activation(hs[:, :, :], hs[:, :, :], ACT.Gelu).then_inc(by_act, 1)
                act.wait_ge(by_act, b + 3)
                nc.scalar.activation(scale[:, :], scale[:, :], ACT.Sqrt).then_inc(by_act, 1)

            @block.tensor
            def _(pe):
                for i in range(2):
                    pe.wait_ge(by_pe, p + 2 * i + 1)
                    nc.tensor.matmul(k.psum[0][:, 0:D], k.ones[:, :], part[:, :], start=True, stop=True).then_inc(by_pe, 1)
    k.since.passed(4, by_act, by_pe)


def relation_output(k):
    nc, link, acc, stat = k.nc, k.link, k.acc, k.stat
    by_act, by_pe = k.stage["bulk_act"], k.stage["bulk_pe"]
    b, p = k.since(by_act), k.since(by_pe)
    full = [P, WIN, D]
    with ExitStack() as own:
        col, row, top = k.sb(own, "top_col", [P, 1]), k.sb(own, "top_row", [1, 1]), k.sb(own, "top_all", [P, 1])
        with nc.Block() as block:
            @block.vector
            def _(dve):
                nc.vector.tensor_reduce(col[:, :], acc[:, 0:WIN, D + 1], AX, ALU.min).then_inc(by_pe, 1)
                dve.wait_ge(by_pe, p + 2)
                nc.vector.tensor_reduce(row[:, :], k.psum[0][0:1, 0:P], AX, ALU.min).then_inc(by_pe, 1)
                dve.wait_ge(by_pe, p + 4)
                link(dve, nc.vector.tensor_copy(top[:, :], k.psum[1][:, 0:1]))
                link(dve, nc.vector.tensor_scalar(stat[0][:, :], acc[:, 0:WIN, D + 1], -1.0, None, ALU.mult))
                nc.vector.tensor_scalar(stat[0][:, :], stat[0][:, :], top[:, :], 0.0, ALU.add, ALU.min).then_inc(by_act, 1)
                dve.wait_ge(by_act, b + 2)
                link(dve, nc.vector.tensor_tensor(stat[1][:, :], acc[:, 0:WIN, D], stat[0][:, :], ALU.mult))
                link(dve, nc.vector.tensor_scalar(stat[1][:, :], stat[1][:, :], 1e-10, None, ALU.add))
                link(dve, nc.vector.reciprocal(stat[1][:, :], stat[1][:, :]))
                link(dve, nc.vector.tensor_tensor(stat[1][:, :], stat[1][:, :], stat[0][:, :], ALU.mult))
                link(dve, nc.vector.tensor_tensor(acc[:, 0:WIN, 0:D], acc[:, 0:WIN, 0:D],
                                                  stat[1][:, :].unsqueeze(2).to_broadcast(full), ALU.mult))
                link(dve, nc.vector.tensor_tensor(k.hs[:, :, :], k.hs[:, :, :], acc[:, 0:WIN, 0:D], ALU.add))

            @block.scalar
            def _(act):
                act.wait_ge(by_act, b + 1)
                nc.scalar.activation(stat[0][:, :], stat[0][:, :], ACT.Exp).then_inc(by_act, 1)

            @block.tensor
            def _(pe):
                pe.wait_ge(by_pe, p + 1)
                nc.tensor.transpose(k.psum[0][0:1, 0:P], col[:, :], k.ident[:, :]).then_inc(by_pe, 1)
                pe.wait_ge(by_pe, p + 3)
                nc.tensor.matmul(k.psum[1][:, 0:1], k.ones[0:1, :], row[:, :], start=True, stop=True).then_inc(by_pe, 1)
    k.since.passed(2, by_act)
    k.since.passed(4, by_pe)


def store_nodes(k):
    nc, out = k.nc, k.stored
    b = k.since(out)
    with nc.Block() as block:
        @block.sync
        def _(sp):
            sp.dma_start(k.out[0:(WIN - 1) * P, :].rearrange("(w p) d -> p w d", p=P), k.xs[:, 0:WIN - 1, :]).then_inc(out, 16)
            sp.dma_start(k.out[(WIN - 1) * P:NODES, :], k.xs[0:LAST, WIN - 1, :]).then_inc(out, 16)
            sp.wait_ge(out, b + 32)
    k.since.passed(32, out)

_INS = ["x", "src", "dst", "edge_attr_20", "edge_type_64", "edge_weight1", "L0_gnn_W1", "L0_gnn_b1", "L0_gnn_W2",
        "L0_gnn_b2", "L1_gnn_W_in", "L1_gnn_W_f1", "L1_gnn_b_f1", "L1_gnn_W_f2", "L1_gnn_b_f2", "L1_gnn_W_o1",
        "L1_gnn_b_o1", "L1_gnn_W_o2", "L1_gnn_b_o2", "L2_gnn_Wl", "L2_gnn_bl", "L2_gnn_Wr", "L2_gnn_br", "L2_gnn_We",
        "L2_gnn_att", "L2_gnn_bias_out", "L2_gnn_bn_gamma", "L2_gnn_bn_beta", "L3_gnn_rel_embed_weight", "L3_gnn_W"]


def kernel(**inputs):
    import numpy as np
    import concourse.bacc as bacc
    from concourse.bass_utils import run_bass_kernel_spmd

    nc = bacc.Bacc("TRN2", target_bir_lowering=False, num_devices=1)
    arrays, args = {}, []
    for name in _INS:
        a = np.asarray(inputs[name])
        a = np.ascontiguousarray(a.T if name == "L3_gnn_W" else a)
        arrays["in_" + name] = a
        args.append(nc.dram_tensor("in_" + name, a.shape, mybir.dt.from_np(a.dtype), kind="ExternalInput").ap())
    args.append(nc.dram_tensor("out_nodes", (NODES, D), F32, kind="ExternalOutput").ap())
    program(nc, *args)
    r = run_bass_kernel_spmd(nc, [arrays], core_ids=[0])
    return r.results[0]["out_nodes"]
```
